# Optimizing a Trainium2 kernel written in Bass

```python
import numpy as np
import jax
import jax.numpy as jnp

def _softmax(x, axis=-1):
    return jax.nn.softmax(x, axis=axis)

def _gelu(x):
    return jax.nn.gelu(x, approximate=True)

def _silu(x):
    return jax.nn.silu(x)

def _sigmoid(x):
    return jax.nn.sigmoid(x)

def _layernorm(x, axis=-1, eps=1e-05):
    m = jnp.mean(x, axis=axis, keepdims=True)
    v = jnp.var(x, axis=axis, keepdims=True)
    return (x - m) / jnp.sqrt(v + eps)

def _scatter_add(tgt, idx, src, axis=0):
    return tgt.at[idx].add(src)

def _segment_sum(src, seg, n):
    return jax.ops.segment_sum(src, seg, n)
kernel_name = 'mk_seq_preln_d1_jaxref_r8_c281ae'

def setup_inputs(seed: int=0):
    np.random.seed(seed)
    _w = jnp.asarray

    def _L0_attn_setup():
        import jax, jax.numpy as jnp
        import numpy as np
        N_EMBD = 128
        N_HEADS = 16
        HEAD_DIM = N_EMBD // N_HEADS
        NUM_BUCKETS = 32
        MAX_DISTANCE = 64

        def _relative_position_bucket(relative_position):
            rp = jnp.maximum(-relative_position, 0)
            max_exact = NUM_BUCKETS // 2
            is_small = rp < max_exact
            rp_f = jnp.maximum(rp, 1).astype(jnp.float32)
            large = max_exact + (jnp.log(rp_f / max_exact) / np.log(MAX_DISTANCE / max_exact) * (NUM_BUCKETS - max_exact)).astype(jnp.int32)
            large = jnp.minimum(large, NUM_BUCKETS - 1)
            return jnp.where(is_small, rp, large)
        key = jax.random.key(seed)
        ks = jax.random.split(key, 10)
        B, S = (2, 256)
        std = 1.0 / np.sqrt(N_EMBD)
        inp = {'hidden_states': jax.random.normal(ks[0], (B, S, N_EMBD), dtype=jnp.float32), 'Wq': jax.random.normal(ks[1], (N_EMBD, N_EMBD), dtype=jnp.float32) * std, 'bq': jnp.zeros((N_EMBD,), jnp.float32), 'Wk': jax.random.normal(ks[2], (N_EMBD, N_EMBD), dtype=jnp.float32) * std, 'bk': jnp.zeros((N_EMBD,), jnp.float32), 'Wv': jax.random.normal(ks[3], (N_EMBD, N_EMBD), dtype=jnp.float32) * std, 'bv': jnp.zeros((N_EMBD,), jnp.float32), 'Wo': jax.random.normal(ks[4], (N_EMBD, N_EMBD), dtype=jnp.float32) * std, 'bo': jnp.zeros((N_EMBD,), jnp.float32), 'rel_bias': jax.random.normal(ks[5], (NUM_BUCKETS, N_HEADS), dtype=jnp.float32) * 0.1}
        return inp
    _L0_attn_in = _L0_attn_setup()

    def _L0_ffn_setup():
        import jax, jax.numpy as jnp
        import numpy as np
        D_MODEL, D_FF, N_EXPERTS, TOP_K = (128, 512, 8, 2)
        B, S = (2, 256)
        key = jax.random.key(seed)
        ks = jax.random.split(key, 7)
        scale = 0.02
        return {'x': jax.random.normal(ks[0], (B, S, D_MODEL), dtype=jnp.float32), 'W1': jax.random.normal(ks[1], (N_EXPERTS, D_MODEL, D_FF), dtype=jnp.float32) * scale, 'b1': jnp.zeros((N_EXPERTS, D_FF), dtype=jnp.float32), 'W2': jax.random.normal(ks[2], (N_EXPERTS, D_FF, D_MODEL), dtype=jnp.float32) * scale, 'b2': jnp.zeros((N_EXPERTS, D_MODEL), dtype=jnp.float32), 'Wg': jax.random.normal(ks[3], (D_MODEL, N_EXPERTS), dtype=jnp.float32) * scale, 'bg': jnp.zeros((N_EXPERTS,), dtype=jnp.float32)}
    _L0_ffn_in = _L0_ffn_setup()
    _d = {'L0_attn_hidden_states': _L0_attn_in['hidden_states'], 'L0_attn_Wq': _L0_attn_in['Wq'], 'L0_attn_bq': _L0_attn_in['bq'], 'L0_attn_Wk': _L0_attn_in['Wk'], 'L0_attn_bk': _L0_attn_in['bk'], 'L0_attn_Wv': _L0_attn_in['Wv'], 'L0_attn_bv': _L0_attn_in['bv'], 'L0_attn_Wo': _L0_attn_in['Wo'], 'L0_attn_bo': _L0_attn_in['bo'], 'L0_attn_rel_bias': _L0_attn_in['rel_bias'], 'L0_ffn_W1': _L0_ffn_in['W1'], 'L0_ffn_b1': _L0_ffn_in['b1'], 'L0_ffn_W2': _L0_ffn_in['W2'], 'L0_ffn_b2': _L0_ffn_in['b2'], 'L0_ffn_Wg': _L0_ffn_in['Wg'], 'L0_ffn_bg': _L0_ffn_in['bg']}
    _x0 = _d['L0_attn_hidden_states']
    _d['L0_attn_hidden_states'] = jax.random.normal(jax.random.fold_in(jax.random.key(seed), 1), (16, 512, 128), dtype=_x0.dtype)
    del _x0
    return _d

def reference(L0_attn_hidden_states, L0_attn_Wq, L0_attn_bq, L0_attn_Wk, L0_attn_bk, L0_attn_Wv, L0_attn_bv, L0_attn_Wo, L0_attn_bo, L0_attn_rel_bias, L0_ffn_W1, L0_ffn_b1, L0_ffn_W2, L0_ffn_b2, L0_ffn_Wg, L0_ffn_bg):

    def _L0_attn_ref(hidden_states, Wq, bq, Wk, bk, Wv, bv, Wo, bo, rel_bias):
        import jax, jax.numpy as jnp
        import numpy as np
        N_EMBD = 128
        N_HEADS = 16
        HEAD_DIM = N_EMBD // N_HEADS
        NUM_BUCKETS = 32
        MAX_DISTANCE = 64

        def _relative_position_bucket(relative_position):
            rp = jnp.maximum(-relative_position, 0)
            max_exact = NUM_BUCKETS // 2
            is_small = rp < max_exact
            rp_f = jnp.maximum(rp, 1).astype(jnp.float32)
            large = max_exact + (jnp.log(rp_f / max_exact) / np.log(MAX_DISTANCE / max_exact) * (NUM_BUCKETS - max_exact)).astype(jnp.int32)
            large = jnp.minimum(large, NUM_BUCKETS - 1)
            return jnp.where(is_small, rp, large)
        B, S, _ = hidden_states.shape

        def shape(x):
            return x.reshape(B, S, N_HEADS, HEAD_DIM).transpose(0, 2, 1, 3)
        scale = 1.0 / np.sqrt(HEAD_DIM)
        q = shape(hidden_states @ Wq + bq)
        k = shape(hidden_states @ Wk + bk)
        v = shape(hidden_states @ Wv + bv)
        scores = jnp.einsum('bhqd,bhkd->bhqk', q * scale, k)
        ctx = jnp.arange(S)[:, None]
        mem = jnp.arange(S)[None, :]
        bucket = _relative_position_bucket(mem - ctx)
        position_bias = rel_bias[bucket].transpose(2, 0, 1)[None]
        scores = scores + position_bias * 8.0
        attn = jax.nn.softmax(scores.astype(jnp.float32), axis=-1).astype(scores.dtype)
        ctx_out = jnp.einsum('bhqk,bhkd->bhqd', attn, v)
        ctx_out = ctx_out.transpose(0, 2, 1, 3).reshape(B, S, N_EMBD)
        return ctx_out @ Wo + bo

    def _L0_ffn_ref(x, W1, b1, W2, b2, Wg, bg):
        import jax, jax.numpy as jnp
        import numpy as np
        D_MODEL, D_FF, N_EXPERTS, TOP_K = (128, 512, 8, 2)
        B, S = (2, 256)
        Bx, Sx, d = x.shape
        E = W1.shape[0]
        logits = jnp.einsum('bsd,de->bse', x, Wg) + bg
        topk_scores, topk_idx = jax.lax.top_k(logits, TOP_K)
        topk_scores = jax.nn.softmax(topk_scores, axis=-1)
        tokens = x.reshape(-1, d)
        idx_flat = topk_idx.reshape(-1, TOP_K)
        sc_flat = topk_scores.reshape(-1, TOP_K)
        comb = (jax.nn.one_hot(idx_flat, E, dtype=x.dtype) * sc_flat[..., None]).sum(axis=1)
        h = jnp.einsum('td,edf->etf', tokens, W1) + b1[:, None, :]
        even = (jnp.arange(E) % 2 == 0)[:, None, None]
        a = jnp.where(even, jax.nn.gelu(h, approximate=False), jax.nn.silu(h))
        y = jnp.einsum('etf,efd->etd', a, W2) + b2[:, None, :]
        out = jnp.einsum('te,etd->td', comb, y)
        return out.reshape(Bx, Sx, d)
    x = L0_attn_hidden_states
    x = x + _L0_attn_ref(_layernorm(x, axis=-1), L0_attn_Wq, L0_attn_bq, L0_attn_Wk, L0_attn_bk, L0_attn_Wv, L0_attn_bv, L0_attn_Wo, L0_attn_bo, L0_attn_rel_bias)
    x = x + _L0_ffn_ref(_layernorm(x, axis=-1), L0_ffn_W1, L0_ffn_b1, L0_ffn_W2, L0_ffn_b2, L0_ffn_Wg, L0_ffn_bg)
    return x

_drawn_inputs = setup_inputs


def setup_inputs(seed=0):
    import zlib

    import numpy as np

    out = dict(_drawn_inputs(seed))
    spreads = {'L0_attn_bq': (0.0, 0.571),
     'L0_attn_bk': (0.0, 0.8),
     'L0_attn_bv': (0.0, 0.1),
     'L0_attn_bo': (0.0, 0.1),
     'L0_ffn_b1': (0.0, 0.468),
     'L0_ffn_b2': (0.0, 0.1),
     'L0_ffn_bg': (0.0, 0.1)}
    factors = {}
    for name, (base, spread) in spreads.items():
        noise = np.random.default_rng([zlib.crc32(name.encode()), seed]).standard_normal(out[name].shape)
        drawn = base * np.exp(spread * noise) if base else spread * noise
        out[name] = jnp.asarray(drawn.astype(out[name].dtype))
    for name, factor in factors.items():
        out[name] = (out[name] * factor).astype(out[name].dtype)
    return out
```

```python
from contextlib import ExitStack

import numpy as np

import concourse.bass as bass
from concourse import mybir
from concourse.alu_op_type import AluOpType as ALU

F32 = mybir.dt.float32
BF16 = mybir.dt.bfloat16
F16 = mybir.dt.float16
I32 = mybir.dt.int32
U32 = mybir.dt.uint32
ACT = mybir.ActivationFunctionType
AXX = mybir.AxisListType.X

P = 128
S = 512
D = 128
H = 16
HD = D // H
T = S // P
BUCKETS = 32
FAR = 59
HALF = 64
NPARTS = 3
STACK = NPARTS * NPARTS * HD
STEPS = (S // HALF - 1) * NPARTS
ROWS1 = STACK + STEPS
ROWS2 = ROWS1 + NPARTS
UH = 8
BW = 2 * HALF - 6
B1W = P + HALF
FWD = 192
BIAS_SCALE = 16.0
LOW_SCALE = 2048.0
LEAD = 12
EPS = 1e-5
RSQRT_SEED = 1597463007.0
LN_STEPS = 4 + 3 * 4

E = 8
TOPK = 2
DFF = 512
FT = DFF // P
ROW = D + 4
ID_COL, W_COL, PAD_COL = D, D + 1, D + 3
R2 = 2 * E
C_IDS = 0
C_IOTA8 = C_IDS + T
C_SIGN = C_IOTA8 + E
C_BASE = C_SIGN + E
C_DUMMY = C_BASE + R2
C_PADID = C_DUMMY + 1
C_IOTA = C_PADID + 1
DEEP = 4


class Seq:

    def __init__(self, i, p):
        self.i, self.p, self.b = i, p, 2 * i + p

    def next(self, k):
        return Seq(self.i + (self.p + k) // 2, (self.p + k) % 2)

    @property
    def known(self):
        return isinstance(self.b, int)


def layer(nc, ctx, nb, io, out):
    sb = lambda name, shape, dt: ctx.enter_context(nc.sbuf_tensor(name, shape, dt))
    pb = lambda name, shape, dt: ctx.enter_context(nc.psum_tensor(name, shape, dt))
    sem = lambda name: ctx.enter_context(nc.semaphore(name))
    dram = lambda name, shape, dt: nc.dram_tensor(name, shape, dt, kind="Internal").ap()

    tokens = nb * S
    region = tokens + P
    tiles = tokens // P + E
    tiles += -tiles % DEEP
    ntiles = TOPK * tiles
    numbers_w = C_IOTA + tiles

    wq = sb("wq", [P, D], F32)
    wk = sb("wk", [P, D], F32)
    wv = sb("wv", [P, D], F32)
    wo = sb("wo", [P, D], F32)
    bq = sb("bq", [P, 1], F32)
    bqs = sb("bqs", [P, 1], F32)
    bk = sb("bk", [P, 1], F32)
    bv = sb("bv", [P, D], F32)
    bo = sb("bo", [P, D], F32)
    ident = sb("ident", [P, P], F32)
    pick = sb("pick", [P, 3, P], F16)
    rel = sb("rel", [BUCKETS, H], F32)
    onehot = sb("onehot", [BUCKETS, S], F32)
    stepmask = sb("stepmask", [STEPS, S + NPARTS], F32)
    stacks = sb("stacks", [P, 4, 2, UH, S], BF16)
    qst = [stacks[0:ROWS2, n, 0] for n in range(4)]
    kst = [stacks[0:ROWS2, n, 1] for n in range(4)]
    pt = [sb(f"pt{n}", [P, 4, T, S], F32) for n in range(2)]
    vp = [sb(f"vp{n}", [P, T, H, 32], F32) for n in range(2)]
    band2 = sb("band2", [P, H, BW], F16)
    band1 = sb("band1", [P, H, B1W], F16)
    xin = [sb(f"xin{n}", [P, T, D], F32) for n in range(2)]
    xres = sb("xres", [P, T, D], F32)
    x2 = sb("x2", [P, T, D], F32)
    xn = sb("xn", [P, T, D], F32)
    xnt = [sb(f"xnt{n}", [P, S], F32) for n in range(2)]
    q32 = sb("q32", [P, S], F32)
    k32 = sb("k32", [P, S], F32)
    rest = sb("rest", [P, S], F32)
    qparts = sb("qparts", [P, NPARTS, S], BF16)
    kparts = sb("kparts", [P, NPARTS, S], BF16)
    ctxu = [sb(f"ctxu{n}", [P, S], F32) for n in range(2)]
    ctxt = sb("ctxt", [P, S], F32)
    den = sb("den", [P, S // HD], F32)
    rden = sb("rden", [P, S // HD], F32)
    rdenb = sb("rdenb", [P, S], F32)
    stats, mv, ln_a, ln_y, ln_t = (
        [sb(f"{name}{n}", shape, F32) for n in range(2)]
        for name, shape in (("stats", [P, T, 6]), ("mv", [P, T, 2]), ("ln_a", [P, T]), ("ln_y", [P, T]), ("ln_t", [P, T])))
    negm = [sb(f"negm{n}", [P, UH * T], F32) for n in range(2)]
    m32 = [sb(f"m32{n}", [UH * T, P], F32) for n in range(2)]
    mrest = sb("mrest", [UH * T, P], F32)
    mparts = [sb(f"mparts{n}", [UH * T, NPARTS, P], BF16) for n in range(2)]
    dparts = sb("dparts", [STEPS, NPARTS, H], BF16)
    drest = sb("drest", [STEPS, H], F32)
    dsel = sb("dsel", [STEPS, H], F32)

    wg = sb("wg", [P, E], F32)
    bg = sb("bg", [P, E], F32)
    numbers = sb("numbers", [P, numbers_w], F32)
    order = sb("order", [P, 2, P], BF16)
    rows = sb("rows", [P, T, ROW], F32)
    rowst = sb("rowst", [P, S], F32)
    logits = sb("logits", [P, T, E], F32)
    top = sb("top", [P, T, E], F32)
    topi = sb("topi", [P, T, E], U32)
    choice = sb("choice", [P, T, TOPK], F32)
    chosen = sb("chosen", [P, T * TOPK, E], F32)
    chosenb = sb("chosenb", [P, T * TOPK, E], BF16)
    gate_d = sb("gate_d", [P, T], F32)
    gate_e = sb("gate_e", [P, T], F32)
    gate_s = sb("gate_s", [P, T], F32)
    token_base = sb("token_base", [P, 1], F32)
    counts = sb("counts", [P, R2], F32)
    place = sb("place", [P, T, R2], F32)
    slot_f = sb("slot_f", [P, T * TOPK], F32)
    slot_i = sb("slot_i", [P, T * TOPK], U32)
    b1col = sb("b1col", [P, E * DFF // P], F32)
    b2col = sb("b2col", [P, E * D // P], F32)
    bcols = sb("bcols", [P, NPARTS, (E * DFF + E * D) // P], BF16)
    brest = sb("brest", [P, E * DFF // P], F32)
    ones3 = sb("ones3", [NPARTS, P], BF16)

    w1 = stacks[:, 0].rearrange("p k h s -> p (k h s)").bitcast(F32)
    w2 = stacks[:, 1].rearrange("p k h s -> p (k h s)").bitcast(F32)
    tab_row = q32[:, 0:ntiles].bitcast(I32)
    tab_off = q32[:, ntiles:2 * ntiles].bitcast(I32)
    tab_gelu = q32[:, 2 * ntiles:3 * ntiles]
    tab_silu = k32[:, 0:ntiles]
    tab_half = k32[:, ntiles:2 * ntiles]
    pad_i = k32[:, 2 * ntiles:2 * ntiles + R2 + 1].bitcast(U32)

    s1p = [pb(f"s1p{n}", [P, S], F32) for n in range(2)]
    s2p = [pb(f"s2p{n}", [P, 2, S], F32) for n in range(2)]
    pvp = pb("pvp", [P, S], F32)
    misc = pb("misc", [P, S], F32)

    bias_scr = dram("bias_scr", (P, H, S), F32)
    qk_scr = [dram(f"qk_scr{n}", (2, NPARTS, P, S), BF16) for n in range(2)]
    ctx_scr = [dram(f"ctx_scr{n}", (4, P, S), F32) for n in range(2)]
    m_scr = [dram(f"m_scr{n}", (NPARTS, UH * T, P), BF16) for n in range(2)]
    disp = dram("disp", (R2 * region + P, ROW), F32)
    b_scr = dram("b_scr", (NPARTS, E * DFF + E * D), BF16)
    rden_scr = [dram(f"rden_scr{n}", (P, S // HD), F32) for n in range(2)]

    flat0 = pt[0][:].rearrange("p a t s -> p (a t s)")
    bias_rows = pt[1][:].rearrange("p a t s -> p (a t) s")
    toep2 = flat0[:, 0:H * BW].rearrange("p (h w) -> p h w", h=H)
    toep1 = flat0[:, 2048:2048 + H * B1W].rearrange("p (h w) -> p h w", h=H)
    steprows = flat0[0:STEPS, 5120:5120 + UH * S // 2].bitcast(BF16).rearrange("p (h s) -> p h s", h=UH)

    spare = [pt[n][:].rearrange("p a t s -> p (a t s)") for n in range(2)]
    cut = lambda n, at, width: spare[n][:, at:at + width]
    few = cut(0, 0, 16 * 64).rearrange("p (r n) -> p r n", r=R2)[:, :, 0:tokens // P]
    before = cut(0, 1024, ntiles * E).rearrange("p (n e) -> p n e", e=E)
    weighed = cut(0, 2560, ntiles * E).rearrange("p (n e) -> p n e", e=E)
    tcount = cut(0, 4096, R2)
    tsum = cut(0, 4112, R2)
    cnt = cut(0, 4128, R2)
    one8 = cut(0, 4144, E)
    tab_e = cut(0, 4160, ntiles)
    tab_t = cut(0, 4320, ntiles)
    tab_r = cut(0, 4480, ntiles)
    pad_f = cut(0, 4640, R2 + 1)
    padrow = cut(0, 4672, ROW)
    xg = [cut(1, ROW * n, ROW) for n in range(DEEP)]
    xgt = [cut(1, 640 + P * n, P) for n in range(2)]
    ids = [cut(1, 900 + 4 * n, 1).bitcast(U32) for n in range(DEEP)]
    wts = [cut(1, 916 + 4 * n, TOPK) for n in range(DEEP)]
    yw = [cut(1, 1024 + D * n, D) for n in range(DEEP)]
    gelu = [cut(1, 1536 + DFF * n, DFF) for n in range(2)]
    tanh = [cut(1, 2560 + DFF * n, DFF) for n in range(2)]
    silu = [cut(1, 3584 + DFF * n, DFF) for n in range(2)]
    acts = [cut(1, 4608 + DFF * n, DFF) for n in range(2)]
    actst = [cut(1, 5632 + DFF * n, DFF) for n in range(2)]
    b1rows = vp[0][0:NPARTS].rearrange("s t h c -> s (t h c)").bitcast(BF16)
    b2rows = spare[0][0:NPARTS, 4864:4864 + E * DFF // 2].bitcast(BF16)
    hp = s1p
    xgtp = [s2p[0][:, n, 0:P] for n in range(2)]
    actstp = [s2p[1][:, n, :] for n in range(2)]
    yp = [pvp[:, 0:D], misc[:, 0:D]]

    bias_consts_in = sem("bias_consts_in")
    consts_in = sem("consts_in")
    ones_set = sem("ones_set")
    bias_ps = sem("bias_ps")
    bias_sb = sem("bias_sb")
    bias_out = sem("bias_out")
    toep_in = sem("toep_in")
    bias_chain = sem("bias_chain")
    steps_set = sem("steps_set")
    steps_out = sem("steps_out")
    static_in = sem("static_in")
    band_set = sem("band_set")
    bqs_set = sem("bqs_set")
    x_in = [sem(f"x_in{n}") for n in range(2)]
    ln_chain = sem("ln_chain")
    xn_set = sem("xn_set")
    misc_full = sem("misc_full")
    misc_free = sem("misc_free")
    parts_chain = sem("parts_chain")
    qk_parts = sem("qk_parts")
    qk_out = [sem(f"qk_out{n}") for n in range(2)]
    stack_in = [sem(f"stack_in{n}") for n in range(4)]
    s1_full = sem("s1_full")
    s1_free = sem("s1_free")
    m_parts = sem("m_parts")
    m_chain = sem("m_chain")
    m_out = [sem(f"m_out{n}") for n in range(2)]
    m_in = [sem(f"m_in{n}") for n in range(4)]
    s2_full = sem("s2_full")
    exp_done = sem("exp_done")
    pv_done = sem("pv_done")
    ctx_copied = sem("ctx_copied")
    ctx_out = [sem(f"ctx_out{n}") for n in range(2)]
    den_in = sem("den_in")
    rden_set = sem("rden_set")
    rden_out = sem("rden_out")
    norm_in = sem("norm_in")
    ctxt_set = sem("ctxt_set")
    xres_in = sem("xres_in")
    xres_set = sem("xres_set")
    x2_out = sem("x2_out")
    ln2_chain = sem("ln2_chain")
    rows_set = sem("rows_set")
    gate_chain = sem("gate_chain")
    gate_diff = sem("gate_diff")
    gate_exp = sem("gate_exp")
    chosen_set = sem("chosen_set")
    slots_set = sem("slots_set")
    dispatched = sem("dispatched")
    bcol_in = sem("bcol_in")
    bcol_chain = sem("bcol_chain")
    bcol_set = sem("bcol_set")
    bcol_out = sem("bcol_out")
    brow_in = sem("brow_in")
    dummy_set = sem("dummy_set")
    base_set = sem("base_set")
    w_in = sem("w_in")
    table_chain = sem("table_chain")
    pads_set = sem("pads_set")
    padded = sem("padded")
    tables_set = sem("tables_set")
    xg_in = [sem(f"xg_in{n}") for n in range(DEEP)]
    meta_set = sem("meta_set")
    xgt_full = sem("xgt_full")
    xgt_set = sem("xgt_set")
    h_full = sem("h_full")
    functions_set = sem("functions_set")
    silu_set = sem("silu_set")
    acts_set = sem("acts_set")
    actst_full = sem("actst_full")
    actst_set = sem("actst_set")
    y_full = sem("y_full")
    y_set = sem("y_set")
    y_out = [sem(f"y_out{n}") for n in range(DEEP)]
    dummy_out = sem("dummy_out")
    dispatch_started = sem("dispatch_started")
    stats_seen = sem("stats_seen")
    logits_seen = sem("logits_seen")
    split_started = sem("split_started")
    add_started = sem("add_started")

    LAST = nb - 1

    PROLOGUE = ["xt0", "q0", "k0", "v0", "xt1", "q1", "k1", "m0"]
    SLOT = ["rank", "m_mid", "v", "xt", "q", "k", "out", "rowst", "m_end", "gate"]
    TAIL = ["rank_a", "out", "rowst", "gate", "rank_b"]

    def slot_jobs(b):
        jobs = list(SLOT)
        if b == 0:
            jobs = [j for j in jobs if j not in ("out", "rowst", "gate")]
        if b < 2:
            jobs.remove("rank")
        if b + 2 > LAST:
            jobs = [j for j in jobs if j not in ("xt", "q", "k")]
        if b == LAST:
            jobs = [j for j in jobs if j not in ("v", "m_end")]
        return jobs

    def misc_count(seq, job):
        if not seq.known:
            return len(PROLOGUE) + len(slot_jobs(0)) + len(slot_jobs(1)) + len(SLOT) * (seq.b - 2) + SLOT.index(job) + 1
        before = len(PROLOGUE) + sum(len(slot_jobs(b)) for b in range(min(seq.b, nb)))
        return before + (TAIL if seq.b > LAST else slot_jobs(seq.b)).index(job) + 1

    def out_count(seq):
        return misc_count(seq.next(1), "out")

    def head_no(seq, h):
        return H * seq.b + h

    def slots(emit, eng):
        emit(Seq(0, 0))
        emit(Seq(0, 1))
        if nb > 4:
            with eng.Fori(1, nb // 2 - 1) as i:
                emit(Seq(i, 0))
                emit(Seq(i, 1))
        emit(Seq(nb // 2 - 1, 0))
        emit(Seq(nb // 2 - 1, 1))

    def ahead(seq, h):
        g = h + LEAD
        s = seq.next(g // H)
        return None if s.known and s.b > LAST else (s, g % H)

    def unit_buf(seq, h):
        return 2 * seq.p + h // UH

    def unit_no(seq, h):
        return 2 * seq.b + h // UH

    turns = ntiles // DEEP

    def tile_loop(emit, eng, phases):
        emit(0, 0)
        cuts = [1, turns // 2, turns - 1] if phases else [1, turns - 1]
        for c in range(len(cuts) - 1):
            with eng.Fori(cuts[c], cuts[c + 1]) as m:
                emit(m, c)
        emit(turns - 1, 1)

    def at_least(eng, sem_, value, from_):
        if not isinstance(from_, int) or from_ >= 0:
            eng.wait_ge(sem_, value)

    def experts_loads(sp):
        sp.wait_ge(pv_done, 4 * T * nb)
        sp.dma_start(b2rows.rearrange("s (e f) -> s e f", e=E)[:, :, 0:D], b_scr[:, E * DFF:].rearrange("s (e d) -> s e d", e=E)).then_inc(brow_in, 16)
        sp.wait_ge(tables_set, 1)
        sp.wait_ge(padded, 16 * (R2 + 1))
        sp.wait_ge(dispatched, 16 * TOPK * T * nb)

        def turn(m, c):
            for k in range(DEEP):
                n = DEEP * m + k
                row = sp.value_load(tab_row[0:1, bass.ds(n, 1)], min_val=0, max_val=R2 * region)
                at_least(sp, xgt_full, n - DEEP + 1, n - DEEP)
                at_least(sp, meta_set, n - DEEP + 1, n - DEEP)
                sp.dma_start(xg[k], disp[bass.ds(row, P)]).then_inc(xg_in[k], 16)

        tile_loop(turn, sp, False)
        for k in range(DEEP):
            sp.wait_ge(y_out[k], 16 * turns)

    def experts_products(pe):
        pe.wait_ge(w_in, 32)
        pe.wait_ge(brow_in, 32)
        pe.wait_ge(bcol_set, 2)
        pe.wait_ge(tables_set, 1)

        def transpose_rows(n, k, m):
            pe.wait_ge(xg_in[k], 16 * (m + 1))
            at_least(pe, xgt_set, n - 1, n - 2)
            nc.tensor.transpose(xgtp[k % 2], xg[k][:, 0:D], ident[:]).then_inc(xgt_full, 1)

        def hidden(n, k):
            off = pe.value_load(tab_off[0:1, bass.ds(n, 1)], min_val=0, max_val=(E - 1) * DFF)
            pe.wait_ge(xgt_set, n + 1)
            at_least(pe, silu_set, n - 1, n - 2)
            nc.tensor.matmul(hp[k % 2][:], xgt[k % 2], w1[:, bass.ds(off, DFF)], start=True, stop=False)
            nc.tensor.matmul(hp[k % 2][:], ones3[:], b1rows[:, bass.ds(off, DFF)], start=False, stop=True).then_inc(h_full, 1)

        def transpose_acts(n, k):
            pe.wait_ge(acts_set, n + 1)
            at_least(pe, actst_set, n - 1, n - 2)
            for f in range(FT):
                mm = nc.tensor.transpose(actstp[k % 2][:, P * f:P * f + P], acts[k % 2][:, P * f:P * f + P], ident[:])
            mm.then_inc(actst_full, 1)

        def back(n, k):
            off = pe.value_load(tab_off[0:1, bass.ds(n, 1)], min_val=0, max_val=(E - 1) * DFF)
            pe.wait_ge(actst_set, n + 1)
            at_least(pe, y_set, n - 1, n - 2)
            for f in range(FT):
                nc.tensor.matmul(yp[k % 2], actst[k % 2][:, P * f:P * f + P], w2[:, bass.ds(off + P * f, D)], start=(f == 0), stop=False)
            nc.tensor.matmul(yp[k % 2], ones3[:], b2rows[:, bass.ds(off, D)], start=False, stop=True).then_inc(y_full, 1)

        for n in range(3):
            transpose_rows(n, n, 0)
        for n in range(2):
            hidden(n, n)

        def turn(m, c):
            for k in range(DEEP):
                n = DEEP * m + k
                left = ntiles - n if isinstance(n, int) else DEEP
                transpose_acts(n, k)
                if left > 2:
                    hidden(n + 2, (k + 2) % DEEP)
                back(n, k)
                if left > 3:
                    transpose_rows(n + 3, (k + 3) % DEEP, m + (k + 3) // DEEP)

        tile_loop(turn, pe, False)

    def experts_functions(act):
        act.wait_ge(tables_set, 1)

        def copy_rows(n, k):
            act.wait_ge(xgt_full, n + 1)
            at_least(act, h_full, n - 1, n - 2)
            nc.scalar.copy(xgt[k % 2], xgtp[k % 2]).then_inc(xgt_set, 1)

        def functions(n, k):
            act.wait_ge(h_full, n + 1)
            at_least(act, acts_set, n - 1, n - 2)
            nc.scalar.activation(gelu[k % 2], hp[k % 2][:], ACT.Gelu, scale=tab_gelu[:, bass.ds(n, 1)])
            nc.scalar.activation(tanh[k % 2], hp[k % 2][:], ACT.Tanh, scale=tab_half[:, bass.ds(n, 1)]).then_inc(functions_set, 1)

        for n in range(3):
            copy_rows(n, n)
        for n in range(2):
            functions(n, n)

        def turn(m, c):
            for k in range(DEEP):
                n = DEEP * m + k
                left = ntiles - n if isinstance(n, int) else DEEP
                if left > 2:
                    functions(n + 2, (k + 2) % DEEP)
                if left > 3:
                    copy_rows(n + 3, (k + 3) % DEEP)

        tile_loop(turn, act, False)

    def experts_vectors(dve):
        done = [0]

        def link(ins):
            done[0] += 1
            ins.then_inc(table_chain, 1)
            dve.wait_ge(table_chain, done[0])

        link(nc.vector.tensor_tensor(cnt, counts[:], numbers[:, C_BASE:C_BASE + R2], ALU.subtract))
        link(nc.vector.tensor_scalar(pad_f[:, 0:R2], counts[:], numbers[:, C_PADID:C_PADID + 1], -float(tokens), ALU.add, ALU.add))
        link(nc.vector.tensor_copy(pad_f[:, R2:], numbers[:, C_DUMMY:C_DUMMY + 1]))
        link(nc.vector.tensor_copy(pad_i, pad_f))
        link(nc.vector.memset(padrow, 0.0))
        nc.vector.memset(padrow[:, PAD_COL:PAD_COL + 1], 1.0)
        nc.vector.tensor_copy(padrow[:, ID_COL:ID_COL + 1], numbers[:, C_PADID:C_PADID + 1]).then_inc(pads_set, 1)
        link(nc.vector.tensor_scalar(cnt, cnt, 1.0 / P, None, ALU.mult))
        wide = (P, R2, tokens // P)
        link(nc.vector.tensor_tensor(few, numbers[:, C_IOTA:C_IOTA + tokens // P].rearrange("p (o n) -> p o n", o=1).to_broadcast(wide),
                                     cnt.rearrange("p (r o) -> p r o", o=1).to_broadcast(wide), ALU.is_lt))
        link(nc.vector.tensor_reduce(tcount, few, AXX, ALU.add))
        link(nc.vector.memset(one8, 1.0))
        for c in range(TOPK):
            link(nc.vector.tensor_tensor_scan(tsum[:, E * c:E * c + E], one8, tcount[:, E * c:E * c + E], 0.0, ALU.mult, ALU.add))
        wide = (P, tiles, E)
        for c in range(TOPK):
            mine = slice(tiles * c, tiles * c + tiles)
            per_e = lambda ap: ap.rearrange("p (o e) -> p o e", o=1).to_broadcast(wide)
            link(nc.vector.tensor_tensor(before[:, mine, :], per_e(tsum[:, E * c:E * c + E]),
                                         numbers[:, C_IOTA:C_IOTA + tiles].rearrange("p (n o) -> p n o", o=1).to_broadcast(wide), ALU.is_le))
            link(nc.vector.tensor_tensor(weighed[:, mine, :], before[:, mine, :], per_e(tcount[:, E * c:E * c + E]), ALU.mult))
            link(nc.vector.tensor_reduce(tab_t[:, mine], weighed[:, mine, 0:E - 1], AXX, ALU.add))
            link(nc.vector.tensor_tensor(tab_t[:, mine], numbers[:, C_IOTA:C_IOTA + tiles], tab_t[:, mine], ALU.subtract))
            link(nc.vector.tensor_scalar(tab_t[:, mine], tab_t[:, mine], float(P), float(E * c * region), ALU.mult, ALU.add))
            link(nc.vector.tensor_tensor(weighed[:, mine, :], before[:, mine, :], per_e(numbers[:, C_SIGN:C_SIGN + E]), ALU.mult))
        link(nc.vector.tensor_reduce(tab_e, before[:, :, 0:E - 1], AXX, ALU.add))
        link(nc.vector.tensor_scalar(tab_r, tab_e, float(DFF), None, ALU.mult))
        link(nc.vector.tensor_copy(tab_off, tab_r))
        link(nc.vector.tensor_reduce(tab_silu, weighed[:, :, 0:E - 1], AXX, ALU.add))
        link(nc.vector.tensor_scalar(tab_gelu, tab_silu, -1.0, 1.0, ALU.mult, ALU.add))
        link(nc.vector.tensor_scalar(tab_half, tab_silu, 0.5, None, ALU.mult))
        link(nc.vector.scalar_tensor_tensor(tab_r, tab_e, float(region), tab_t, ALU.mult, ALU.add))
        link(nc.vector.tensor_scalar(tab_t, tab_r, -1.0, float(R2 * region), ALU.mult, ALU.add))
        link(nc.vector.tensor_tensor(tab_t, tab_t, before[:, :, E - 1], ALU.mult))
        link(nc.vector.tensor_tensor(tab_r, tab_r, tab_t, ALU.add))
        nc.vector.tensor_copy(tab_row, tab_r).then_inc(tables_set, 1)

        def take_numbers(n, k, m):
            dve.wait_ge(xg_in[k], 16 * (m + 1))
            at_least(dve, y_out[k], 16 * m, m - 1)
            nc.vector.scalar_tensor_tensor(ids[k], xg[k][:, PAD_COL:PAD_COL + 1], float(P * k), xg[k][:, ID_COL:ID_COL + 1], ALU.mult, ALU.add)
            nc.vector.tensor_copy(wts[k], xg[k][:, W_COL:W_COL + TOPK]).then_inc(meta_set, 1)

        def activations(n, k):
            dve.wait_ge(functions_set, n + 1)
            nc.vector.scalar_tensor_tensor(silu[k % 2], tanh[k % 2], tab_silu[:, bass.ds(n, 1)], hp[k % 2][:], ALU.add, ALU.mult).then_inc(silu_set, 1)
            dve.wait_ge(silu_set, n + 1)
            at_least(dve, actst_full, n - 1, n - 2)
            nc.vector.scalar_tensor_tensor(acts[k % 2], silu[k % 2], 0.5, gelu[k % 2], ALU.mult, ALU.add).then_inc(acts_set, 1)

        def copy_acts(n, k):
            dve.wait_ge(actst_full, n + 1)
            at_least(dve, y_full, n - 1, n - 2)
            nc.vector.tensor_copy(actst[k % 2], actstp[k % 2]).then_inc(actst_set, 1)

        def weigh(n, k, c):
            dve.wait_ge(y_full, n + 1)
            nc.vector.tensor_scalar(yw[k], yp[k % 2], wts[k][:, c:c + 1], None, ALU.mult).then_inc(y_set, 1)

        dve.wait_ge(tables_set, 1)
        for n in range(3):
            take_numbers(n, n, 0)
        activations(0, 0)

        def turn(m, c):
            for k in range(DEEP):
                n = DEEP * m + k
                left = ntiles - n if isinstance(n, int) else DEEP
                copy_acts(n, k)
                if left > 1:
                    activations(n + 1, (k + 1) % DEEP)
                weigh(n, k, c)
                if left > 3:
                    take_numbers(n + 3, (k + 3) % DEEP, m + (k + 3) // DEEP)

        tile_loop(turn, dve, True)

    def experts_scatters(pool):
        pool.wait_ge(pads_set, 1)
        for r in range(R2 + 1):
            pool.indirect_dma_start(disp, bass.IndirectOffsetOnAxis(pad_i[:, r:r + 1], 0), padrow, None).then_inc(padded, 16)
        pool.wait_ge(x2_out, 16 * nb)
        pool.wait_ge(dummy_out, 16)

        def turn(m, c):
            if isinstance(m, int) and m == turns - 1:
                c = 1
            for k in range(DEEP):
                pool.wait_ge(y_set, DEEP * m + k + 1).then_inc(add_started, 1)
                pool.indirect_dma_start(out, bass.IndirectOffsetOnAxis(ids[k], 0), yw[k], None, compute_op=ALU.add).then_inc(y_out[k], 16)

        half = turns // 2
        turn(0, 0)
        with pool.Fori(1, half) as m:
            turn(m, 0)
        for k in range(DEEP):
            pool.wait_ge(y_out[k], 16 * half)
        with pool.Fori(half, turns - 1) as m:
            turn(m, 1)
        turn(turns - 1, 1)

    block = ctx.enter_context(nc.Block())

    @block.sync
    def _(sp):
        for dst, src in ((rel[:], io["rel"]), (onehot[:], io["onehot"]), (stepmask[:], io["stepmask"])):
            sp.dma_start(dst, src).then_inc(bias_consts_in, 16)

        def load_x(seq):
            if not (seq.known and seq.b < 2):
                sp.wait_ge(xn_set, seq.b - 1)
            sp.dma_start(xin[seq.p][:], io["x"][bass.ds(seq.b, 1)].rearrange("o (t p) d -> p (o t) d", p=P)).then_inc(x_in[seq.p], 16)

        def store_parts(seq):
            sp.wait_ge(qk_parts, 2 * seq.b + 1)
            sp.dma_start(qk_scr[seq.p][0].rearrange("i p s -> p i s"), qparts[:]).then_inc(qk_out[0], 16)
            sp.wait_ge(qk_parts, 2 * seq.b + 2)
            sp.dma_start(qk_scr[seq.p][1].rearrange("i p s -> p i s"), kparts[:]).then_inc(qk_out[1], 16)

        def load_stack(seq, half):
            buf = 2 * seq.p + half
            if not (seq.known and seq.b < 2):
                sp.wait_ge(s2_full, 2 * (H * (seq.b - 2) + UH * (half + 1)))
            for k in range(2):
                sp.wait_ge(qk_out[k], 16 * (seq.b + 1))
            for i in range(NPARTS):
                for j in range(NPARTS):
                    r = HD * (NPARTS * i + j)
                    for dst, which, part in ((qst, 0, i), (kst, 1, j)):
                        src = qk_scr[seq.p][which, part].rearrange("(h d) s -> d h s", d=HD)
                        sp.dma_start(dst[buf][r:r + HD], src[:, UH * half:UH * half + UH, :]).then_inc(stack_in[buf], 16)

        def load_maxima(seq, half):
            buf = 2 * seq.p + half
            sp.wait_ge(m_parts, 2 * seq.b + half + 1)
            sp.dma_start(m_scr[half].rearrange("s g n -> g s n"), mparts[half][:]).then_inc(m_out[half], 16)
            sp.wait_ge(m_out[half], 16 * (seq.b + 1))
            sp.dma_start(qst[buf][ROWS1:ROWS2].rearrange("s h n -> s (h n)"),
                         m_scr[half].rearrange("s g n -> s (g n)")).then_inc(m_in[buf], 16)

        def store_ctx(seq, g):
            sp.wait_ge(ctx_copied, 4 * seq.b + g + 1)
            sp.dma_start(ctx_scr[seq.p][g], ctxu[g % 2][:]).then_inc(ctx_out[g % 2], 16)

        load_x(Seq(0, 0))
        load_x(Seq(0, 1))
        sp.wait_ge(dummy_set, 1)
        sp.dma_start(out[tokens:].rearrange("(k p) d -> p k d", p=P), xn[:, 0:DEEP, :]).then_inc(dummy_out, 16)
        for dst, src in ((ident[:], io["ident"]), (wg[:], io["wg"]), (numbers[:], io["numbers"]), (order[:], io["order"]),
                         (bg[:], io["bg"].rearrange("(o e) -> o e", o=1).to_broadcast((P, E))),
                         (wq[:], io["wq"]), (wk[:], io["wk"]), (wv[:], io["wv"]),
                         (wo[:], io["wo"]), (bq[:], io["bq"].rearrange("(p o) -> p o", o=1)),
                         (bk[:], io["bk"].rearrange("(p o) -> p o", o=1)),
                         (bv[:], io["bv"].rearrange("(o d) -> o d", o=1).to_broadcast((P, D))),
                         (bo[:], io["bo"].rearrange("(o d) -> o d", o=1).to_broadcast((P, D))),
                         (pick[:], io["pick"].rearrange("k p n -> p k n"))):
            sp.dma_start(dst, src).then_inc(consts_in, 16)
        for buf in range(4):
            sp.dma_start(kst[buf][STACK:ROWS2], io["kstatic"].rearrange("r (o s) -> r o s", o=1).to_broadcast((ROWS2 - STACK, UH, S))).then_inc(static_in, 16)
        sp.wait_ge(bias_sb, H)
        sp.dma_start(bias_scr, bias_rows).then_inc(bias_out, 16)
        for half in range(2):
            sp.wait_ge(steps_set, half + 1)
            for buf in (half, half + 2):
                sp.dma_start(qst[buf][STACK:ROWS1], steprows).then_inc(steps_out, 16)
        sp.wait_ge(bias_out, 16)
        for lo in (0, HALF):
            sp.dma_start(toep2[lo:lo + HALF], bass.AP(bias_scr.tensor, HALF - 1, [[H * S - 1, HALF], [S, H], [1, BW]])).then_inc(toep_in, 16)
        sp.dma_start(toep1, bass.AP(bias_scr.tensor, FWD + P - 1, [[H * S - 1, P], [S, H], [1, B1W]])).then_inc(toep_in, 16)
        sp.dma_start(b1col[:], io["b1"].rearrange("e (a f) -> (e a) f", a=P // E)).then_inc(bcol_in, 16)
        sp.dma_start(b2col[:], io["b2"].rearrange("e (a d) -> (e a) d", a=P // E)).then_inc(bcol_in, 16)
        store_parts(Seq(0, 0))
        for half in range(2):
            load_stack(Seq(0, 0), half)
        store_parts(Seq(0, 1))
        load_stack(Seq(0, 1), 0)
        load_maxima(Seq(0, 0), 0)
        sp.wait_ge(bcol_set, 2)
        nb1, nb2 = E * DFF // P, E * D // P
        sp.dma_start(b_scr[:, 0:E * DFF].rearrange("s (p f) -> p s f", p=P), bcols[:, :, 0:nb1]).then_inc(bcol_out, 16)
        sp.dma_start(b_scr[:, E * DFF:].rearrange("s (p f) -> p s f", p=P), bcols[:, :, nb1:]).then_inc(bcol_out, 16)

        def slot(seq):
            prev, nxt, inp = seq.next(-1), seq.next(1), seq.next(2)
            first = seq.known and seq.b == 0
            last = seq.known and seq.b == LAST
            inputs = not (seq.known and seq.b + 2 > LAST)
            if inputs:
                load_x(inp)
            if not first:
                if not (seq.known and seq.b == 1):
                    sp.wait_ge(misc_free, out_count(seq.next(-2)))
                sp.dma_start(xres[:], io["x"][bass.ds(prev.b, 1)].rearrange("o (t p) d -> p (o t) d", p=P)).then_inc(xres_in, 16)
                store_ctx(prev, 2)
            if not last:
                load_stack(nxt, 1)
            load_maxima(seq, 1)
            if not first:
                finish_ctx(prev)
            store_ctx(seq, 0)
            if not first:
                store_x2(prev)
            if inputs:
                store_parts(inp)
                load_stack(inp, 0)
            if not last:
                load_maxima(nxt, 0)
            store_ctx(seq, 1)
            if last:
                load_expert_weights()

        def finish_ctx(seq):
            store_ctx(seq, 3)
            sp.wait_ge(ctx_out[0], 32 * (seq.b + 1))
            sp.wait_ge(ctx_out[1], 32 * (seq.b + 1))
            heads = ctx_scr[seq.p].rearrange("g (c r) s -> (g c) r s", r=32)
            sp.dma_start(den[:], heads[:, HD, :].rearrange("h (j n) -> h j n", j=HD)).then_inc(den_in, 16)
            sp.dma_start(ctxt[:], heads[:, 0:HD, :]).then_inc(norm_in, 16)
            sp.wait_ge(rden_set, seq.b + 1)
            sp.dma_start(rden_scr[seq.p], rden[:]).then_inc(rden_out, 16)
            sp.wait_ge(rden_out, 16 * (seq.b + 1))
            sp.dma_start(rdenb[:], rden_scr[seq.p].rearrange("(h o j) n -> h o (j n)", j=HD, o=1).to_broadcast((H, HD, S))).then_inc(norm_in, 16)

        def store_x2(seq):
            sp.wait_ge(misc_free, out_count(seq))
            sp.dma_start(out[0:tokens].rearrange("(b t p) d -> b p t d", p=P, t=T)[bass.ds(seq.b, 1)].rearrange("o p t d -> p (o t) d"),
                         x2[:]).then_inc(x2_out, 16)

        def load_expert_weights():
            sp.wait_ge(s2_full, 2 * H * LAST)
            sp.wait_ge(bcol_out, 32)
            sp.wait_ge(pv_done, 4 * T * LAST)
            sp.dma_start(b1rows, b_scr[:, 0:E * DFF]).then_inc(brow_in, 16)
            sp.dma_start(w1.rearrange("d (e f) -> d e f", e=E), io["w1"].rearrange("e d f -> d e f")).then_inc(w_in, 16)
            sp.dma_start(w2.rearrange("f (e d) -> f e d", d=D), io["w2"].rearrange("e (t f) d -> f (e t) d", f=P)).then_inc(w_in, 16)

        slots(slot, sp)
        end = Seq(LAST // 2, LAST % 2)
        sp.wait_ge(misc_free, out_count(Seq((LAST - 1) // 2, (LAST - 1) % 2)))
        sp.dma_start(xres[:], io["x"][LAST:LAST + 1].rearrange("o (t p) d -> p (o t) d", p=P)).then_inc(xres_in, 16)
        store_ctx(end, 2)
        finish_ctx(end)
        store_x2(end)
        sp.wait_ge(x2_out, 16 * nb)
        experts_loads(sp)

    @block.tensor
    def _(pe):
        filled = [0]

        def open_misc(count):
            if not (isinstance(count, int) and count == 1):
                pe.wait_ge(misc_free, count - 1)

        def job_xt(seq, count):
            open_misc(count)
            pe.wait_ge(xn_set, seq.b + 1)
            for t in range(T):
                mm = nc.tensor.transpose(misc[:, P * t:P * t + P], xn[:, t, :], ident[:])
            mm.then_inc(misc_full, 1)

        def job_project(seq, count, w, xt_count):
            open_misc(count)
            pe.wait_ge(misc_free, xt_count)
            nc.tensor.matmul(misc[:], w[:], xnt[seq.p][:], start=True, stop=True).then_inc(misc_full, 1)

        def job_v(seq, count):
            open_misc(count)
            for t in range(T):
                mm = nc.tensor.matmul(misc[:, D * t:D * t + D], xnt[seq.p][:, P * t:P * t + P], wv[:], start=True, stop=True)
            mm.then_inc(misc_full, 1)

        def job_m(seq, half, count):
            open_misc(count)
            pe.wait_ge(s1_free, 4 * (head_no(seq, UH * half) + UH))
            nc.tensor.transpose(misc[0:UH * T, 0:P], negm[half][:], ident[:]).then_inc(misc_full, 1)

        def job_out(seq, count):
            open_misc(count)
            pe.wait_ge(ctxt_set, seq.b + 1)
            for t in range(T):
                mm = nc.tensor.matmul(misc[:, D * t:D * t + D], ctxt[:, P * t:P * t + P], wo[:], start=True, stop=True)
            mm.then_inc(misc_full, 1)

        def job_rowst(seq, count):
            open_misc(count)
            pe.wait_ge(rows_set, seq.b + 1)
            for t in range(T):
                mm = nc.tensor.transpose(misc[:, P * t:P * t + P], rows[:, t, 0:D], ident[:])
            mm.then_inc(misc_full, 1)

        def job_gate(seq, count):
            open_misc(count)
            for t in range(T):
                mm = nc.tensor.matmul(misc[:, E * t:E * t + E], rowst[:, P * t:P * t + P], wg[:], start=True, stop=True)
            mm.then_inc(misc_full, 1)

        def job_rank(seq, count):
            open_misc(count)
            pe.wait_ge(chosen_set, seq.b + 1)
            for t in range(T + 1):
                dst = misc[:, R2 * t:R2 * t + R2]
                whole = range(t)
                for u in whole:
                    mm = nc.tensor.matmul(dst, order[:, 1, :], chosenb[:, TOPK * u:TOPK * u + TOPK, :],
                                          start=(u == 0), stop=(t == T and u == T - 1))
                if t < T:
                    mm = nc.tensor.matmul(dst, order[:, 0, :], chosenb[:, TOPK * t:TOPK * t + TOPK, :],
                                          start=(t == 0), stop=True)
            mm.then_inc(misc_full, 1)

        def max_scores(seq, h, tiles):
            buf, hh = unit_buf(seq, h), h % UH
            if h % UH == 0 and tiles[0] == 0:
                uses = 18 * 16
                pe.wait_ge(stack_in[buf], uses * (seq.i + 1))
            for t in tiles:
                n = 4 * head_no(seq, h) + t
                if not (seq.known and n < 2):
                    pe.wait_ge(s1_free, n - 1)
                lo = max(0, P * t - HALF)
                nc.tensor.matmul(s1p[t % 2][:], qst[buf][0:ROWS1, hh, P * t:P * t + P], kst[buf][0:ROWS1, hh, :],
                                 start=True, stop=False)
                nc.tensor.matmul(s1p[t % 2][:, lo:P * t + P], pick[:, 2, :], band1[:, h, lo - P * t + HALF:],
                                 start=False, stop=True).then_inc(s1_full, 1)

        def exp_scores(seq, h, pair):
            buf, hh = unit_buf(seq, h), h % UH
            n = 2 * head_no(seq, h) + pair
            if h % UH == 0 and pair == 0:
                pe.wait_ge(m_in[buf], 16 * (seq.i + 1))
            if not (seq.known and n < 2):
                pe.wait_ge(exp_done, n - 1)
            for j in range(2):
                t = 2 * pair + j
                out = s2p[pair][:, j, :]
                nc.tensor.matmul(out, kst[buf][:, hh, P * t:P * t + P], qst[buf][:, hh, :], start=True, stop=False)
                for g in range(2):
                    q0 = P * t + HALF * g
                    w = min(BW, S - q0)
                    mm = nc.tensor.matmul(out[:, q0:q0 + w], pick[:, g, :], band2[:, h, 0:w], start=False, stop=(g == 1))
            mm.then_inc(s2_full, 1)

        def weigh_values(seq, h):
            t, par = h % 4, (h // 4) % 2
            g = 4 * seq.b + h // 4
            if t == 0:
                pe.wait_ge(exp_done, 8 * (g + 1))
                if not (seq.known and g == 0):
                    pe.wait_ge(ctx_copied, g)
            for c in range(4):
                mm = nc.tensor.matmul(pvp[32 * c:32 * c + 32, :], vp[seq.p][:, t, 4 * (h // 4) + c, :],
                                      pt[par][:, c, t, :], start=(t == 0), stop=(t == T - 1))
            mm.then_inc(pv_done, 1)

        pe.wait_ge(bias_consts_in, 48)
        banks = [s2p[0][:, 0, :], s2p[0][:, 1, :], s2p[1][:, 0, :], s2p[1][:, 1, :]]
        for h in range(H):
            if h >= 4:
                pe.wait_ge(bias_sb, h - 3)
            nc.tensor.matmul(banks[h % 4], rel[:, h:h + 1].to_broadcast((BUCKETS, P)), onehot[:], start=True, stop=True).then_inc(bias_ps, 1)
        pe.wait_ge(consts_in, 14 * 16)
        for n in range(2):
            s = Seq(0, n)
            k = PROLOGUE.index(f"xt{n}") + 1
            job_xt(s, k)
            job_project(s, k + 1, wq, k)
            job_project(s, k + 2, wk, k)
            if n == 0:
                job_v(s, k + 3)
        pe.wait_ge(static_in, 64)
        pe.wait_ge(steps_out, 64)
        pe.wait_ge(band_set, 1)
        for h in range(UH):
            max_scores(Seq(0, 0), h, range(T))
        job_m(Seq(0, 0), 0, len(PROLOGUE))
        for h in range(UH, LEAD):
            max_scores(Seq(0, 0), h, range(T))

        def slot(seq):
            prev, nxt, inp = seq.next(-1), seq.next(1), seq.next(2)
            first = seq.known and seq.b == 0
            last = seq.known and seq.b == LAST
            inputs = not (seq.known and seq.b + 2 > LAST)
            for h in range(H):
                exp_scores(seq, h, 0)
                lead = ahead(seq, h)
                if lead:
                    max_scores(*lead, (0, 1))
                if h == 1 and not (seq.known and seq.b < 2):
                    job_rank(seq.next(-2), misc_count(seq, "rank"))
                if h == 5:
                    job_m(seq, 1, misc_count(seq, "m_mid"))
                if h == 6 and not last:
                    job_v(nxt, misc_count(seq, "v"))
                if inputs:
                    if h == 8:
                        job_xt(inp, misc_count(seq, "xt"))
                    if h == 9:
                        job_project(inp, misc_count(seq, "q"), wq, misc_count(seq, "xt"))
                    if h == 10:
                        job_project(inp, misc_count(seq, "k"), wk, misc_count(seq, "xt"))
                if not first:
                    if h == 11:
                        job_out(prev, misc_count(seq, "out"))
                    if h == 13:
                        job_rowst(prev, misc_count(seq, "rowst"))
                    if h == 15:
                        job_gate(prev, misc_count(seq, "gate"))
                exp_scores(seq, h, 1)
                if lead:
                    max_scores(*lead, (2, 3))
                if h == 13 and not last:
                    job_m(nxt, 0, misc_count(seq, "m_end"))
                if h >= 4:
                    weigh_values(seq, h - 4)
                elif not first:
                    weigh_values(prev, h + 12)

        slots(slot, pe)
        end = Seq(LAST // 2, LAST % 2)
        for h in range(4):
            weigh_values(end, h + 12)
        job_rank(end.next(-1), misc_count(end.next(1), "rank_a"))
        job_out(end, out_count(end))
        job_rowst(end, misc_count(end.next(1), "rowst"))
        job_gate(end, misc_count(end.next(1), "gate"))
        job_rank(end, misc_count(end.next(1), "rank_b"))
        experts_products(pe)

    @block.scalar
    def _(act):
        def copy_xt(seq, count):
            act.wait_ge(misc_full, count)
            nc.scalar.copy(xnt[seq.p][:], misc[:]).then_inc(misc_free, 1)

        def copy_q(seq, count):
            act.wait_ge(misc_full, count)
            if not (seq.known and seq.b == 0):
                act.wait_ge(qk_parts, 2 * seq.b - 1)
            nc.scalar.activation(q32[:], misc[:], ACT.Identity, bias=bqs[:], scale=HD ** -0.5).then_inc(misc_free, 1)

        def copy_k(seq, count):
            act.wait_ge(misc_full, count)
            if not (seq.known and seq.b == 0):
                act.wait_ge(qk_parts, 2 * seq.b)
            nc.scalar.activation(k32[:], misc[:], ACT.Identity, bias=bk[:], scale=1.0).then_inc(misc_free, 1)

        def copy_rowst(seq, count):
            act.wait_ge(misc_full, count)
            nc.scalar.copy(rowst[:], misc[:]).then_inc(misc_free, 1)

        def gate_exponent(seq):
            act.wait_ge(gate_diff, seq.b + 1)
            nc.scalar.activation(gate_e[:], gate_d[:], ACT.Exp).then_inc(gate_exp, 1)

        def copy_ctx(seq, g):
            n = 4 * seq.b + g
            act.wait_ge(pv_done, 4 * (n + 1))
            if not (seq.known and n < 2):
                act.wait_ge(ctx_out[g % 2], 16 * (2 * seq.b + g // 2))
            nc.scalar.copy(ctxu[g % 2][:], pvp[:]).then_inc(ctx_copied, 1)

        for h in range(H):
            act.wait_ge(bias_ps, h + 1)
            bank = s2p[h % 4 // 2][:, h % 2, :]
            nc.scalar.copy(bias_rows[:, h, :], bank).then_inc(bias_sb, 1)
        act.wait_ge(consts_in, 14 * 16)
        nc.scalar.mul(bqs[:], bq[:], HD ** -0.5).then_inc(bqs_set, 1)
        act.wait_ge(bqs_set, 1)
        for n in range(2):
            k = PROLOGUE.index(f"xt{n}") + 1
            copy_xt(Seq(0, n), k)
            copy_q(Seq(0, n), k + 1)
            copy_k(Seq(0, n), k + 2)
        act.wait_ge(band_set, 1)
        act.wait_ge(steps_out, 64)
        act.wait_ge(bias_out, 16)

        def slot(seq):
            prev, inp = seq.next(-1), seq.next(2)
            first = seq.known and seq.b == 0
            inputs = not (seq.known and seq.b + 2 > LAST)
            for h in range(H):
                g = 4 * seq.b + h // 4
                if h % 4 == 0 and not (seq.known and g < 2):
                    act.wait_ge(pv_done, 4 * (g - 1))
                for pair in range(2):
                    act.wait_ge(s2_full, 2 * head_no(seq, h) + pair + 1)
                    nc.scalar.activation(pt[(h // 4) % 2][:, h % 4, 2 * pair:2 * pair + 2, :], s2p[pair][:],
                                         ACT.Exp).then_inc(exp_done, 1)
                    if pair == 0:
                        if h % 4 == 0:
                            if h >= 8:
                                copy_ctx(seq, h // 4 - 2)
                            elif not first:
                                copy_ctx(prev, h // 4 + 2)
                        if inputs and h == 9:
                            copy_xt(inp, misc_count(seq, "xt"))
                        if inputs and h == 10:
                            copy_q(inp, misc_count(seq, "q"))
                        if inputs and h == 11:
                            copy_k(inp, misc_count(seq, "k"))
                        if h == 13 and not first:
                            copy_rowst(prev, misc_count(seq, "rowst"))
                        if h == 0 and not (seq.known and seq.b < 2):
                            gate_exponent(seq.next(-2))

        slots(slot, act)
        end = Seq(LAST // 2, LAST % 2)
        copy_ctx(end, 2)
        copy_ctx(end, 3)
        gate_exponent(end.next(-1))
        copy_rowst(end, misc_count(end.next(1), "rowst"))
        gate_exponent(end)
        experts_functions(act)

    @block.vector
    def _(dve):
        def layernorm_rows(seq):
            done = [0]

            def link(ins):
                done[0] += 1
                ins.then_inc(ln_chain, 1)
                return dve.wait_ge(ln_chain, LN_STEPS * seq.b + done[0])

            dve.wait_ge(x_in[seq.p], 16 * (seq.i + 1))
            statistics(0, xin[seq.p], link)
            if not (seq.known and seq.b == 0):
                before = seq.next(-1)
                count = 1 if before.known and before.b == 0 else (
                    5 if before.known and before.b == 1 else misc_count(before.next(-2), "xt"))
                dve.wait_ge(misc_full, count)
            for t in range(T):
                ins = nc.vector.tensor_scalar(xn[:, t, :], xin[seq.p][:, t, :], mv[0][:, t, 0:1], ln_y[0][:, t:t + 1],
                                              ALU.subtract, ALU.mult)
            ins.then_inc(xn_set, 1)
            assert done[0] == LN_STEPS

        def statistics(n, src, link):
            for t in range(T):
                ins = nc.vector.bn_stats(stats[n][:, t, :], src[:, t, :])
            link(ins).then_inc(stats_seen, 1)
            for t in range(T):
                ins = nc.vector.bn_aggr(mv[n][:, t, :], stats[n][:, t, :])
            link(ins)
            a, y, yy = ln_a[n], ln_y[n], ln_t[n]
            link(nc.vector.tensor_scalar(a[:], mv[n][:, :, 1], EPS, None, ALU.add))
            link(nc.vector.tensor_scalar(y[:].bitcast(I32), a[:].bitcast(I32), -0.5, RSQRT_SEED, ALU.mult, ALU.add))
            for _ in range(4):
                link(nc.vector.scalar_tensor_tensor(yy[:], y[:], -0.5, y[:], ALU.mult, ALU.mult))
                link(nc.vector.tensor_tensor(yy[:], yy[:], a[:], ALU.mult))
                link(nc.vector.scalar_tensor_tensor(y[:], yy[:], 1.5, y[:], ALU.add, ALU.mult))

        def normalise_x2(seq, count):
            done = [0]

            def link(ins):
                done[0] += 1
                ins.then_inc(ln2_chain, 1)
                return dve.wait_ge(ln2_chain, LN_STEPS * seq.b + done[0])

            dve.wait_ge(misc_free, count)
            statistics(1, x2, link)
            if not (seq.known and seq.b == 0):
                dve.wait_ge(dispatched, 16 * TOPK * T * seq.b)
            for t in range(T):
                nc.vector.tensor_scalar(rows[:, t, 0:D], x2[:, t, :], mv[1][:, t, 0:1], ln_y[1][:, t:t + 1],
                                        ALU.subtract, ALU.mult)
            nc.vector.tensor_scalar(rows[:, :, ID_COL], numbers[:, C_IDS:C_IDS + T], token_base[:], None, ALU.add).then_inc(rows_set, 1)
            dve.wait_ge(rows_set, seq.b + 1)
            nc.vector.tensor_scalar(token_base[:], token_base[:], float(S), None, ALU.add).then_inc(base_set, 1)
            dve.wait_ge(base_set, seq.b + 1)

        GATE_STEPS = 10

        def gate_link(seq):
            done = [0]

            def link(ins):
                done[0] += 1
                ins.then_inc(gate_chain, 1)
                dve.wait_ge(gate_chain, GATE_STEPS * seq.b + done[0])
            return link

        def choose(seq, count):
            link = gate_link(seq)
            dve.wait_ge(misc_full, count)
            nc.vector.tensor_tensor(logits[:], misc[:, 0:T * E].rearrange("p (t e) -> p t e", t=T),
                                    bg[:].rearrange("p (o e) -> p o e", o=1).to_broadcast((P, T, E)), ALU.add).then_inc(misc_free, 1)
            dve.wait_ge(misc_free, count).then_inc(logits_seen, 1)
            for t in range(T):
                ins = nc.vector.max(top[:, t, :], logits[:, t, :])
            link(ins)
            nc.vector.tensor_tensor(gate_d[:], top[:, :, 1], top[:, :, 0], ALU.subtract).then_inc(gate_diff, 1)
            for t in range(T):
                ins = nc.vector.max_index(topi[:, t, :], top[:, t, :], logits[:, t, :])
            link(ins)
            link(nc.vector.tensor_copy(choice[:], topi[:, :, 0:TOPK]))
            link(nc.vector.tensor_tensor(
                chosen[:], choice[:].rearrange("p t (c o) -> p (t c) o", o=1).to_broadcast((P, T * TOPK, E)),
                numbers[:, C_IOTA8:C_IOTA8 + E].rearrange("p (o e) -> p o e", o=1).to_broadcast((P, T * TOPK, E)),
                ALU.is_equal))
            nc.vector.tensor_copy(chosenb[:], chosen[:]).then_inc(chosen_set, 1)

        def weigh_choices(seq):
            dve.wait_ge(gate_exp, seq.b + 1)
            n = GATE_STEPS * seq.b + 4

            def step(k, ins):
                ins.then_inc(gate_chain, 1)
                dve.wait_ge(gate_chain, n + k)

            step(1, nc.vector.tensor_scalar(gate_s[:], gate_e[:], 1.0, None, ALU.add))
            step(2, nc.vector.reciprocal(rows[:, :, W_COL], gate_s[:]))
            step(3, nc.vector.tensor_tensor(rows[:, :, W_COL + 1], rows[:, :, W_COL], gate_e[:], ALU.mult))

        def place_rows(seq, count):
            n = GATE_STEPS * seq.b + 7

            def step(k, ins):
                ins.then_inc(gate_chain, 1)
                dve.wait_ge(gate_chain, n + k)

            over_t = lambda ap: ap.rearrange("p (o r) -> p o r", o=1).to_broadcast((P, T, R2))
            dve.wait_ge(misc_full, count)
            step(1, nc.vector.tensor_tensor(place[:], misc[:, 0:T * R2].rearrange("p (t r) -> p t r", t=T), over_t(counts[:]), ALU.add))
            nc.vector.tensor_tensor(counts[:], counts[:], misc[:, T * R2:(T + 1) * R2], ALU.add).then_inc(misc_free, 1)
            step(2, nc.vector.tensor_tensor(place[:].rearrange("p t (c e) -> p (t c) e", e=E), place[:].rearrange("p t (c e) -> p (t c) e", e=E),
                                            chosen[:], ALU.mult))
            step(3, nc.vector.tensor_reduce(slot_f[:], place[:].rearrange("p t (c e) -> p (t c) e", e=E), AXX, ALU.add))
            if not (seq.known and seq.b == 0):
                dve.wait_ge(dispatched, 16 * TOPK * T * seq.b)
            nc.vector.tensor_copy(slot_i[:], slot_f[:]).then_inc(slots_set, 1)

        def add_v_bias(seq, count):
            dve.wait_ge(misc_full, count)
            if not (seq.known and seq.b < 2):
                dve.wait_ge(pv_done, 16 * (seq.b - 1))
            nc.vector.tensor_tensor(vp[seq.p][:, :, :, 0:HD], misc[:].rearrange("p (t h d) -> p t h d", t=T, h=H),
                                    bv[:].rearrange("p (o h d) -> p o h d", o=1, h=H).to_broadcast((P, T, H, HD)),
                                    ALU.add).then_inc(misc_free, 1)

        def copy_m(half, u, count):
            dve.wait_ge(misc_full, count)
            if not (isinstance(u, int) and u < 2):
                dve.wait_ge(m_parts, u - 1)
            nc.vector.tensor_copy(m32[half][:], misc[0:UH * T, 0:P]).then_inc(misc_free, 1)

        def take_maxima(seq, h):
            half = h // UH
            for t in range(T):
                dve.wait_ge(s1_full, 4 * head_no(seq, h) + t + 1)
                nc.vector.tensor_reduce(negm[half][:, (h % UH) * T + t:(h % UH) * T + t + 1], s1p[t % 2][:], AXX,
                                        ALU.max, negate=True).then_inc(s1_free, 1)

        def invert_sums(seq):
            dve.wait_ge(den_in, 16 * (seq.b + 1))
            if not (seq.known and seq.b == 0):
                dve.wait_ge(rden_out, 16 * seq.b)
            nc.vector.reciprocal(rden[:], den[:]).then_inc(rden_set, 1)

        def add_residual(seq, count):
            dve.wait_ge(misc_full, count)
            dve.wait_ge(xres_set, seq.b + 1)
            if not (seq.known and seq.b == 0):
                dve.wait_ge(x2_out, 16 * seq.b)
            nc.vector.tensor_tensor(x2[:].rearrange("p t d -> p (t d)"), misc[:], xres[:].rearrange("p t d -> p (t d)"),
                                    ALU.add).then_inc(misc_free, 1)

        chain = [0]

        def link(ins):
            chain[0] += 1
            ins.then_inc(bias_chain, 1)
            dve.wait_ge(bias_chain, chain[0])

        nc.vector.memset(token_base[:], 0.0)
        nc.vector.memset(rows[:], 0.0)
        nc.vector.memset(xn[:, 0:DEEP, :], 0.0).then_inc(dummy_set, 1)
        dve.wait_ge(dummy_out, 16)
        layernorm_rows(Seq(0, 0))
        dve.wait_ge(bias_sb, H)
        dve.wait_ge(bias_consts_in, 48)
        delta = bias_rows[0:STEPS, :, 0]
        link(nc.vector.tensor_copy(dparts[:, 0, :], delta))
        link(nc.vector.tensor_tensor(drest[:], delta, dparts[:, 0, :], ALU.subtract))
        link(nc.vector.tensor_copy(dparts[:, 1, :], drest[:]))
        link(nc.vector.tensor_tensor(dparts[:, 2, :], drest[:], dparts[:, 1, :], ALU.subtract))
        link(nc.vector.tensor_scalar(dsel[:], dparts[:, 0, :], stepmask[:, S:S + 1], None, ALU.mult))
        for s in (1, 2):
            link(nc.vector.scalar_tensor_tensor(dsel[:], dparts[:, s, :], stepmask[:, S + s:S + s + 1], dsel[:], ALU.mult, ALU.add))
        for half in range(2):
            if half:
                dve.wait_ge(steps_out, 32)
            for hh in range(UH):
                h = UH * half + hh
                ins = nc.vector.tensor_scalar(steprows[:, hh, :], stepmask[:, 0:S], dsel[:, h:h + 1], None, ALU.mult)
            ins.then_inc(steps_set, 1)
        dve.wait_ge(consts_in, 14 * 16)
        nc.vector.tensor_copy(counts[:], numbers[:, C_BASE:C_BASE + R2])
        add_v_bias(Seq(0, 0), PROLOGUE.index("v0") + 1)
        layernorm_rows(Seq(0, 1))
        dve.wait_ge(toep_in, 48)
        link(nc.vector.tensor_scalar(band2[:], toep2, 1.0 / BIAS_SCALE, None, ALU.mult))
        link(nc.vector.scalar_tensor_tensor(toep2[HALF:P], toep2[HALF:P], 1.0 / BIAS_SCALE, band2[HALF:P], ALU.mult, ALU.subtract))
        link(nc.vector.tensor_scalar(band1[:], toep1, 1.0 / BIAS_SCALE, None, ALU.mult))
        link(nc.vector.memset(band1[0:HALF, :, P:B1W], 0.0))
        nc.vector.tensor_scalar(band2[HALF:P], toep2[HALF:P], LOW_SCALE, None, ALU.mult).then_inc(band_set, 1)
        for h in range(UH):
            take_maxima(Seq(0, 0), h)
        for h in range(UH, LEAD):
            take_maxima(Seq(0, 0), h)
            if h == UH:
                copy_m(0, 0, len(PROLOGUE))

        def slot(seq):
            prev, nxt, inp = seq.next(-1), seq.next(1), seq.next(2)
            first = seq.known and seq.b == 0
            last = seq.known and seq.b == LAST
            inputs = not (seq.known and seq.b + 2 > LAST)
            for h in range(H):
                lead = ahead(seq, h)
                if lead:
                    take_maxima(*lead)
                if h == 5:
                    copy_m(1, unit_no(seq, UH), misc_count(seq, "m_mid"))
                if h == 0 and not (seq.known and seq.b < 2):
                    weigh_choices(seq.next(-2))
                if h == 1 and not (seq.known and seq.b < 2):
                    place_rows(seq.next(-2), misc_count(seq, "rank"))
                if h == 6 and not last:
                    add_v_bias(nxt, misc_count(seq, "v"))
                if h == 6 and inputs:
                    layernorm_rows(inp)
                if h == 7 and not first:
                    invert_sums(prev)
                if h == 11 and not first:
                    add_residual(prev, misc_count(seq, "out"))
                    normalise_x2(prev, misc_count(seq, "out"))
                if h == 13 and not last:
                    copy_m(0, unit_no(nxt, 0), misc_count(seq, "m_end"))
                if h == 15 and not first:
                    choose(prev, misc_count(seq, "gate"))

        slots(slot, dve)
        end = Seq(LAST // 2, LAST % 2)
        weigh_choices(end.next(-1))
        place_rows(end.next(-1), misc_count(end.next(1), "rank_a"))
        invert_sums(end)
        add_residual(end, out_count(end))
        normalise_x2(end, out_count(end))
        choose(end, misc_count(end.next(1), "gate"))
        weigh_choices(end)
        place_rows(end, misc_count(end.next(1), "rank_b"))
        experts_vectors(dve)

    @block.gpsimd
    def _(pool):
        for n in range(2):
            ins = pool.memset(vp[n][:, :, :, HD:32], 1.0)
        ins.then_inc(ones_set, 1)

        def split(seq, k, count, src, parts):
            pool.wait_ge(misc_free, count)
            if not (seq.known and seq.b == 0):
                pool.wait_ge(qk_out[k], 16 * seq.b).then_inc(split_started, 1)
            base = 6 * seq.b + 3 * k
            pool.tensor_copy(parts[:, 0, :], src[:]).then_inc(parts_chain, 1)
            pool.wait_ge(parts_chain, base + 1)
            pool.tensor_tensor(rest[:], src[:], parts[:, 0, :], ALU.subtract).then_inc(parts_chain, 1)
            pool.wait_ge(parts_chain, base + 2).then_inc(split_started, 1)
            pool.tensor_copy(parts[:, 1, :], rest[:]).then_inc(parts_chain, 1)
            pool.wait_ge(parts_chain, base + 3)
            pool.tensor_tensor(parts[:, 2, :], rest[:], parts[:, 1, :], ALU.subtract).then_inc(qk_parts, 1)

        def split_m(seq, half, count):
            pool.wait_ge(misc_free, count)
            if not (seq.known and seq.b == 0):
                pool.wait_ge(m_out[half], 16 * seq.b).then_inc(split_started, 1)
            base = 3 * (2 * seq.b + half)
            pool.tensor_copy(mparts[half][:, 0, :], m32[half][:]).then_inc(m_chain, 1)
            pool.wait_ge(m_chain, base + 1)
            pool.tensor_tensor(mrest[:], m32[half][:], mparts[half][:, 0, :], ALU.subtract).then_inc(m_chain, 1)
            pool.wait_ge(m_chain, base + 2).then_inc(split_started, 1)
            pool.tensor_copy(mparts[half][:, 1, :], mrest[:]).then_inc(m_chain, 1)
            pool.wait_ge(m_chain, base + 3)
            pool.tensor_tensor(mparts[half][:, 2, :], mrest[:], mparts[half][:, 1, :], ALU.subtract).then_inc(m_parts, 1)

        def add_out_bias(seq):
            pool.wait_ge(xres_in, 16 * (seq.b + 1))
            pool.tensor_tensor(xres[:], xres[:], bo[:].rearrange("p (o d) -> p o d", o=1).to_broadcast((P, T, D)),
                               ALU.add).then_inc(xres_set, 1)

        def dispatch(seq):
            pool.wait_ge(slots_set, seq.b + 1).then_inc(dispatch_started, 1)
            for t in range(T):
                for c in range(TOPK):
                    k = TOPK * t + c
                    pool.indirect_dma_start(disp, bass.IndirectOffsetOnAxis(slot_i[:, k:k + 1], 0), rows[:, t, :], None).then_inc(dispatched, 16)

        def normalise(seq):
            pool.wait_ge(norm_in, 32 * (seq.b + 1))
            pool.tensor_tensor(ctxt[:], ctxt[:], rdenb[:], ALU.mult).then_inc(ctxt_set, 1)

        def split_biases():
            nb1 = E * DFF // P
            pool.wait_ge(bcol_in, 32)
            steps = 0
            for src, lo, hi in ((b1col, 0, nb1), (b2col, nb1, (E * DFF + E * D) // P)):
                r = brest[:, 0:hi - lo]
                for n, (o, i0, i1) in enumerate(((bcols[:, 0, lo:hi], src[:], None), (r, src[:], bcols[:, 0, lo:hi]),
                                                 (bcols[:, 1, lo:hi], r, None), (bcols[:, 2, lo:hi], r, bcols[:, 1, lo:hi]))):
                    ins = pool.tensor_copy(o, i0) if i1 is None else pool.tensor_tensor(o, i0, i1, ALU.subtract)
                    ins.then_inc(bcol_chain, 1)
                    steps += 1
                    pool.wait_ge(bcol_chain, steps)
            pool.memset(ones3[:], 1.0).then_inc(bcol_set, 2)

        for n in range(2):
            k = PROLOGUE.index(f"xt{n}") + 1
            split(Seq(0, n), 0, k + 1, q32, qparts)
            split(Seq(0, n), 1, k + 2, k32, kparts)
        split_m(Seq(0, 0), 0, len(PROLOGUE))
        split_biases()
        pool.wait_ge(consts_in, 14 * 16)

        def slot(seq):
            prev, nxt, inp = seq.next(-1), seq.next(1), seq.next(2)
            first = seq.known and seq.b == 0
            last = seq.known and seq.b == LAST
            inputs = not (seq.known and seq.b + 2 > LAST)
            if not (seq.known and seq.b < 2):
                dispatch(seq.next(-2))
            split_m(seq, 1, misc_count(seq, "m_mid"))
            if not first:
                add_out_bias(prev)
                normalise(prev)
            if inputs:
                split(inp, 0, misc_count(seq, "q"), q32, qparts)
                split(inp, 1, misc_count(seq, "k"), k32, kparts)
            if not last:
                split_m(nxt, 0, misc_count(seq, "m_end"))

        slots(slot, pool)
        end = Seq(LAST // 2, LAST % 2)
        dispatch(end.next(-1))
        add_out_bias(end)
        normalise(end)
        dispatch(end)
        experts_scatters(pool)


def buckets():
    d = np.arange(S)
    f = np.maximum(d, 1).astype(np.float32) / np.float32(16)
    large = 16 + (np.log(f) / np.float32(np.log(4.0)) * np.float32(16)).astype(np.int32)
    return np.where(d < 16, d, np.minimum(large, BUCKETS - 1))


def constants(nb):
    bf16 = mybir.dt.np(BF16)
    tokens = nb * S
    region = tokens + P
    tiles = tokens // P + E
    tiles += -tiles % DEEP
    numbers = np.zeros((P, C_IOTA + tiles), np.float32)
    lane = np.arange(P)
    numbers[:, C_IDS:C_IOTA8] = lane[:, None] + P * np.arange(T)
    numbers[:, C_IOTA8:C_SIGN] = np.arange(E)
    numbers[:, C_SIGN:C_BASE] = 1 - 2 * (np.arange(E) % 2)
    numbers[:, C_BASE:C_DUMMY] = region * np.arange(R2)
    numbers[:, C_DUMMY] = R2 * region + lane
    numbers[:, C_PADID] = tokens + lane
    numbers[:, C_IOTA:] = np.arange(tiles)
    order = np.ones((P, 2, P), np.float32)
    order[:, 0, :] = lane[:, None] < lane[None, :]
    bucket = buckets()
    assert bucket[FAR] == BUCKETS - 1 and bucket[FAR - 1] < BUCKETS - 1
    onehot = np.zeros((BUCKETS, S), np.float32)
    for e in range(S):
        d = e - (HALF - 1) if e < FWD else FWD - 1 - (e - FWD)
        onehot[bucket[max(d, 0)], e] += 8.0
        onehot[BUCKETS - 1, e] -= 8.0
    stepmask = np.zeros((STEPS, S + NPARTS), np.float32)
    kstatic = np.zeros((ROWS2 - STACK, S), np.float32)
    for u in range(1, S // HALF):
        for s in range(NPARTS):
            r = NPARTS * (u - 1) + s
            stepmask[r, 0:HALF * u] = 1.0
            stepmask[r, S + s] = 1.0
            kstatic[r, HALF * u:HALF * u + HALF] = 1.0
    kstatic[STEPS:] = 1.0
    pick = np.zeros((3, P, P), np.float16)
    for g in range(2):
        for r in range(HALF):
            pick[g, r, HALF * g + r] = BIAS_SCALE
            pick[g, HALF + r, HALF * g + r] = BIAS_SCALE / LOW_SCALE
    pick[2] = np.eye(P) * BIAS_SCALE
    return {"onehot": onehot, "stepmask": stepmask, "kstatic": kstatic.astype(bf16), "pick": pick,
            "ident": np.eye(P, dtype=np.float32), "numbers": numbers, "order": order.astype(bf16)}


NAMES = {"x": "L0_attn_hidden_states", "wq": "L0_attn_Wq", "bq": "L0_attn_bq", "wk": "L0_attn_Wk", "bk": "L0_attn_bk",
         "wv": "L0_attn_Wv", "bv": "L0_attn_bv", "wo": "L0_attn_Wo", "bo": "L0_attn_bo", "rel": "L0_attn_rel_bias",
         "w1": "L0_ffn_W1", "b1": "L0_ffn_b1", "w2": "L0_ffn_W2", "b2": "L0_ffn_b2", "wg": "L0_ffn_Wg", "bg": "L0_ffn_bg"}


def build(nc, nb, io, out):
    with ExitStack() as ctx:
        layer(nc, ctx, nb, io, out)


def kernel(**inputs):
    import concourse.bacc as bacc
    from concourse.bass_utils import run_bass_kernel_spmd

    nc = bacc.Bacc("TRN2", target_bir_lowering=False, num_devices=1)
    arrays = {name: np.ascontiguousarray(inputs[full]) for name, full in NAMES.items()}
    nb = arrays["x"].shape[0]
    arrays.update(constants(nb))
    io = {name: nc.dram_tensor(f"in_{name}", a.shape, mybir.dt.from_np(a.dtype), kind="ExternalInput").ap()
          for name, a in arrays.items()}
    out = nc.dram_tensor("out_rows", (nb * S + DEEP * P, D), F32, kind="ExternalOutput").ap()
    build(nc, nb, io, out)
    r = run_bass_kernel_spmd(nc, [{f"in_{name}": a for name, a in arrays.items()}], core_ids=[0])
    return r.results[0]["out_rows"][0:nb * S].reshape(nb, S, D)
```

```python
from contextlib import ExitStack

import numpy as np

import concourse.bass as bass
from concourse import mybir
from concourse.alu_op_type import AluOpType as ALU

F32 = mybir.dt.float32
BF16 = mybir.dt.bfloat16
F16 = mybir.dt.float16
I32 = mybir.dt.int32
U32 = mybir.dt.uint32
ACT = mybir.ActivationFunctionType
AXX = mybir.AxisListType.X

P = 128
S = 512
D = 128
H = 16
HD = D // H
T = S // P
BUCKETS = 32
FAR = 59
HALF = 64
NPARTS = 3
STACK = NPARTS * NPARTS * HD
STEPS = (S // HALF - 1) * NPARTS
ROWS1 = STACK + STEPS
ROWS2 = ROWS1 + NPARTS
UH = 8
BW = 2 * HALF - 6
B1W = P + HALF
FWD = 192
BIAS_SCALE = 16.0
LOW_SCALE = 2048.0
LEAD = 12
EPS = 1e-5
RSQRT_SEED = 1597463007.0
NEWTON = 3
LN_STEPS = 4 + 3 * NEWTON

E = 8
TOPK = 2
DFF = 512
FT = DFF // P
TILE = 2 * P
TJ = TILE // P
ROW = D + 4
ID_COL, W_COL = D, D + 1
C_IDS = 0
C_IOTA8 = C_IDS + T
C_SIGN = C_IOTA8 + E
C_BASE = C_SIGN + E
C_PADID = C_BASE + E
C_IOTA = C_PADID + TJ
DEEP = 4


class Seq:

    def __init__(self, i, p):
        self.i, self.p, self.b = i, p, 2 * i + p

    def next(self, k):
        return Seq(self.i + (self.p + k) // 2, (self.p + k) % 2)

    @property
    def known(self):
        return isinstance(self.b, int)


def layer(nc, ctx, nb, io, out):
    sb = lambda name, shape, dt: ctx.enter_context(nc.sbuf_tensor(name, shape, dt))
    pb = lambda name, shape, dt: ctx.enter_context(nc.psum_tensor(name, shape, dt))
    sem = lambda name: ctx.enter_context(nc.semaphore(name))
    dram = lambda name, shape, dt: nc.dram_tensor(name, shape, dt, kind="Internal").ap()

    tokens = nb * S
    region = tokens + TILE
    ntiles = TOPK * tokens // TILE + E - 1
    ntiles += -ntiles % DEEP
    numbers_w = C_IOTA + ntiles

    wq = sb("wq", [P, D], F32)
    wk = sb("wk", [P, D], F32)
    wv = sb("wv", [P, D], F32)
    wo = sb("wo", [P, D], F32)
    bq = sb("bq", [P, 1], F32)
    bqs = sb("bqs", [P, 1], F32)
    bk = sb("bk", [P, 1], F32)
    bv = sb("bv", [P, D], F32)
    bo = sb("bo", [P, D], F32)
    ident = sb("ident", [P, P], F32)
    pick = sb("pick", [P, 3, P], F16)
    rel = sb("rel", [BUCKETS, H], F32)
    stacks = sb("stacks", [P, 4, 2, UH, S], BF16)
    qst = [stacks[0:ROWS2, n, 0] for n in range(4)]
    kst = [stacks[0:ROWS2, n, 1] for n in range(4)]
    pt = [sb(f"pt{n}", [P, 4, T, S], F32) for n in range(2)]
    vp = [sb(f"vp{n}", [P, T, H, 32], F32) for n in range(2)]
    band2 = sb("band2", [P, H, BW], F16)
    band1 = sb("band1", [P, H, B1W], F16)
    xin = [sb(f"xin{n}", [P, T, D], F32) for n in range(2)]
    xres = sb("xres", [P, T, D], F32)
    x2 = sb("x2", [P, T, D], F32)
    xn = sb("xn", [P, T, D], F32)
    xnt = [sb(f"xnt{n}", [P, S], F32) for n in range(2)]
    q32 = sb("q32", [P, S], F32)
    k32 = sb("k32", [P, S], F32)
    rest = sb("rest", [P, S], F32)
    qparts = sb("qparts", [P, NPARTS, S], BF16)
    kparts = sb("kparts", [P, NPARTS, S], BF16)
    ctxu = [sb(f"ctxu{n}", [P, S], F32) for n in range(2)]
    ctxt = sb("ctxt", [P, S], F32)
    den = sb("den", [P, S // HD], F32)
    rden = sb("rden", [P, S // HD], F32)
    rdenb = sb("rdenb", [P, S], F32)
    stats, mv, ln_a, ln_y, ln_t = (
        [sb(f"{name}{n}", shape, F32) for n in range(2)]
        for name, shape in (("stats", [P, T, 6]), ("mv", [P, T, 2]), ("ln_a", [P, T]), ("ln_y", [P, T]), ("ln_t", [P, T])))
    negm = [sb(f"negm{n}", [P, UH * T], F32) for n in range(2)]
    mrest = sb("mrest", [UH * T, P], F32)
    mparts = [sb(f"mparts{n}", [UH * T, NPARTS, P], BF16) for n in range(2)]
    delta = sb("delta", [STEPS, H], F32)
    dparts = sb("dparts", [STEPS, NPARTS, H], BF16)
    drest = sb("drest", [STEPS, H], F32)
    dsel = sb("dsel", [STEPS, H], F32)

    wg = sb("wg", [P, E], F32)
    bg = sb("bg", [P, E], F32)
    numbers = sb("numbers", [P, numbers_w], F32)
    order = sb("order", [P, 2, P], BF16)
    rows = sb("rows", [P, T, TOPK, ROW], F32)
    padrows = sb("padrows", [P, TJ, ROW], F32)
    rowst = sb("rowst", [P, S], F32)
    logits = sb("logits", [P, T, E], F32)
    top = sb("top", [P, T, E], F32)
    topi = sb("topi", [P, T, E], U32)
    choice = sb("choice", [P, T, TOPK], F32)
    chosen = sb("chosen", [P, T * TOPK, E], F32)
    picked = sb("picked", [P, T * TOPK, E], F32)
    chosenb = sb("chosenb", [P, T, E], BF16)
    gate_d = sb("gate_d", [P, T], F32)
    gate_e = sb("gate_e", [P, T], F32)
    gate_s = sb("gate_s", [P, T], F32)
    token_base = sb("token_base", [P, 1], F32)
    counts = sb("counts", [P, E], F32)
    place = sb("place", [P, T, E], F32)
    slot_f = sb("slot_f", [P, T * TOPK], F32)
    slot_i = sb("slot_i", [P, T * TOPK], U32)
    b1col = sb("b1col", [P, E * DFF // P], F32)
    b2col = sb("b2col", [P, E * D // P], F32)
    bcols = sb("bcols", [P, NPARTS, (E * DFF + E * D) // P], BF16)
    brest = sb("brest", [P, E * DFF // P], F32)
    ones3 = sb("ones3", [NPARTS, TILE], BF16)

    w1 = stacks[:, 0].rearrange("p k h s -> p (k h s)").bitcast(F32)
    w2 = stacks[:, 1].rearrange("p k h s -> p (k h s)").bitcast(F32)
    tab_row = q32[:, 0:ntiles].bitcast(I32)
    tab_off = q32[:, ntiles:2 * ntiles].bitcast(I32)
    tab_gelu = q32[:, 2 * ntiles:3 * ntiles]
    tab_silu = k32[:, 0:ntiles]
    tab_half = k32[:, ntiles:2 * ntiles]
    tab_pad = k32[:, 2 * ntiles:2 * ntiles + E].bitcast(I32)

    s1p = [pb(f"s1p{n}", [P, S], F32) for n in range(2)]
    s2p = [pb(f"s2p{n}", [P, 2, S], F32) for n in range(2)]
    pvp = pb("pvp", [P, S], F32)
    misc = pb("misc", [P, S], F32)

    bias_scr = dram("bias_scr", (H, S), F32)
    qk_scr = [dram(f"qk_scr{n}", (2, NPARTS, P, S), BF16) for n in range(2)]
    ctx_scr = [dram(f"ctx_scr{n}", (4, P, S), F32) for n in range(2)]
    m_scr = [dram(f"m_scr{n}", (NPARTS, UH * T, P), BF16) for n in range(2)]
    disp = dram("disp", (E * region + TILE, ROW), F32)
    b_scr = dram("b_scr", (NPARTS, E * DFF + E * D), BF16)
    rden_scr = [dram(f"rden_scr{n}", (P, S // HD), F32) for n in range(2)]

    flat0 = pt[0][:].rearrange("p a t s -> p (a t s)")
    bias_rows = pt[1][0:H, 0, 0, :]
    toep2 = flat0[:, 0:H * BW].rearrange("p (h w) -> p h w", h=H)
    at = H * BW
    toep1 = flat0[:, at:at + H * B1W].rearrange("p (h w) -> p h w", h=H)
    at += H * B1W
    steprows = flat0[0:STEPS, at:at + UH * S // 2].bitcast(BF16).rearrange("p (h s) -> p h s", h=UH)
    at += UH * S // 2
    stepmask = flat0[0:STEPS, at:at + S + NPARTS]
    at += S + NPARTS
    onehot = flat0[0:BUCKETS, at:at + S]

    spare = [pt[n][:].rearrange("p a t s -> p (a t s)") for n in range(2)]
    cut = lambda n, at, width: spare[n][:, at:at + width]
    per_expert = tokens // TILE
    few = cut(0, 0, E * per_expert).rearrange("p (e n) -> p e n", e=E)
    before = cut(0, 1024, ntiles * E).rearrange("p (n e) -> p n e", e=E)
    weighed = cut(0, 2048, ntiles * E).rearrange("p (n e) -> p n e", e=E)
    tcount = cut(0, 3072, E)
    tsum = cut(0, 3088, E)
    cnt = cut(0, 3104, E)
    one8 = cut(0, 3120, E)
    tab_e = cut(0, 3136, ntiles)
    tab_t = cut(0, 3264, ntiles)
    tab_r = cut(0, 3392, ntiles)
    gelu = [cut(1, 4 * TILE * n, 4 * TILE).rearrange("p (f n) -> p f n", f=FT) for n in range(2)]
    tanh = [cut(1, 4 * TILE * (2 + n), 4 * TILE).rearrange("p (f n) -> p f n", f=FT) for n in range(2)]
    acts = [cut(1, 4 * TILE * (4 + n), 4 * TILE).rearrange("p (f n) -> p f n", f=FT) for n in range(2)]
    xg = [cut(1, 6144 + TJ * ROW * n, TJ * ROW).rearrange("p (j r) -> p j r", j=TJ) for n in range(DEEP)]
    xgt = [cut(1, 7200 + TILE * n, TILE) for n in range(2)]
    w1t = [buf[:].rearrange("p t d -> p (t d)") for buf in xin] + [buf[:] for buf in xnt]
    yw = [cut(0, 6912 + TJ * D * n, TJ * D).rearrange("p (j d) -> p j d", j=TJ) for n in range(2)]
    b1t = [cut(0, 3520 + DFF // 2 * n, DFF // 2)[0:NPARTS].bitcast(BF16) for n in range(DEEP)]
    ids = [cut(0, 7936 + 4 * n, TJ).bitcast(U32) for n in range(DEEP)]
    wts = [cut(0, 7952 + 4 * n, TJ) for n in range(DEEP)]
    b1rows = vp[0][0:NPARTS].rearrange("s t h c -> s (t h c)").bitcast(BF16)
    b2rows = spare[0][0:NPARTS, 4864:4864 + E * DFF // 2].bitcast(BF16)
    hp = [s2p[n][:].rearrange("p b (f n) -> p (b f) n", n=TILE) for n in range(2)]
    xgtp = [s1p[n][:, 0:TILE] for n in range(2)]
    yp = [pvp[:, 0:TJ * D].rearrange("p (j d) -> p j d", j=TJ), misc[:, 0:TJ * D].rearrange("p (j d) -> p j d", j=TJ)]

    bias_consts_in = sem("bias_consts_in")
    consts_in = sem("consts_in")
    ones_set = sem("ones_set")
    bias_ps = sem("bias_ps")
    proj_in = sem("proj_in")
    band1_set = sem("band1_set")
    band2_chain = sem("band2_chain")
    bias_sb = sem("bias_sb")
    bias_out = sem("bias_out")
    toep_in = sem("toep_in")
    bias_chain = sem("bias_chain")
    steps_set = sem("steps_set")
    steps_out = [sem(f"steps_out{n}") for n in range(2)]
    static_in = [sem(f"static_in{n}") for n in range(2)]
    late_consts_in = sem("late_consts_in")
    band_set = sem("band_set")
    bqs_set = sem("bqs_set")
    x_in = [sem(f"x_in{n}") for n in range(2)]
    ln_chain = sem("ln_chain")
    xn_set = sem("xn_set")
    misc_full = sem("misc_full")
    misc_free = sem("misc_free")
    parts_chain = sem("parts_chain")
    qk_parts = sem("qk_parts")
    qk_out = [sem(f"qk_out{n}") for n in range(2)]
    stack_in = [sem(f"stack_in{n}") for n in range(4)]
    s1_full = sem("s1_full")
    s1_free = sem("s1_free")
    m_parts = sem("m_parts")
    m_chain = sem("m_chain")
    m_out = [sem(f"m_out{n}") for n in range(2)]
    m_in = [sem(f"m_in{n}") for n in range(4)]
    s2_full = sem("s2_full")
    exp_done = sem("exp_done")
    pv_done = sem("pv_done")
    ctx_copied = sem("ctx_copied")
    ctx_out = [sem(f"ctx_out{n}") for n in range(2)]
    den_in = sem("den_in")
    rden_set = sem("rden_set")
    rden_out = sem("rden_out")
    norm_in = sem("norm_in")
    ctxt_set = sem("ctxt_set")
    xres_in = sem("xres_in")
    xres_set = sem("xres_set")
    x2_out = sem("x2_out")
    ln2_chain = sem("ln2_chain")
    rows_set = sem("rows_set")
    gate_chain = sem("gate_chain")
    gate_diff = sem("gate_diff")
    gate_exp = sem("gate_exp")
    chosen_set = sem("chosen_set")
    slots_set = sem("slots_set")
    dispatched = sem("dispatched")
    bcol_in = sem("bcol_in")
    bcol_chain = sem("bcol_chain")
    bcol_set = sem("bcol_set")
    bcol_out = sem("bcol_out")
    brow_in = sem("brow_in")
    dummy_set = sem("dummy_set")
    base_set = sem("base_set")
    w_in = sem("w_in")
    table_chain = sem("table_chain")
    pads_set = sem("pads_set")
    padded = sem("padded")
    tables_set = sem("tables_set")
    xg_in = [sem(f"xg_in{n}") for n in range(DEEP)]
    meta_set = sem("meta_set")
    xgt_full = sem("xgt_full")
    xgt_set = sem("xgt_set")
    h_full = sem("h_full")
    functions_set = sem("functions_set")
    silu_set = sem("silu_set")
    acts_set = sem("acts_set")
    y_full = sem("y_full")
    y_set = sem("y_set")
    y_out = sem("y_out")
    w1_in = [sem(f"w1_in{n}") for n in range(DEEP)]
    rows_doubled = sem("rows_doubled")
    dummy_out = sem("dummy_out")
    dispatch_started = sem("dispatch_started")
    stats_seen = sem("stats_seen")
    logits_seen = sem("logits_seen")
    split_started = sem("split_started")
    add_started = sem("add_started")
    double_started = sem("double_started")

    LAST = nb - 1

    PROLOGUE = ["xt0", "q0", "k0", "v0", "xt1", "q1", "k1", "m0"]
    SLOT = ["gate", "rank", "m_mid", "v", "xt", "q", "k", "out", "m_end", "rowst"]
    TAIL = ["gate_a", "rank_a", "out", "rowst", "gate_b", "rank_b"]

    def slot_jobs(b):
        jobs = list(SLOT)
        if b == 0:
            jobs = [j for j in jobs if j not in ("out", "rowst")]
        if b < 2:
            jobs = [j for j in jobs if j not in ("gate", "rank")]
        if b + 2 > LAST:
            jobs = [j for j in jobs if j not in ("xt", "q", "k")]
        if b == LAST:
            jobs = [j for j in jobs if j not in ("v", "m_end")]
        return jobs

    def misc_count(seq, job):
        if not seq.known:
            return len(PROLOGUE) + len(slot_jobs(0)) + len(slot_jobs(1)) + len(SLOT) * (seq.b - 2) + SLOT.index(job) + 1
        before = len(PROLOGUE) + sum(len(slot_jobs(b)) for b in range(min(seq.b, nb)))
        return before + (TAIL if seq.b > LAST else slot_jobs(seq.b)).index(job) + 1

    def out_count(seq):
        return misc_count(seq.next(1), "out")

    def head_no(seq, h):
        return H * seq.b + h

    def slots(emit, eng):
        emit(Seq(0, 0))
        emit(Seq(0, 1))
        if nb > 4:
            with eng.Fori(1, nb // 2 - 1) as i:
                emit(Seq(i, 0))
                emit(Seq(i, 1))
        emit(Seq(nb // 2 - 1, 0))
        emit(Seq(nb // 2 - 1, 1))

    def ahead(seq, h):
        g = h + LEAD
        s = seq.next(g // H)
        return None if s.known and s.b > LAST else (s, g % H)

    def unit_buf(seq, h):
        return 2 * seq.p + h // UH

    def unit_no(seq, h):
        return 2 * seq.b + h // UH

    turns = ntiles // DEEP

    def tile_loop(emit, eng):
        emit(0)
        with eng.Fori(1, turns - 1) as m:
            emit(m)
        emit(turns - 1)

    def at_least(eng, sem_, value, from_):
        if not isinstance(from_, int) or from_ >= 0:
            eng.wait_ge(sem_, value)

    by_tile = lambda ap: ap.rearrange("(j p) r -> p j r", p=P)

    def experts_loads(sp):
        sp.wait_ge(pv_done, 4 * T * nb)
        sp.dma_start(b2rows.rearrange("s (e f) -> s e f", e=E)[:, :, 0:D], b_scr[:, E * DFF:].rearrange("s (e d) -> s e d", e=E)).then_inc(brow_in, 16)
        sp.wait_ge(pads_set, 2)
        for e in range(E):
            row = sp.value_load(tab_pad[0:1, e:e + 1], min_val=0, max_val=E * region)
            sp.dma_start(by_tile(disp[bass.ds(row, TILE)]), padrows[:]).then_inc(padded, 16)
        sp.wait_ge(brow_in, 32)
        sp.wait_ge(w_in, 32)
        sp.wait_ge(tables_set, 1)
        sp.wait_ge(padded, 16 * (E + 1))
        sp.wait_ge(dispatched, 16 * TOPK * T * nb)

        def load_tile(n, k):
            row = sp.value_load(tab_row[0:1, bass.ds(n, 1)], min_val=0, max_val=E * region)
            at_least(sp, xgt_full, n - DEEP + 1, n - DEEP)
            at_least(sp, meta_set, n - DEEP + 1, n - DEEP)
            sp.dma_start(xg[k], by_tile(disp[bass.ds(row, TILE)])).then_inc(xg_in[k], 16)

        def load_w1(n, k):
            off = sp.value_load(tab_off[0:1, bass.ds(n, 1)], min_val=0, max_val=(E - 1) * DFF)
            at_least(sp, h_full, n - DEEP + 1, n - DEEP)
            sp.dma_start(w1t[k], w1[:, bass.ds(off, DFF)]).then_inc(w1_in[k], 16)
            sp.dma_start(b1t[k], b1rows[:, bass.ds(off, DFF)]).then_inc(w1_in[k], 16)

        for n in range(DEEP):
            load_tile(n, n)
            if n < 3:
                load_w1(n, n)

        def turn(m):
            for k in range(DEEP):
                n = DEEP * m + k
                left = ntiles - n if isinstance(n, int) else DEEP
                if left > DEEP or not isinstance(n, int):
                    load_tile(n + DEEP, k)
                if left > 3:
                    load_w1(n + 3, (k + 3) % DEEP)

        tile_loop(turn, sp)
        sp.wait_ge(y_out, 32 * ntiles)

    def experts_products(pe):
        pe.wait_ge(w_in, 32)
        pe.wait_ge(brow_in, 32)
        pe.wait_ge(bcol_set, 2)
        pe.wait_ge(tables_set, 1)

        def transpose_rows(n, k, m):
            pe.wait_ge(xg_in[k], 16 * (m + 1))
            at_least(pe, xgt_set, n - 1, n - 2)
            for j in range(TJ):
                mm = nc.tensor.transpose(xgtp[k % 2][:, P * j:P * j + P], xg[k][:, j, 0:D], ident[:])
            mm.then_inc(xgt_full, 1)

        def hidden(n, k, m):
            pe.wait_ge(w1_in[k], 32 * (m + 1))
            pe.wait_ge(xgt_set, n + 1)
            at_least(pe, silu_set, n - 1, n - 2)
            for f in range(FT):
                nc.tensor.matmul(hp[k % 2][:, f, :], w1t[k][:, P * f:P * f + P], xgt[k % 2], start=True, stop=False)
                mm = nc.tensor.matmul(hp[k % 2][:, f, :], b1t[k][:, P * f:P * f + P], ones3[:], start=False, stop=True)
            mm.then_inc(h_full, 1)

        def back(n, k):
            off = pe.value_load(tab_off[0:1, bass.ds(n, 1)], min_val=0, max_val=(E - 1) * DFF)
            pe.wait_ge(acts_set, n + 1)
            at_least(pe, y_set, n - 1, n - 2)
            for j in range(TJ):
                for f in range(FT):
                    nc.tensor.matmul(yp[k % 2][:, j, :], acts[k % 2][:, f, P * j:P * j + P], w2[:, bass.ds(off + P * f, D)],
                                     start=(f == 0), stop=False)
                mm = nc.tensor.matmul(yp[k % 2][:, j, :], ones3[:, 0:P], b2rows[:, bass.ds(off, D)], start=False, stop=True)
            mm.then_inc(y_full, 1)

        for n in range(2):
            transpose_rows(n, n, 0)
        hidden(0, 0, 0)
        transpose_rows(2, 2, 0)
        hidden(1, 1, 0)

        def turn(m):
            for k in range(DEEP):
                n = DEEP * m + k
                left = ntiles - n if isinstance(n, int) else DEEP
                if left > 3:
                    transpose_rows(n + 3, (k + 3) % DEEP, m + (k + 3) // DEEP)
                if left > 2:
                    hidden(n + 2, (k + 2) % DEEP, m + (k + 2) // DEEP)
                back(n, k)

        tile_loop(turn, pe)

    def experts_functions(act):
        act.wait_ge(tables_set, 1)

        def copy_rows(n, k):
            act.wait_ge(xgt_full, n + 1)
            at_least(act, h_full, n - 1, n - 2)
            nc.scalar.copy(xgt[k % 2], xgtp[k % 2]).then_inc(xgt_set, 1)

        def functions(n, k):
            act.wait_ge(h_full, n + 1)
            at_least(act, acts_set, n - 1, n - 2)
            nc.scalar.activation(gelu[k % 2], hp[k % 2], ACT.Gelu, scale=tab_gelu[:, bass.ds(n, 1)])
            nc.scalar.activation(tanh[k % 2], hp[k % 2], ACT.Tanh, scale=tab_half[:, bass.ds(n, 1)]).then_inc(functions_set, 1)

        for n in range(2):
            copy_rows(n, n)
        functions(0, 0)
        copy_rows(2, 2)
        functions(1, 1)

        def turn(m):
            for k in range(DEEP):
                n = DEEP * m + k
                left = ntiles - n if isinstance(n, int) else DEEP
                if left > 3:
                    copy_rows(n + 3, (k + 3) % DEEP)
                if left > 2:
                    functions(n + 2, (k + 2) % DEEP)

        tile_loop(turn, act)

    def chain_on(eng, sem_, before):
        done = [0]

        def link(ins):
            done[0] += 1
            ins.then_inc(sem_, 1)
            return eng.wait_ge(sem_, before + done[0])
        return link

    def split(eng, seq, k, count, src, parts):
        eng.wait_ge(misc_free, count)
        if not (seq.known and seq.b == 0):
            eng.wait_ge(qk_out[k], 16 * seq.b).then_inc(split_started, 1)
        base = 6 * seq.b + 3 * k
        eng.tensor_copy(parts[:, 0, :], src[:]).then_inc(parts_chain, 1)
        eng.wait_ge(parts_chain, base + 1)
        eng.tensor_tensor(rest[:], src[:], parts[:, 0, :], ALU.subtract).then_inc(parts_chain, 1)
        eng.wait_ge(parts_chain, base + 2).then_inc(split_started, 1)
        eng.tensor_copy(parts[:, 1, :], rest[:]).then_inc(parts_chain, 1)
        eng.wait_ge(parts_chain, base + 3)
        eng.tensor_tensor(parts[:, 2, :], rest[:], parts[:, 1, :], ALU.subtract).then_inc(qk_parts, 1)

    def experts_vectors(dve):
        link = chain_on(dve, table_chain, 0)

        link(nc.vector.tensor_copy(tab_pad, counts[:])).then_inc(pads_set, 1)
        link(nc.vector.tensor_tensor(cnt, counts[:], numbers[:, C_BASE:C_BASE + E], ALU.subtract))
        link(nc.vector.tensor_scalar(cnt, cnt, 1.0 / TILE, None, ALU.mult))
        wide = (P, E, per_expert)
        link(nc.vector.tensor_tensor(few, numbers[:, C_IOTA:C_IOTA + per_expert].rearrange("p (o n) -> p o n", o=1).to_broadcast(wide),
                                     cnt.rearrange("p (e o) -> p e o", o=1).to_broadcast(wide), ALU.is_lt))
        link(nc.vector.tensor_reduce(tcount, few, AXX, ALU.add))
        link(nc.vector.memset(one8, 1.0))
        link(nc.vector.tensor_tensor_scan(tsum, one8, tcount, 0.0, ALU.mult, ALU.add))
        wide = (P, ntiles, E)
        iota = numbers[:, C_IOTA:C_IOTA + ntiles]
        per_e = lambda ap: ap.rearrange("p (o e) -> p o e", o=1).to_broadcast(wide)
        link(nc.vector.tensor_tensor(before, per_e(tsum), iota.rearrange("p (n o) -> p n o", o=1).to_broadcast(wide), ALU.is_le))
        link(nc.vector.tensor_tensor(weighed, before, per_e(tcount), ALU.mult))
        link(nc.vector.tensor_reduce(tab_t, weighed[:, :, 0:E - 1], AXX, ALU.add))
        link(nc.vector.tensor_tensor(tab_t, iota, tab_t, ALU.subtract))
        link(nc.vector.tensor_scalar(tab_t, tab_t, float(TILE), None, ALU.mult))
        link(nc.vector.tensor_tensor(weighed, before, per_e(numbers[:, C_SIGN:C_SIGN + E]), ALU.mult))
        link(nc.vector.tensor_reduce(tab_e, before[:, :, 0:E - 1], AXX, ALU.add))
        link(nc.vector.tensor_scalar(tab_off, tab_e, float(DFF), None, ALU.mult))
        link(nc.vector.tensor_reduce(tab_silu, weighed[:, :, 0:E - 1], AXX, ALU.add))
        link(nc.vector.tensor_scalar(tab_gelu, tab_silu, -1.0, 1.0, ALU.mult, ALU.add))
        link(nc.vector.tensor_scalar(tab_half, tab_silu, 0.5, None, ALU.mult))
        link(nc.vector.scalar_tensor_tensor(tab_r, tab_e, float(region), tab_t, ALU.mult, ALU.add))
        link(nc.vector.tensor_scalar(tab_t, tab_r, -1.0, float(E * region), ALU.mult, ALU.add))
        link(nc.vector.tensor_tensor(tab_t, tab_t, before[:, :, E - 1], ALU.mult))
        nc.vector.tensor_tensor(tab_row, tab_r, tab_t, ALU.add).then_inc(tables_set, 1)

        def take_numbers(n, k, m):
            dve.wait_ge(xg_in[k], 16 * (m + 1))
            at_least(dve, y_out, 32 * (n - DEEP + 1), n - DEEP)
            nc.vector.tensor_copy(ids[k], xg[k][:, :, ID_COL])
            nc.vector.tensor_copy(wts[k], xg[k][:, :, W_COL]).then_inc(meta_set, 1)

        def activations(n, k):
            dve.wait_ge(functions_set, n + 1)
            nc.vector.scalar_tensor_tensor(tanh[k % 2], tanh[k % 2], tab_silu[:, bass.ds(n, 1)], hp[k % 2], ALU.add, ALU.mult).then_inc(silu_set, 1)
            dve.wait_ge(silu_set, n + 1)
            at_least(dve, y_full, n - 1, n - 2)
            nc.vector.scalar_tensor_tensor(acts[k % 2], tanh[k % 2], 0.5, gelu[k % 2], ALU.mult, ALU.add).then_inc(acts_set, 1)

        def weigh(n, k):
            dve.wait_ge(y_full, n + 1)
            at_least(dve, y_out, 32 * (n - 1), n - 2)
            for j in range(TJ):
                ins = nc.vector.tensor_scalar(yw[k % 2][:, j, :], yp[k % 2][:, j, :], wts[k][:, j:j + 1], None, ALU.mult)
            ins.then_inc(y_set, 1)

        dve.wait_ge(tables_set, 1)
        for n in range(2):
            take_numbers(n, n, 0)
        activations(0, 0)

        def turn(m):
            for k in range(DEEP):
                n = DEEP * m + k
                left = ntiles - n if isinstance(n, int) else DEEP
                if left > 1:
                    activations(n + 1, (k + 1) % DEEP)
                weigh(n, k)
                if left > 2:
                    take_numbers(n + 2, (k + 2) % DEEP, m + (k + 2) // DEEP)

        tile_loop(turn, dve)

    def experts_scatters(pool):
        pool.wait_ge(x2_out, 16 * nb)
        pool.wait_ge(dummy_out, 16)

        def turn(m):
            for k in range(DEEP):
                n = DEEP * m + k
                at_least(pool, y_out, 32 * n, n - 1)
                pool.wait_ge(y_set, n + 1).then_inc(add_started, 1)
                for j in range(TJ):
                    pool.indirect_dma_start(out, bass.IndirectOffsetOnAxis(ids[k][:, j:j + 1], 0), yw[k % 2][:, j, :], None, compute_op=ALU.add).then_inc(y_out, 16)

        tile_loop(turn, pool)

    block = ctx.enter_context(nc.Block())

    @block.sync
    def _(sp):
        for dst, src in ((rel[:], io["rel"]), (onehot, io["onehot"]), (stepmask, io["stepmask"])):
            sp.dma_start(dst, src).then_inc(bias_consts_in, 16)

        def load_x(seq):
            if not (seq.known and seq.b < 2):
                sp.wait_ge(xn_set, seq.b - 1)
            sp.dma_start(xin[seq.p][:], io["x"][bass.ds(seq.b, 1)].rearrange("o (t p) d -> p (o t) d", p=P)).then_inc(x_in[seq.p], 16)

        def store_parts(seq):
            sp.wait_ge(qk_parts, 2 * seq.b + 1)
            sp.dma_start(qk_scr[seq.p][0].rearrange("i p s -> p i s"), qparts[:]).then_inc(qk_out[0], 16)
            sp.wait_ge(qk_parts, 2 * seq.b + 2)
            sp.dma_start(qk_scr[seq.p][1].rearrange("i p s -> p i s"), kparts[:]).then_inc(qk_out[1], 16)

        def load_stack(seq, half):
            buf = 2 * seq.p + half
            if not (seq.known and seq.b < 2):
                sp.wait_ge(s2_full, 2 * (H * (seq.b - 2) + UH * (half + 1)))
            for k in range(2):
                sp.wait_ge(qk_out[k], 16 * (seq.b + 1))
            for i in range(NPARTS):
                for j in range(NPARTS):
                    r = HD * (NPARTS * i + j)
                    for dst, which, part in ((qst, 0, i), (kst, 1, j)):
                        src = qk_scr[seq.p][which, part].rearrange("(h d) s -> d h s", d=HD)
                        sp.dma_start(dst[buf][r:r + HD], src[:, UH * half:UH * half + UH, :]).then_inc(stack_in[buf], 16)

        def store_ctx(seq, g):
            sp.wait_ge(ctx_copied, 4 * seq.b + g + 1)
            sp.dma_start(ctx_scr[seq.p][g], ctxu[g % 2][:]).then_inc(ctx_out[g % 2], 16)

        load_x(Seq(0, 0))
        load_x(Seq(0, 1))
        static_rows = io["kstatic"].rearrange("r (o s) -> r o s", o=1).to_broadcast((ROWS2 - STACK, UH, S))
        sp.wait_ge(dummy_set, 1)
        sp.dma_start(by_tile(out[tokens:]), padrows[:, :, 0:D]).then_inc(dummy_out, 16)
        for dst, src in ((ident[:], io["ident"]), (wq[:], io["wq"]), (wk[:], io["wk"]),
                         (bq[:], io["bq"].rearrange("(p o) -> p o", o=1)), (bk[:], io["bk"].rearrange("(p o) -> p o", o=1))):
            sp.dma_start(dst, src).then_inc(proj_in, 16)
        sp.wait_ge(bias_sb, 1)
        sp.dma_start(bias_scr, bias_rows).then_inc(bias_out, 16)
        for dst, src in ((wv[:], io["wv"]), (bv[:], io["bv"].rearrange("(o d) -> o d", o=1).to_broadcast((P, D))),
                         (pick[:], io["pick"].rearrange("k p n -> p k n")), (numbers[:], io["numbers"])):
            sp.dma_start(dst, src).then_inc(consts_in, 16)
        sp.wait_ge(bias_out, 16)
        sp.dma_start(toep1, bass.AP(bias_scr.tensor, FWD, [[1, P], [S, H], [1, B1W]])).then_inc(toep_in, 16)
        for lo in (0, HALF):
            sp.dma_start(toep2[lo:lo + HALF], bass.AP(bias_scr.tensor, 0, [[1, HALF], [S, H], [1, BW]])).then_inc(toep_in, 16)
        for half in range(2):
            sp.wait_ge(steps_set, half + 1)
            for buf in (half, half + 2):
                sp.dma_start(qst[buf][STACK:ROWS1], steprows).then_inc(steps_out[half], 16)
            if half == 0:
                sp.dma_start(kst[0][STACK:ROWS2], static_rows).then_inc(static_in[0], 16)
                store_parts(Seq(0, 0))
                load_stack(Seq(0, 0), 0)
        for buf in range(1, 4):
            sp.dma_start(kst[buf][STACK:ROWS2], static_rows).then_inc(static_in[1], 16)
        load_stack(Seq(0, 0), 1)
        for dst, src in ((wg[:], io["wg"]), (order[:], io["order"]), (wo[:], io["wo"]),
                         (bg[:], io["bg"].rearrange("(o e) -> o e", o=1).to_broadcast((P, E))),
                         (bo[:], io["bo"].rearrange("(o d) -> o d", o=1).to_broadcast((P, D)))):
            sp.dma_start(dst, src).then_inc(late_consts_in, 16)
        sp.wait_ge(pads_set, 1)
        sp.dma_start(by_tile(disp[E * region:]), padrows[:]).then_inc(padded, 16)
        sp.dma_start(b1col[:], io["b1"].rearrange("e (a f) -> (e a) f", a=P // E)).then_inc(bcol_in, 16)
        sp.dma_start(b2col[:], io["b2"].rearrange("e (a d) -> (e a) d", a=P // E)).then_inc(bcol_in, 16)
        store_parts(Seq(0, 1))
        load_stack(Seq(0, 1), 0)
        sp.wait_ge(bcol_set, 2)
        nb1, nb2 = E * DFF // P, E * D // P
        sp.dma_start(b_scr[:, 0:E * DFF].rearrange("s (p f) -> p s f", p=P), bcols[:, :, 0:nb1]).then_inc(bcol_out, 16)
        sp.dma_start(b_scr[:, E * DFF:].rearrange("s (p f) -> p s f", p=P), bcols[:, :, nb1:]).then_inc(bcol_out, 16)

        def slot(seq):
            prev, nxt, inp = seq.next(-1), seq.next(1), seq.next(2)
            first = seq.known and seq.b == 0
            last = seq.known and seq.b == LAST
            inputs = not (seq.known and seq.b + 2 > LAST)
            if inputs:
                load_x(inp)
            if not first:
                if not (seq.known and seq.b == 1):
                    sp.wait_ge(misc_free, out_count(seq.next(-2)))
                sp.dma_start(xres[:], io["x"][bass.ds(prev.b, 1)].rearrange("o (t p) d -> p (o t) d", p=P)).then_inc(xres_in, 16)
                store_ctx(prev, 2)
            if not last:
                load_stack(nxt, 1)
            if not first:
                finish_ctx(prev)
            store_ctx(seq, 0)
            if not first:
                store_x2(prev)
            if inputs:
                store_parts(inp)
                load_stack(inp, 0)
            store_ctx(seq, 1)
            if last:
                load_expert_weights()

        def finish_ctx(seq):
            store_ctx(seq, 3)
            sp.wait_ge(ctx_out[0], 32 * (seq.b + 1))
            sp.wait_ge(ctx_out[1], 32 * (seq.b + 1))
            heads = ctx_scr[seq.p].rearrange("g (c r) s -> (g c) r s", r=32)
            sp.dma_start(den[:], heads[:, HD, :].rearrange("h (j n) -> h j n", j=HD)).then_inc(den_in, 16)
            sp.dma_start(ctxt[:], heads[:, 0:HD, :]).then_inc(norm_in, 16)
            sp.wait_ge(rden_set, seq.b + 1)
            sp.dma_start(rden_scr[seq.p], rden[:]).then_inc(rden_out, 16)
            sp.wait_ge(rden_out, 16 * (seq.b + 1))
            sp.dma_start(rdenb[:], rden_scr[seq.p].rearrange("(h o j) n -> h o (j n)", j=HD, o=1).to_broadcast((H, HD, S))).then_inc(norm_in, 16)

        def store_x2(seq):
            sp.wait_ge(misc_free, out_count(seq))
            sp.dma_start(out[0:tokens].rearrange("(b t p) d -> b p t d", p=P, t=T)[bass.ds(seq.b, 1)].rearrange("o p t d -> p (o t) d"),
                         x2[:]).then_inc(x2_out, 16)

        def load_expert_weights():
            sp.wait_ge(s2_full, 2 * H * LAST)
            sp.wait_ge(bcol_out, 32)
            sp.wait_ge(pv_done, 4 * T * LAST)
            sp.dma_start(b1rows, b_scr[:, 0:E * DFF]).then_inc(brow_in, 16)
            sp.dma_start(w1.rearrange("d (e f) -> d e f", e=E), io["w1"].rearrange("e d f -> d e f")).then_inc(w_in, 16)
            sp.dma_start(w2.rearrange("f (e d) -> f e d", d=D), io["w2"].rearrange("e (t f) d -> f (e t) d", f=P)).then_inc(w_in, 16)

        slots(slot, sp)
        end = Seq(LAST // 2, LAST % 2)
        sp.wait_ge(misc_free, out_count(Seq((LAST - 1) // 2, (LAST - 1) % 2)))
        sp.dma_start(xres[:], io["x"][LAST:LAST + 1].rearrange("o (t p) d -> p (o t) d", p=P)).then_inc(xres_in, 16)
        store_ctx(end, 2)
        finish_ctx(end)
        store_x2(end)
        sp.wait_ge(x2_out, 16 * nb)
        experts_loads(sp)

    @block.tensor
    def _(pe):
        filled = [0]

        def open_misc(count):
            if not (isinstance(count, int) and count == 1):
                pe.wait_ge(misc_free, count - 1)

        def job_xt(seq, count):
            open_misc(count)
            pe.wait_ge(xn_set, seq.b + 1)
            for t in range(T):
                mm = nc.tensor.transpose(misc[:, P * t:P * t + P], xn[:, t, :], ident[:])
            mm.then_inc(misc_full, 1)

        def job_project(seq, count, w, xt_count):
            open_misc(count)
            pe.wait_ge(misc_free, xt_count)
            nc.tensor.matmul(misc[:], w[:], xnt[seq.p][:], start=True, stop=True).then_inc(misc_full, 1)

        def job_v(seq, count):
            open_misc(count)
            for t in range(T):
                mm = nc.tensor.matmul(misc[:, D * t:D * t + D], xnt[seq.p][:, P * t:P * t + P], wv[:], start=True, stop=True)
            mm.then_inc(misc_full, 1)

        def job_m(seq, half, count):
            open_misc(count)
            pe.wait_ge(s1_free, 4 * (head_no(seq, UH * half) + UH))
            nc.tensor.transpose(misc[0:UH * T, 0:P], negm[half][:], ident[:]).then_inc(misc_full, 1)

        def job_out(seq, count):
            open_misc(count)
            pe.wait_ge(ctxt_set, seq.b + 1)
            for t in range(T):
                mm = nc.tensor.matmul(misc[:, D * t:D * t + D], ctxt[:, P * t:P * t + P], wo[:], start=True, stop=True)
            mm.then_inc(misc_full, 1)

        def job_rowst(seq, count):
            open_misc(count)
            pe.wait_ge(rows_set, seq.b + 1)
            for t in range(T):
                mm = nc.tensor.transpose(misc[:, P * t:P * t + P], rows[:, t, 0, 0:D], ident[:])
            mm.then_inc(misc_full, 1)

        def job_gate(seq, count):
            open_misc(count)
            for t in range(T):
                mm = nc.tensor.matmul(misc[:, E * t:E * t + E], rowst[:, P * t:P * t + P], wg[:], start=True, stop=True)
            mm.then_inc(misc_full, 1)

        def job_rank(seq, count):
            open_misc(count)
            pe.wait_ge(chosen_set, seq.b + 1)
            for t in range(T + 1):
                dst = misc[:, E * t:E * t + E]
                for u in range(t):
                    mm = nc.tensor.matmul(dst, order[:, 1, :], chosenb[:, u, :], start=(u == 0), stop=(t == T and u == T - 1))
                if t < T:
                    mm = nc.tensor.matmul(dst, order[:, 0, :], chosenb[:, t, :], start=(t == 0), stop=True)
            mm.then_inc(misc_full, 1)

        def max_scores(seq, h, tiles):
            buf, hh = unit_buf(seq, h), h % UH
            if h % UH == 0 and tiles[0] == 0:
                uses = 18 * 16
                pe.wait_ge(stack_in[buf], uses * (seq.i + 1))
            for t in tiles:
                n = 4 * head_no(seq, h) + t
                if not (seq.known and n < 2):
                    pe.wait_ge(s1_free, n - 1)
                lo = max(0, P * t - HALF)
                nc.tensor.matmul(s1p[t % 2][:], qst[buf][0:ROWS1, hh, P * t:P * t + P], kst[buf][0:ROWS1, hh, :],
                                 start=True, stop=False)
                nc.tensor.matmul(s1p[t % 2][:, lo:P * t + P], pick[:, 2, :], band1[:, h, lo - P * t + HALF:],
                                 start=False, stop=True).then_inc(s1_full, 1)

        def exp_scores(seq, h, pair):
            buf, hh = unit_buf(seq, h), h % UH
            n = 2 * head_no(seq, h) + pair
            if h % UH == 0 and pair == 0:
                pe.wait_ge(m_in[buf], 16 * (seq.i + 1))
            if not (seq.known and n < 2):
                pe.wait_ge(exp_done, n - 1)
            for j in range(2):
                t = 2 * pair + j
                out = s2p[pair][:, j, :]
                nc.tensor.matmul(out, kst[buf][:, hh, P * t:P * t + P], qst[buf][:, hh, :], start=True, stop=False)
                for g in range(2):
                    q0 = P * t + HALF * g
                    w = min(BW, S - q0)
                    mm = nc.tensor.matmul(out[:, q0:q0 + w], pick[:, g, :], band2[:, h, 0:w], start=False, stop=(g == 1))
            mm.then_inc(s2_full, 1)

        def weigh_values(seq, h):
            t, par = h % 4, (h // 4) % 2
            g = 4 * seq.b + h // 4
            if t == 0:
                pe.wait_ge(exp_done, 8 * (g + 1))
                if not (seq.known and g == 0):
                    pe.wait_ge(ctx_copied, g)
            for c in range(4):
                mm = nc.tensor.matmul(pvp[32 * c:32 * c + 32, :], vp[seq.p][:, t, 4 * (h // 4) + c, :],
                                      pt[par][:, c, t, :], start=(t == 0), stop=(t == T - 1))
            mm.then_inc(pv_done, 1)

        pe.wait_ge(bias_consts_in, 48)
        nc.tensor.matmul(s2p[0][0:H, 0, :], rel[:], onehot, start=True, stop=True).then_inc(bias_ps, 1)
        nc.tensor.matmul(s2p[1][0:STEPS, 0, 0:H], onehot[:, 0:1].to_broadcast((BUCKETS, STEPS)), rel[:], start=True, stop=True).then_inc(bias_ps, 1)
        pe.wait_ge(proj_in, 5 * 16)
        for n in range(2):
            s = Seq(0, n)
            k = PROLOGUE.index(f"xt{n}") + 1
            job_xt(s, k)
            job_project(s, k + 1, wq, k)
            job_project(s, k + 2, wk, k)
            if n == 0:
                pe.wait_ge(consts_in, 4 * 16)
                job_v(s, k + 3)
        pe.wait_ge(static_in[0], 16)
        pe.wait_ge(steps_out[0], 32)
        pe.wait_ge(band1_set, 1)
        for h in range(UH):
            max_scores(Seq(0, 0), h, range(T))
        pe.wait_ge(static_in[1], 48)
        pe.wait_ge(steps_out[1], 32)
        pe.wait_ge(late_consts_in, 5 * 16)
        pe.wait_ge(band_set, 1)
        job_m(Seq(0, 0), 0, len(PROLOGUE))
        for h in range(UH, LEAD):
            max_scores(Seq(0, 0), h, range(T))

        def slot(seq):
            prev, nxt, inp = seq.next(-1), seq.next(1), seq.next(2)
            first = seq.known and seq.b == 0
            last = seq.known and seq.b == LAST
            inputs = not (seq.known and seq.b + 2 > LAST)
            for h in range(H):
                exp_scores(seq, h, 0)
                lead = ahead(seq, h)
                if lead:
                    max_scores(*lead, (0, 1))
                if h == 0 and not (seq.known and seq.b < 2):
                    job_gate(seq.next(-2), misc_count(seq, "gate"))
                if h == 2 and not (seq.known and seq.b < 2):
                    job_rank(seq.next(-2), misc_count(seq, "rank"))
                if h == 4:
                    job_m(seq, 1, misc_count(seq, "m_mid"))
                if h == 6 and not last:
                    job_v(nxt, misc_count(seq, "v"))
                if inputs:
                    if h == 8:
                        job_xt(inp, misc_count(seq, "xt"))
                    if h == 9:
                        job_project(inp, misc_count(seq, "q"), wq, misc_count(seq, "xt"))
                    if h == 10:
                        job_project(inp, misc_count(seq, "k"), wk, misc_count(seq, "xt"))
                if h == 12 and not last:
                    job_m(nxt, 0, misc_count(seq, "m_end"))
                if not first:
                    if h == 11:
                        job_out(prev, misc_count(seq, "out"))
                    if h == 15:
                        job_rowst(prev, misc_count(seq, "rowst"))
                exp_scores(seq, h, 1)
                if lead:
                    max_scores(*lead, (2, 3))
                if h >= 4:
                    weigh_values(seq, h - 4)
                elif not first:
                    weigh_values(prev, h + 12)

        slots(slot, pe)
        end = Seq(LAST // 2, LAST % 2)
        for h in range(4):
            weigh_values(end, h + 12)
        job_gate(end.next(-1), misc_count(end.next(1), "gate_a"))
        job_rank(end.next(-1), misc_count(end.next(1), "rank_a"))
        job_out(end, out_count(end))
        job_rowst(end, misc_count(end.next(1), "rowst"))
        job_gate(end, misc_count(end.next(1), "gate_b"))
        job_rank(end, misc_count(end.next(1), "rank_b"))
        experts_products(pe)

    @block.scalar
    def _(act):
        def copy_xt(seq, count):
            act.wait_ge(misc_full, count)
            nc.scalar.copy(xnt[seq.p][:], misc[:]).then_inc(misc_free, 1)

        def copy_q(seq, count):
            act.wait_ge(misc_full, count)
            if not (seq.known and seq.b == 0):
                act.wait_ge(qk_parts, 2 * seq.b - 1)
            nc.scalar.activation(q32[:], misc[:], ACT.Identity, bias=bqs[:], scale=HD ** -0.5).then_inc(misc_free, 1)

        def copy_k(seq, count):
            act.wait_ge(misc_full, count)
            if not (seq.known and seq.b == 0):
                act.wait_ge(qk_parts, 2 * seq.b)
            nc.scalar.activation(k32[:], misc[:], ACT.Identity, bias=bk[:], scale=1.0).then_inc(misc_free, 1)

        def copy_rowst(seq, count):
            act.wait_ge(misc_full, count)
            nc.scalar.copy(rowst[:], misc[:]).then_inc(misc_free, 1)

        def gate_exponent(seq):
            act.wait_ge(gate_diff, seq.b + 1)
            nc.scalar.activation(gate_e[:], gate_d[:], ACT.Exp).then_inc(gate_exp, 1)

        def store_maxima(seq, half):
            act.wait_ge(m_parts, 2 * seq.b + half + 1)
            act.dma_start(m_scr[half].rearrange("s g n -> g s n"), mparts[half][:]).then_inc(m_out[half], 16)

        def load_maxima(seq, half):
            buf = 2 * seq.p + half
            act.wait_ge(m_out[half], 16 * (seq.b + 1))
            if not (seq.known and seq.b < 2):
                act.wait_ge(s2_full, 2 * (H * (seq.b - 2) + UH * (half + 1)))
            act.dma_start(qst[buf][ROWS1:ROWS2].rearrange("s h n -> s (h n)"),
                          m_scr[half].rearrange("s g n -> s (g n)")).then_inc(m_in[buf], 16)

        def copy_ctx(seq, g):
            n = 4 * seq.b + g
            act.wait_ge(pv_done, 4 * (n + 1))
            if not (seq.known and n < 2):
                act.wait_ge(ctx_out[g % 2], 16 * (2 * seq.b + g // 2))
            nc.scalar.copy(ctxu[g % 2][:], pvp[:]).then_inc(ctx_copied, 1)

        act.wait_ge(bias_ps, 1)
        nc.scalar.copy(bias_rows, s2p[0][0:H, 0, :]).then_inc(bias_sb, 1)
        act.wait_ge(proj_in, 5 * 16)
        nc.scalar.mul(bqs[:], bq[:], HD ** -0.5).then_inc(bqs_set, 1)
        act.wait_ge(bqs_set, 1)
        for n in range(2):
            k = PROLOGUE.index(f"xt{n}") + 1
            copy_xt(Seq(0, n), k)
            copy_q(Seq(0, n), k + 1)
            copy_k(Seq(0, n), k + 2)
        act.wait_ge(band1_set, 1)
        act.wait_ge(band_set, 1)
        act.wait_ge(steps_out[0], 32)
        act.wait_ge(steps_out[1], 32)
        act.wait_ge(bias_out, 16)
        store_maxima(Seq(0, 0), 0)
        load_maxima(Seq(0, 0), 0)

        def slot(seq):
            prev, nxt, inp = seq.next(-1), seq.next(1), seq.next(2)
            first = seq.known and seq.b == 0
            last = seq.known and seq.b == LAST
            inputs = not (seq.known and seq.b + 2 > LAST)
            for h in range(H):
                g = 4 * seq.b + h // 4
                if h % 4 == 0 and not (seq.known and g < 2):
                    act.wait_ge(pv_done, 4 * (g - 1))
                for pair in range(2):
                    act.wait_ge(s2_full, 2 * head_no(seq, h) + pair + 1)
                    nc.scalar.activation(pt[(h // 4) % 2][:, h % 4, 2 * pair:2 * pair + 2, :], s2p[pair][:],
                                         ACT.Exp).then_inc(exp_done, 1)
                    if pair == 1:
                        if inputs and h == 8:
                            copy_xt(inp, misc_count(seq, "xt"))
                        if inputs and h == 9:
                            copy_q(inp, misc_count(seq, "q"))
                        if inputs and h == 10:
                            copy_k(inp, misc_count(seq, "k"))
                        if h == 15 and not first:
                            copy_rowst(prev, misc_count(seq, "rowst"))
                        if h == 1 and not (seq.known and seq.b < 2):
                            gate_exponent(seq.next(-2))
                        if h == 5:
                            store_maxima(seq, 1)
                        if h == 6:
                            load_maxima(seq, 1)
                        if h == 13 and not last:
                            store_maxima(nxt, 0)
                        if h == 14 and not last:
                            load_maxima(nxt, 0)
                    if pair == 0 and h % 4 == 0:
                        if h >= 8:
                            copy_ctx(seq, h // 4 - 2)
                        elif not first:
                            copy_ctx(prev, h // 4 + 2)

        slots(slot, act)
        end = Seq(LAST // 2, LAST % 2)
        copy_ctx(end, 2)
        copy_ctx(end, 3)
        gate_exponent(end.next(-1))
        copy_rowst(end, misc_count(end.next(1), "rowst"))
        gate_exponent(end)
        experts_functions(act)

    @block.vector
    def _(dve):
        def chain_of(sem_, before):
            return chain_on(dve, sem_, before)

        def measure(n, src, link):
            for t in range(T):
                ins = nc.vector.bn_stats(stats[n][:, t, :], src[:, t, :])
            link(ins).then_inc(stats_seen, 1)
            for t in range(T):
                ins = nc.vector.bn_aggr(mv[n][:, t, :], stats[n][:, t, :])
            link(ins)

        def guess(n, link):
            a, y = ln_a[n], ln_y[n]
            link(nc.vector.tensor_scalar(a[:], mv[n][:, :, 1], EPS, None, ALU.add))
            link(nc.vector.tensor_scalar(y[:].bitcast(I32), a[:].bitcast(I32), -0.5, RSQRT_SEED, ALU.mult, ALU.add))

        def newton(n, link):
            a, y, yy = ln_a[n], ln_y[n], ln_t[n]
            link(nc.vector.scalar_tensor_tensor(yy[:], y[:], -0.5, y[:], ALU.mult, ALU.mult))
            link(nc.vector.tensor_tensor(yy[:], yy[:], a[:], ALU.mult))
            link(nc.vector.scalar_tensor_tensor(y[:], yy[:], 1.5, y[:], ALU.add, ALU.mult))

        def ln1_measure(seq):
            dve.wait_ge(x_in[seq.p], 16 * (seq.i + 1))
            measure(0, xin[seq.p], chain_of(ln_chain, LN_STEPS * seq.b))

        def ln1_guess(seq):
            link = chain_of(ln_chain, LN_STEPS * seq.b + 2)
            guess(0, link)
            newton(0, link)

        def ln1_refine(seq):
            link = chain_of(ln_chain, LN_STEPS * seq.b + 7)
            for _ in range(NEWTON - 1):
                newton(0, link)

        def ln1_apply(seq):
            if not (seq.known and seq.b == 0):
                before = seq.next(-1)
                count = 1 if before.known and before.b == 0 else (
                    5 if before.known and before.b == 1 else misc_count(before.next(-2), "xt"))
                dve.wait_ge(misc_full, count)
            for t in range(T):
                ins = nc.vector.tensor_scalar(xn[:, t, :], xin[seq.p][:, t, :], mv[0][:, t, 0:1], ln_y[0][:, t:t + 1],
                                              ALU.subtract, ALU.mult)
            ins.then_inc(xn_set, 1)

        def layernorm_rows(seq):
            for stage in (ln1_measure, ln1_guess, ln1_refine, ln1_apply):
                stage(seq)

        def ln2_measure(seq, count):
            dve.wait_ge(misc_free, count)
            measure(1, x2, chain_of(ln2_chain, LN_STEPS * seq.b))

        def ln2_guess(seq):
            link = chain_of(ln2_chain, LN_STEPS * seq.b + 2)
            guess(1, link)
            newton(1, link)

        def ln2_refine(seq):
            link = chain_of(ln2_chain, LN_STEPS * seq.b + 7)
            for _ in range(NEWTON - 1):
                newton(1, link)

        def ln2_apply(seq, half):
            if half == 0 and not (seq.known and seq.b == 0):
                dve.wait_ge(dispatched, 16 * TOPK * T * seq.b)
            for t in (2 * half, 2 * half + 1):
                nc.vector.tensor_scalar(rows[:, t, 0, 0:D], x2[:, t, :], mv[1][:, t, 0:1], ln_y[1][:, t:t + 1],
                                        ALU.subtract, ALU.mult)
            if half:
                nc.vector.tensor_scalar(rows[:, :, :, ID_COL], numbers[:, C_IDS:C_IDS + T].rearrange("p (t o) -> p t o", o=1).to_broadcast((P, T, TOPK)),
                                        token_base[:], None, ALU.add).then_inc(rows_set, 1)
                dve.wait_ge(rows_set, seq.b + 1)
                nc.vector.tensor_scalar(token_base[:], token_base[:], float(S), None, ALU.add).then_inc(base_set, 1)
                dve.wait_ge(base_set, seq.b + 1)

        GATE_STEPS = 10

        def take_top(seq, count):
            link = chain_of(gate_chain, GATE_STEPS * seq.b)
            dve.wait_ge(misc_full, count)
            nc.vector.tensor_tensor(logits[:], misc[:, 0:T * E].rearrange("p (t e) -> p t e", t=T),
                                    bg[:].rearrange("p (o e) -> p o e", o=1).to_broadcast((P, T, E)), ALU.add).then_inc(misc_free, 1)
            dve.wait_ge(misc_free, count).then_inc(logits_seen, 1)
            for t in range(T):
                ins = nc.vector.max(top[:, t, :], logits[:, t, :])
            link(ins)
            nc.vector.tensor_tensor(gate_d[:], top[:, :, 1], top[:, :, 0], ALU.subtract).then_inc(gate_diff, 1)

        def choose(seq):
            link = chain_of(gate_chain, GATE_STEPS * seq.b + 1)
            for t in range(T):
                ins = nc.vector.max_index(topi[:, t, :], top[:, t, :], logits[:, t, :])
            link(ins)
            link(nc.vector.tensor_copy(choice[:], topi[:, :, 0:TOPK]))
            link(nc.vector.tensor_tensor(
                chosen[:], choice[:].rearrange("p t (c o) -> p (t c) o", o=1).to_broadcast((P, T * TOPK, E)),
                numbers[:, C_IOTA8:C_IOTA8 + E].rearrange("p (o e) -> p o e", o=1).to_broadcast((P, T * TOPK, E)),
                ALU.is_equal))
            both = chosen[:].rearrange("p (t c) e -> p t c e", c=TOPK)
            nc.vector.tensor_tensor(chosenb[:], both[:, :, 0, :], both[:, :, 1, :], ALU.add).then_inc(chosen_set, 1)

        def weigh_choices(seq):
            dve.wait_ge(gate_exp, seq.b + 1)
            n = GATE_STEPS * seq.b + 4

            def step(k, ins):
                ins.then_inc(gate_chain, 1)
                dve.wait_ge(gate_chain, n + k)

            step(1, nc.vector.tensor_scalar(gate_s[:], gate_e[:], 1.0, None, ALU.add))
            step(2, nc.vector.reciprocal(rows[:, :, 0, W_COL], gate_s[:]))
            step(3, nc.vector.tensor_tensor(rows[:, :, 1, W_COL], rows[:, :, 0, W_COL], gate_e[:], ALU.mult))

        def place_rows(seq, count):
            n = GATE_STEPS * seq.b + 7

            def step(k, ins):
                ins.then_inc(gate_chain, 1)
                dve.wait_ge(gate_chain, n + k)

            dve.wait_ge(misc_full, count)
            step(1, nc.vector.tensor_tensor(place[:], misc[:, 0:T * E].rearrange("p (t e) -> p t e", t=T),
                                            counts[:].rearrange("p (o e) -> p o e", o=1).to_broadcast((P, T, E)), ALU.add))
            nc.vector.tensor_tensor(counts[:], counts[:], misc[:, T * E:(T + 1) * E], ALU.add).then_inc(misc_free, 1)
            step(2, nc.vector.tensor_tensor(picked[:].rearrange("p (t c) e -> p t c e", c=TOPK), chosen[:].rearrange("p (t c) e -> p t c e", c=TOPK),
                                            place[:].rearrange("p t (o e) -> p t o e", o=1).to_broadcast((P, T, TOPK, E)), ALU.mult))
            step(3, nc.vector.tensor_reduce(slot_f[:], picked[:], AXX, ALU.add))
            if not (seq.known and seq.b == 0):
                dve.wait_ge(dispatched, 16 * TOPK * T * seq.b)
            nc.vector.tensor_copy(slot_i[:], slot_f[:]).then_inc(slots_set, 1)

        def add_v_bias(seq, count):
            dve.wait_ge(misc_full, count)
            if not (seq.known and seq.b < 2):
                dve.wait_ge(pv_done, 16 * (seq.b - 1))
            nc.vector.tensor_tensor(vp[seq.p][:, :, :, 0:HD], misc[:].rearrange("p (t h d) -> p t h d", t=T, h=H),
                                    bv[:].rearrange("p (o h d) -> p o h d", o=1, h=H).to_broadcast((P, T, H, HD)),
                                    ALU.add).then_inc(misc_free, 1)

        def split_m(seq, half, count):
            u = 2 * seq.b + half
            parts, src = mparts[half], misc[0:UH * T, 0:P]
            dve.wait_ge(misc_full, count)
            if not (seq.known and seq.b == 0):
                dve.wait_ge(m_out[half], 16 * seq.b)
            nc.vector.tensor_copy(parts[:, 0, :], src).then_inc(m_chain, 1)
            dve.wait_ge(m_chain, 2 * u + 1)
            nc.vector.tensor_tensor(mrest[:], src, parts[:, 0, :], ALU.subtract).then_inc(misc_free, 1)
            dve.wait_ge(misc_free, count)
            nc.vector.tensor_copy(parts[:, 1, :], mrest[:]).then_inc(m_chain, 1)
            dve.wait_ge(m_chain, 2 * u + 2)
            nc.vector.tensor_tensor(parts[:, 2, :], mrest[:], parts[:, 1, :], ALU.subtract).then_inc(m_parts, 1)

        def take_maxima(seq, h, tiles=range(T)):
            half = h // UH
            for t in tiles:
                dve.wait_ge(s1_full, 4 * head_no(seq, h) + t + 1)
                nc.vector.tensor_reduce(negm[half][:, (h % UH) * T + t:(h % UH) * T + t + 1], s1p[t % 2][:], AXX,
                                        ALU.max, negate=True).then_inc(s1_free, 1)

        def invert_sums(seq):
            dve.wait_ge(den_in, 16 * (seq.b + 1))
            if not (seq.known and seq.b == 0):
                dve.wait_ge(rden_out, 16 * seq.b)
            nc.vector.reciprocal(rden[:], den[:]).then_inc(rden_set, 1)

        def add_residual(seq, count):
            dve.wait_ge(misc_full, count)
            dve.wait_ge(xres_set, seq.b + 1)
            if not (seq.known and seq.b == 0):
                dve.wait_ge(x2_out, 16 * seq.b)
            nc.vector.tensor_tensor(x2[:].rearrange("p t d -> p (t d)"), misc[:], xres[:].rearrange("p t d -> p (t d)"),
                                    ALU.add).then_inc(misc_free, 1)

        chain = [0]

        def link(ins):
            chain[0] += 1
            ins.then_inc(bias_chain, 1)
            dve.wait_ge(bias_chain, chain[0])

        nc.vector.memset(token_base[:], 0.0)
        nc.vector.memset(rows[:], 0.0)
        nc.vector.memset(padrows[:], 0.0).then_inc(dummy_set, 1)
        layernorm_rows(Seq(0, 0))
        dve.wait_ge(bias_ps, 2)
        dve.wait_ge(bias_consts_in, 48)
        link(nc.vector.tensor_copy(delta[:], s2p[1][0:STEPS, 0, 0:H]))
        link(nc.vector.tensor_copy(dparts[:, 0, :], delta[:]))
        link(nc.vector.tensor_tensor(drest[:], delta[:], dparts[:, 0, :], ALU.subtract))
        link(nc.vector.tensor_copy(dparts[:, 1, :], drest[:]))
        link(nc.vector.tensor_tensor(dparts[:, 2, :], drest[:], dparts[:, 1, :], ALU.subtract))
        link(nc.vector.tensor_scalar(dsel[:], dparts[:, 0, :], stepmask[:, S:S + 1], None, ALU.mult))
        for s in (1, 2):
            link(nc.vector.scalar_tensor_tensor(dsel[:], dparts[:, s, :], stepmask[:, S + s:S + s + 1], dsel[:], ALU.mult, ALU.add))
        for half in range(2):
            if half:
                k = PROLOGUE.index("q0") + 1
                split(dve, Seq(0, 0), 0, k, q32, qparts)
                split(dve, Seq(0, 0), 1, k + 1, k32, kparts)
                dve.wait_ge(steps_out[0], 32)
            for hh in range(UH):
                h = UH * half + hh
                ins = nc.vector.tensor_scalar(steprows[:, hh, :], stepmask[:, 0:S], dsel[:, h:h + 1], None, ALU.mult)
            ins.then_inc(steps_set, 1)
        dve.wait_ge(toep_in, 48)
        link(nc.vector.tensor_scalar(band1[:], toep1, 1.0 / BIAS_SCALE, None, ALU.mult))
        nc.vector.memset(band1[HALF:P, :, P:B1W], 0.0).then_inc(band1_set, 1)
        dve.wait_ge(consts_in, 4 * 16)
        add_v_bias(Seq(0, 0), PROLOGUE.index("v0") + 1)
        nc.vector.tensor_copy(counts[:], numbers[:, C_BASE:C_BASE + E])
        dve.wait_ge(dummy_out, 16)
        nc.vector.tensor_copy(padrows[:, :, ID_COL], numbers[:, C_PADID:C_PADID + TJ]).then_inc(pads_set, 1)
        layernorm_rows(Seq(0, 1))
        for h in range(UH):
            take_maxima(Seq(0, 0), h)
        for h in range(UH, LEAD):
            take_maxima(Seq(0, 0), h)
            if h == UH:
                dve.wait_ge(late_consts_in, 5 * 16)
                split_m(Seq(0, 0), 0, len(PROLOGUE))

        def slot(seq):
            prev, nxt, inp = seq.next(-1), seq.next(1), seq.next(2)
            first = seq.known and seq.b == 0
            last = seq.known and seq.b == LAST
            routed = not (seq.known and seq.b < 2)
            inputs = not (seq.known and seq.b + 2 > LAST)
            for h in range(H):
                lead = ahead(seq, h)
                if lead:
                    take_maxima(*lead, (0, 1))
                if routed:
                    if h == 1:
                        choose(seq.next(-2))
                    if h == 2:
                        weigh_choices(seq.next(-2))
                if inputs:
                    if h == 5:
                        ln1_measure(inp)
                    if h == 6:
                        ln1_refine(inp)
                if not first:
                    if h == 7:
                        invert_sums(prev)
                    if h == 12:
                        ln2_measure(prev, misc_count(seq, "out"))
                    if h == 13:
                        ln2_guess(prev)
                    if h == 14:
                        ln2_apply(prev, 0)
                if lead:
                    take_maxima(*lead, (2, 3))
                if routed:
                    if h == 0:
                        take_top(seq.next(-2), misc_count(seq, "gate"))
                    if h == 2:
                        place_rows(seq.next(-2), misc_count(seq, "rank"))
                if h == 4:
                    split_m(seq, 1, misc_count(seq, "m_mid"))
                if inputs:
                    if h == 5:
                        ln1_guess(inp)
                    if h == 7:
                        ln1_apply(inp)
                if not last:
                    if h == 6:
                        add_v_bias(nxt, misc_count(seq, "v"))
                    if h == 12:
                        split_m(nxt, 0, misc_count(seq, "m_end"))
                if not first:
                    if h == 11:
                        add_residual(prev, misc_count(seq, "out"))
                    if h == 13:
                        ln2_refine(prev)
                    if h == 14:
                        ln2_apply(prev, 1)

        slots(slot, dve)
        end = Seq(LAST // 2, LAST % 2)
        take_top(end.next(-1), misc_count(end.next(1), "gate_a"))
        choose(end.next(-1))
        weigh_choices(end.next(-1))
        place_rows(end.next(-1), misc_count(end.next(1), "rank_a"))
        invert_sums(end)
        add_residual(end, out_count(end))
        ln2_measure(end, out_count(end))
        ln2_guess(end)
        ln2_refine(end)
        for half in range(2):
            ln2_apply(end, half)
        take_top(end, misc_count(end.next(1), "gate_b"))
        choose(end)
        weigh_choices(end)
        place_rows(end, misc_count(end.next(1), "rank_b"))
        experts_vectors(dve)

    @block.gpsimd
    def _(pool):
        for n in range(2):
            ins = pool.memset(vp[n][:, :, :, HD:32], 1.0)
        ins.then_inc(ones_set, 1)

        def add_out_bias(seq):
            pool.wait_ge(xres_in, 16 * (seq.b + 1))
            pool.tensor_tensor(xres[:], xres[:], bo[:].rearrange("p (o d) -> p o d", o=1).to_broadcast((P, T, D)),
                               ALU.add).then_inc(xres_set, 1)

        def dispatch(seq):
            pool.wait_ge(rows_set, seq.b + 1).then_inc(double_started, 1)
            pool.tensor_copy(rows[:, :, 1, 0:D], rows[:, :, 0, 0:D]).then_inc(rows_doubled, 1)
            pool.wait_ge(rows_doubled, seq.b + 1)
            pool.wait_ge(slots_set, seq.b + 1).then_inc(dispatch_started, 1)
            for t in range(T):
                for c in range(TOPK):
                    k = TOPK * t + c
                    pool.indirect_dma_start(disp, bass.IndirectOffsetOnAxis(slot_i[:, k:k + 1], 0), rows[:, t, c, :], None).then_inc(dispatched, 16)

        def normalise(seq):
            pool.wait_ge(norm_in, 32 * (seq.b + 1))
            pool.tensor_tensor(ctxt[:], ctxt[:], rdenb[:], ALU.mult).then_inc(ctxt_set, 1)

        def split_biases():
            nb1 = E * DFF // P
            pool.wait_ge(bcol_in, 32)
            steps = 0
            for src, lo, hi in ((b1col, 0, nb1), (b2col, nb1, (E * DFF + E * D) // P)):
                r = brest[:, 0:hi - lo]
                for n, (o, i0, i1) in enumerate(((bcols[:, 0, lo:hi], src[:], None), (r, src[:], bcols[:, 0, lo:hi]),
                                                 (bcols[:, 1, lo:hi], r, None), (bcols[:, 2, lo:hi], r, bcols[:, 1, lo:hi]))):
                    ins = pool.tensor_copy(o, i0) if i1 is None else pool.tensor_tensor(o, i0, i1, ALU.subtract)
                    ins.then_inc(bcol_chain, 1)
                    steps += 1
                    pool.wait_ge(bcol_chain, steps)
            pool.memset(ones3[:], 1.0).then_inc(bcol_set, 2)

        pool.wait_ge(toep_in, 48)
        for step, (dst, args) in enumerate((
                (band2[:], (toep2, 1.0 / BIAS_SCALE, None, ALU.mult)),
                (toep2[HALF:P], (toep2[HALF:P], 1.0 / BIAS_SCALE, None, ALU.mult)))):
            pool.tensor_scalar(dst, *args).then_inc(band2_chain, 1)
            pool.wait_ge(band2_chain, step + 1)
        pool.tensor_tensor(toep2[HALF:P], toep2[HALF:P], band2[HALF:P], ALU.subtract).then_inc(band2_chain, 1)
        pool.wait_ge(band2_chain, 3)
        pool.tensor_scalar(band2[HALF:P], toep2[HALF:P], LOW_SCALE, None, ALU.mult).then_inc(band_set, 1)
        pool.wait_ge(band_set, 1)
        k = PROLOGUE.index("q1") + 1
        split(pool, Seq(0, 1), 0, k, q32, qparts)
        split(pool, Seq(0, 1), 1, k + 1, k32, kparts)
        split_biases()
        pool.wait_ge(late_consts_in, 5 * 16)

        def slot(seq):
            prev, nxt, inp = seq.next(-1), seq.next(1), seq.next(2)
            first = seq.known and seq.b == 0
            last = seq.known and seq.b == LAST
            inputs = not (seq.known and seq.b + 2 > LAST)
            if not (seq.known and seq.b < 2):
                dispatch(seq.next(-2))
            if not first:
                add_out_bias(prev)
                normalise(prev)
            if inputs:
                split(pool, inp, 0, misc_count(seq, "q"), q32, qparts)
                split(pool, inp, 1, misc_count(seq, "k"), k32, kparts)

        slots(slot, pool)
        end = Seq(LAST // 2, LAST % 2)
        dispatch(end.next(-1))
        add_out_bias(end)
        normalise(end)
        dispatch(end)
        experts_scatters(pool)


def buckets():
    d = np.arange(S)
    f = np.maximum(d, 1).astype(np.float32) / np.float32(16)
    large = 16 + (np.log(f) / np.float32(np.log(4.0)) * np.float32(16)).astype(np.int32)
    return np.where(d < 16, d, np.minimum(large, BUCKETS - 1))


def constants(nb):
    bf16 = mybir.dt.np(BF16)
    tokens = nb * S
    region = tokens + TILE
    ntiles = TOPK * tokens // TILE + E - 1
    ntiles += -ntiles % DEEP
    numbers = np.zeros((P, C_IOTA + ntiles), np.float32)
    lane = np.arange(P)
    numbers[:, C_IDS:C_IOTA8] = lane[:, None] + P * np.arange(T)
    numbers[:, C_IOTA8:C_SIGN] = np.arange(E)
    numbers[:, C_SIGN:C_BASE] = 1 - 2 * (np.arange(E) % 2)
    numbers[:, C_BASE:C_PADID] = region * np.arange(E)
    numbers[:, C_PADID:C_IOTA] = tokens + lane[:, None] + P * np.arange(TJ)
    numbers[:, C_IOTA:] = np.arange(ntiles)
    order = np.ones((P, 2, P), np.float32)
    order[:, 0, :] = lane[:, None] < lane[None, :]
    bucket = buckets()
    assert bucket[FAR] == BUCKETS - 1 and bucket[FAR - 1] < BUCKETS - 1
    onehot = np.zeros((BUCKETS, S), np.float32)
    for e in range(S):
        d = e - (HALF - 1) if e < FWD else FWD - 1 - (e - FWD)
        onehot[bucket[max(d, 0)], e] += 8.0
        onehot[BUCKETS - 1, e] -= 8.0
    stepmask = np.zeros((STEPS, S + NPARTS), np.float32)
    kstatic = np.zeros((ROWS2 - STACK, S), np.float32)
    for u in range(1, S // HALF):
        for s in range(NPARTS):
            r = NPARTS * (u - 1) + s
            stepmask[r, 0:HALF * u] = 1.0
            stepmask[r, S + s] = 1.0
            kstatic[r, HALF * u:HALF * u + HALF] = 1.0
    kstatic[STEPS:] = 1.0
    pick = np.zeros((3, P, P), np.float16)
    for g in range(2):
        for r in range(HALF):
            pick[g, HALF - 1 - r, HALF * g + r] = BIAS_SCALE
            pick[g, P - 1 - r, HALF * g + r] = BIAS_SCALE / LOW_SCALE
    pick[2] = np.eye(P)[::-1] * BIAS_SCALE
    return {"onehot": onehot, "stepmask": stepmask, "kstatic": kstatic.astype(bf16), "pick": pick,
            "ident": np.eye(P, dtype=np.float32), "numbers": numbers, "order": order.astype(bf16)}


NAMES = {"x": "L0_attn_hidden_states", "wq": "L0_attn_Wq", "bq": "L0_attn_bq", "wk": "L0_attn_Wk", "bk": "L0_attn_bk",
         "wv": "L0_attn_Wv", "bv": "L0_attn_bv", "wo": "L0_attn_Wo", "bo": "L0_attn_bo", "rel": "L0_attn_rel_bias",
         "w1": "L0_ffn_W1", "b1": "L0_ffn_b1", "w2": "L0_ffn_W2", "b2": "L0_ffn_b2", "wg": "L0_ffn_Wg", "bg": "L0_ffn_bg"}


def build(nc, nb, io, out):
    with ExitStack() as ctx:
        layer(nc, ctx, nb, io, out)


def kernel(**inputs):
    import concourse.bacc as bacc
    from concourse.bass_utils import run_bass_kernel_spmd

    nc = bacc.Bacc("TRN2", target_bir_lowering=False, num_devices=1)
    arrays = {name: np.ascontiguousarray(inputs[full]) for name, full in NAMES.items()}
    nb = arrays["x"].shape[0]
    arrays.update(constants(nb))
    io = {name: nc.dram_tensor(f"in_{name}", a.shape, mybir.dt.from_np(a.dtype), kind="ExternalInput").ap()
          for name, a in arrays.items()}
    out = nc.dram_tensor("out_rows", (nb * S + TILE, D), F32, kind="ExternalOutput").ap()
    build(nc, nb, io, out)
    r = run_bass_kernel_spmd(nc, [{f"in_{name}": a for name, a in arrays.items()}], core_ids=[0])
    return r.results[0]["out_rows"][0:nb * S].reshape(nb, S, D)
```

```python
from contextlib import ExitStack

import numpy as np

import concourse.bass as bass
from concourse import mybir
from concourse.alu_op_type import AluOpType as ALU

F32 = mybir.dt.float32
BF16 = mybir.dt.bfloat16
F16 = mybir.dt.float16
I32 = mybir.dt.int32
U32 = mybir.dt.uint32
ACT = mybir.ActivationFunctionType
AXX = mybir.AxisListType.X

P = 128
S = 512
D = 128
H = 16
HD = D // H
T = S // P
BUCKETS = 32
FAR = 59
HALF = 64
NPARTS = 3
STACK = NPARTS * NPARTS * HD
STEPS = (S // HALF - 1) * NPARTS
ROWS1 = STACK + STEPS
ROWS2 = ROWS1 + NPARTS
UH = 8
BW = 2 * HALF - 6
B1W = P + HALF
FWD = 192
BIAS_SCALE = 16.0
LOW_SCALE = 2048.0
LEAD = 12
EPS = 1e-5
RSQRT_SEED = 1597463007.0
NEWTON = 3
LN_STEPS = 4 + 4 * NEWTON

E = 8
TOPK = 2
DFF = 512
FT = DFF // P
TILE = 2 * P
TJ = TILE // P
ROW = D + 4
ID_COL, W_COL = D, D + 1
C_IDS = 0
C_IOTA8 = C_IDS + T
C_SIGN = C_IOTA8 + E
C_BASE = C_SIGN + E
C_PADID = C_BASE + E
C_IOTA = C_PADID + TJ
DEEP = 4


class Seq:

    def __init__(self, i, p):
        self.i, self.p, self.b = i, p, 2 * i + p

    def next(self, k):
        return Seq(self.i + (self.p + k) // 2, (self.p + k) % 2)

    @property
    def known(self):
        return isinstance(self.b, int)


def layer(nc, ctx, nb, io, out):
    sb = lambda name, shape, dt: ctx.enter_context(nc.sbuf_tensor(name, shape, dt))
    pb = lambda name, shape, dt: ctx.enter_context(nc.psum_tensor(name, shape, dt))
    sem = lambda name: ctx.enter_context(nc.semaphore(name))
    dram = lambda name, shape, dt: nc.dram_tensor(name, shape, dt, kind="Internal").ap()

    tokens = nb * S
    region = tokens + TILE
    ntiles = TOPK * tokens // TILE + E - 1
    table = ntiles + -ntiles % DEEP
    numbers_w = C_IOTA + table

    wq = sb("wq", [P, D], F32)
    wk = sb("wk", [P, D], F32)
    wv = sb("wv", [P, D], F32)
    wo = sb("wo", [P, D], F32)
    bq = sb("bq", [P, 1], F32)
    bqs = sb("bqs", [P, 1], F32)
    bk = sb("bk", [P, 1], F32)
    bv = sb("bv", [P, 1], F32)
    bo = sb("bo", [P, D], F32)
    ident = sb("ident", [P, P], F32)
    pick = sb("pick", [P, 3, P], F16)
    rel = sb("rel", [BUCKETS, H], F32)
    stacks = sb("stacks", [P, 4, 2, UH, S], BF16)
    qst = [stacks[0:ROWS2, n, 0] for n in range(4)]
    kst = [stacks[0:ROWS2, n, 1] for n in range(4)]
    pt = [sb(f"pt{n}", [P, 4, T, S], F32) for n in range(2)]
    vp = [sb(f"vp{n}", [P, T, H, 32], F32) for n in range(2)]
    band2 = sb("band2", [P, H, BW], F16)
    band1 = sb("band1", [P, H, B1W], F16)
    xin = [sb(f"xin{n}", [P, T, D], F32) for n in range(2)]
    xres = sb("xres", [P, T, D], F32)
    x2 = sb("x2", [P, T, D], F32)
    xn = sb("xn", [P, T, D], F32)
    xnt = [sb(f"xnt{n}", [P, S], F32) for n in range(2)]
    q32 = sb("q32", [P, S], F32)
    k32 = sb("k32", [P, S], F32)
    rest = sb("rest", [P, S], F32)
    qparts = sb("qparts", [P, NPARTS, S], BF16)
    kparts = sb("kparts", [P, NPARTS, S], BF16)
    ctxu = [sb(f"ctxu{n}", [P, S], F32) for n in range(2)]
    ctxt = sb("ctxt", [P, S], F32)
    den = sb("den", [P, S // HD], F32)
    rden = sb("rden", [P, S // HD], F32)
    rdenb = sb("rdenb", [P, S], F32)
    stats, mv, ln_a, ln_y, ln_t = (
        [sb(f"{name}{n}", shape, F32) for n in range(2)]
        for name, shape in (("stats", [P, T, 6]), ("mv", [P, T, 2]), ("ln_a", [P, T]), ("ln_y", [P, T]), ("ln_t", [P, T])))
    negm = [sb(f"negm{n}", [P, UH * T], F32) for n in range(2)]
    mrest = sb("mrest", [UH * T, P], F32)
    mparts = [sb(f"mparts{n}", [UH * T, NPARTS, P], BF16) for n in range(2)]
    delta = sb("delta", [STEPS, H], F32)
    dparts = sb("dparts", [STEPS, NPARTS, H], BF16)
    drest = sb("drest", [STEPS, H], F32)
    dsel = sb("dsel", [STEPS, H], F32)

    wg = sb("wg", [P, E], F32)
    bg = sb("bg", [P, E], F32)
    numbers = sb("numbers", [P, numbers_w], F32)
    order = sb("order", [P, 2, P], BF16)
    rows = sb("rows", [P, T, TOPK, ROW], F32)
    padrows = sb("padrows", [P, TJ, ROW], F32)
    rowst = sb("rowst", [P, S], F32)
    logits = sb("logits", [P, T, E], F32)
    top = sb("top", [P, T, E], F32)
    topi = sb("topi", [P, T, E], U32)
    choice = sb("choice", [P, T, TOPK], F32)
    chosen = sb("chosen", [P, T * TOPK, E], F32)
    picked = sb("picked", [P, T * TOPK, E], F32)
    chosenb = sb("chosenb", [P, T + 1, E], BF16)
    gate_d = sb("gate_d", [P, T], F32)
    gate_e = sb("gate_e", [P, T], F32)
    gate_s = sb("gate_s", [P, T], F32)
    token_base = sb("token_base", [P, 1], F32)
    counts = sb("counts", [P, E], F32)
    place = sb("place", [P, T, E], F32)
    slot_f = sb("slot_f", [P, T * TOPK], F32)
    slot_i = sb("slot_i", [P, T * TOPK], U32)
    b1col = sb("b1col", [P, E * DFF // P], F32)
    b2col = sb("b2col", [P, E * D // P], F32)
    bcols = sb("bcols", [P, NPARTS, (E * DFF + E * D) // P], BF16)
    brest = sb("brest", [P, E * DFF // P], F32)
    ones3 = sb("ones3", [NPARTS, TILE], BF16)

    w1 = stacks[:, 0].rearrange("p k h s -> p (k h s)").bitcast(F32)
    w2 = stacks[:, 1].rearrange("p k h s -> p (k h s)").bitcast(F32)
    tab_row = q32[:, 0:table].bitcast(I32)
    tab_off = q32[:, table:2 * table].bitcast(I32)
    tab_gelu = q32[:, 2 * table:3 * table]
    tab_silu = k32[:, 0:table]
    tab_half = k32[:, table:2 * table]
    tab_pad = k32[:, 2 * table:2 * table + E].bitcast(I32)

    s1p = [pb(f"s1p{n}", [P, S], F32) for n in range(2)]
    s2p = [pb(f"s2p{n}", [P, 2, S], F32) for n in range(2)]
    pvp = pb("pvp", [P, S], F32)
    misc = pb("misc", [P, S], F32)

    bias_scr = dram("bias_scr", (H, S), F32)
    q_scr = [dram(f"q_scr{n}", (NPARTS, NPARTS, P, S), BF16) for n in range(2)]
    k_scr = [dram(f"k_scr{n}", (NPARTS, P, S), BF16) for n in range(2)]
    ctx_scr = [dram(f"ctx_scr{n}", (4, P, S), F32) for n in range(2)]
    m_scr = [dram(f"m_scr{n}", (NPARTS, UH * T, P), BF16) for n in range(2)]
    disp = dram("disp", (E * region + TILE, ROW), F32)
    b_scr = dram("b_scr", (NPARTS, E * DFF + E * D), BF16)
    rden_scr = [dram(f"rden_scr{n}", (P, S // HD), F32) for n in range(2)]

    flat0 = pt[0][:].rearrange("p a t s -> p (a t s)")
    bias_rows = pt[1][0:H, 0, 0, :]
    toep2 = flat0[:, 0:H * BW].rearrange("p (h w) -> p h w", h=H)
    at = H * BW
    toep1 = flat0[:, at:at + H * B1W].rearrange("p (h w) -> p h w", h=H)
    at += H * B1W
    steprows = flat0[0:STEPS, at:at + UH * S // 2].bitcast(BF16).rearrange("p (h s) -> p h s", h=UH)
    at += UH * S // 2
    stepmask = flat0[0:STEPS, at:at + S + NPARTS]
    at += S + NPARTS
    onehot = flat0[0:BUCKETS, at:at + S]

    spare = [pt[n][:].rearrange("p a t s -> p (a t s)") for n in range(2)]
    cut = lambda n, at, width: spare[n][:, at:at + width]
    per_expert = tokens // TILE
    few = cut(0, 0, E * per_expert).rearrange("p (e n) -> p e n", e=E)
    before = cut(0, 1024, table * E).rearrange("p (n e) -> p n e", e=E)
    weighed = cut(0, 2048, table * E).rearrange("p (n e) -> p n e", e=E)
    tcount = cut(0, 3072, E)
    tsum = cut(0, 3088, E)
    cnt = cut(0, 3104, E)
    one8 = cut(0, 3120, E)
    tab_e = cut(0, 3136, table)
    tab_t = cut(0, 3264, table)
    tab_r = cut(0, 3392, table)
    gelu = [cut(1, 4 * TILE * n, 4 * TILE).rearrange("p (f n) -> p f n", f=FT) for n in range(2)]
    tanh = [cut(1, 4 * TILE * (2 + n), 4 * TILE).rearrange("p (f n) -> p f n", f=FT) for n in range(2)]
    acts = [cut(1, 4 * TILE * (4 + n), 4 * TILE).rearrange("p (f n) -> p f n", f=FT) for n in range(2)]
    xg = [cut(1, 6144 + TJ * ROW * n, TJ * ROW).rearrange("p (j r) -> p j r", j=TJ) for n in range(DEEP)]
    xgt = [cut(1, 7200 + TILE * n, TILE) for n in range(2)]
    w1t = [buf[:].rearrange("p t d -> p (t d)") for buf in xin] + [buf[:] for buf in xnt]
    yw = [cut(0, 6912 + TJ * D * n, TJ * D).rearrange("p (j d) -> p j d", j=TJ) for n in range(2)]
    b1t = [cut(0, 3520 + DFF // 2 * n, DFF // 2)[0:NPARTS].bitcast(BF16) for n in range(DEEP)]
    ids = [cut(0, 7936 + 4 * n, TJ).bitcast(U32) for n in range(DEEP)]
    wts = [cut(0, 7952 + 4 * n, TJ) for n in range(DEEP)]
    b1rows = vp[0][0:NPARTS].rearrange("s t h c -> s (t h c)").bitcast(BF16)
    b2rows = spare[0][0:NPARTS, 4864:4864 + E * DFF // 2].bitcast(BF16)
    hp = [s2p[n][:].rearrange("p b (f n) -> p (b f) n", n=TILE) for n in range(2)]
    xgtp = [s1p[n][:, 0:TILE] for n in range(2)]
    yp = [pvp[:, 0:TJ * D].rearrange("p (j d) -> p j d", j=TJ), misc[:, 0:TJ * D].rearrange("p (j d) -> p j d", j=TJ)]

    bias_consts_in = sem("bias_consts_in")
    consts_in = sem("consts_in")
    ones_set = sem("ones_set")
    bias_ps = sem("bias_ps")
    proj_in = sem("proj_in")
    band1_set = sem("band1_set")
    band2_chain = sem("band2_chain")
    bias_sb = sem("bias_sb")
    bias_out = sem("bias_out")
    toep_in = sem("toep_in")
    bias_chain = sem("bias_chain")
    steps_set = sem("steps_set")
    steps_out = [sem(f"steps_out{n}") for n in range(2)]
    static_in = [sem(f"static_in{n}") for n in range(2)]
    late_consts_in = sem("late_consts_in")
    band_set = sem("band_set")
    bqs_set = sem("bqs_set")
    bo_set = sem("bo_set")
    x_in = [sem(f"x_in{n}") for n in range(2)]
    ln_chain = sem("ln_chain")
    xn_set = sem("xn_set")
    misc_full = sem("misc_full")
    misc_free = sem("misc_free")
    parts_chain = sem("parts_chain")
    qk_parts = sem("qk_parts")
    qk_out = [sem(f"qk_out{n}") for n in range(2)]
    stack_in = [sem(f"stack_in{n}") for n in range(4)]
    s1_full = sem("s1_full")
    s1_free = sem("s1_free")
    m_parts = sem("m_parts")
    m_chain = sem("m_chain")
    m_out = [sem(f"m_out{n}") for n in range(2)]
    m_in = [sem(f"m_in{n}") for n in range(4)]
    s2_full = sem("s2_full")
    exp_done = sem("exp_done")
    pv_done = sem("pv_done")
    ctx_copied = sem("ctx_copied")
    ctx_out = [sem(f"ctx_out{n}") for n in range(2)]
    den_in = sem("den_in")
    rden_set = sem("rden_set")
    rden_out = sem("rden_out")
    norm_in = sem("norm_in")
    ctxt_set = sem("ctxt_set")
    xres_in = sem("xres_in")
    xres_set = sem("xres_set")
    x2_out = sem("x2_out")
    ln2_chain = sem("ln2_chain")
    rows_set = sem("rows_set")
    gate_chain = sem("gate_chain")
    gate_diff = sem("gate_diff")
    gate_exp = sem("gate_exp")
    chosen_set = sem("chosen_set")
    slots_set = sem("slots_set")
    dispatched = sem("dispatched")
    bcol_in = sem("bcol_in")
    bcol_chain = sem("bcol_chain")
    bcol_set = sem("bcol_set")
    bcol_out = sem("bcol_out")
    brow_in = sem("brow_in")
    dummy_set = sem("dummy_set")
    base_set = sem("base_set")
    w_in = sem("w_in")
    table_chain = sem("table_chain")
    pads_set = sem("pads_set")
    padded = sem("padded")
    tables_set = sem("tables_set")
    xg_in = [sem(f"xg_in{n}") for n in range(DEEP)]
    meta_set = sem("meta_set")
    xgt_full = sem("xgt_full")
    xgt_set = sem("xgt_set")
    h_full = sem("h_full")
    functions_set = sem("functions_set")
    silu_set = sem("silu_set")
    acts_set = sem("acts_set")
    y_full = sem("y_full")
    y_set = sem("y_set")
    y_out = sem("y_out")
    w1_in = [sem(f"w1_in{n}") for n in range(DEEP)]
    rows_doubled = sem("rows_doubled")
    dummy_out = sem("dummy_out")
    dispatch_started = sem("dispatch_started")
    stats_seen = sem("stats_seen")
    logits_seen = sem("logits_seen")
    split_started = sem("split_started")
    add_started = sem("add_started")
    apply_started = sem("apply_started")
    load_started = sem("load_started")
    double_started = sem("double_started")

    LAST = nb - 1
    STORES = (NPARTS, 1)

    PROLOGUE = ["xt0", "q0", "k0", "v0", "xt1", "q1", "k1", "m0", "bias"]
    SLOT = ["gate", "rank", "m_mid", "v", "xt", "q", "k", "out", "m_end", "rowst"]
    TAIL = ["gate_a", "rank_a", "out", "rowst", "gate_b", "rank_b"]

    def slot_jobs(b):
        jobs = list(SLOT)
        if b == 0:
            jobs = [j for j in jobs if j not in ("out", "rowst")]
        if b < 2:
            jobs = [j for j in jobs if j not in ("gate", "rank")]
        if b + 2 > LAST:
            jobs = [j for j in jobs if j not in ("xt", "q", "k")]
        if b == LAST:
            jobs = [j for j in jobs if j not in ("v", "m_end")]
        return jobs

    def misc_count(seq, job):
        if not seq.known:
            return len(PROLOGUE) + len(slot_jobs(0)) + len(slot_jobs(1)) + len(SLOT) * (seq.b - 2) + SLOT.index(job) + 1
        before = len(PROLOGUE) + sum(len(slot_jobs(b)) for b in range(min(seq.b, nb)))
        return before + (TAIL if seq.b > LAST else slot_jobs(seq.b)).index(job) + 1

    def out_count(seq):
        return misc_count(seq.next(1), "out")

    def head_no(seq, h):
        return H * seq.b + h

    def slots(emit, eng):
        emit(Seq(0, 0))
        emit(Seq(0, 1))
        if nb > 4:
            with eng.Fori(1, nb // 2 - 1) as i:
                emit(Seq(i, 0))
                emit(Seq(i, 1))
        emit(Seq(nb // 2 - 1, 0))
        emit(Seq(nb // 2 - 1, 1))

    def ahead(seq, h):
        g = h + LEAD
        s = seq.next(g // H)
        return None if s.known and s.b > LAST else (s, g % H)

    def s1_banks(seq, h):
        own = [s1p[n][:] for n in range(2)]
        return own + [s2p[1][:, n, :] for n in range(2)] if seq.known and seq.b == 0 and h < LEAD else own

    def unit_buf(seq, h):
        return 2 * seq.p + h // UH

    turns = -(-ntiles // DEEP)

    def tile_loop(emit, eng):
        emit(0)
        with eng.Fori(1, turns - 1) as m:
            emit(m)
        emit(turns - 1)

    def at_least(eng, sem_, value, from_):
        if not isinstance(from_, int) or from_ >= 0:
            eng.wait_ge(sem_, value)

    by_tile = lambda ap: ap.rearrange("(j p) r -> p j r", p=P)

    def experts_loads(sp):
        sp.wait_ge(pv_done, 4 * T * nb)
        sp.dma_start(b2rows.rearrange("s (e f) -> s e f", e=E)[:, :, 0:D], b_scr[:, E * DFF:].rearrange("s (e d) -> s e d", e=E)).then_inc(brow_in, 16)
        sp.wait_ge(pads_set, 2)
        for e in range(E):
            row = sp.value_load(tab_pad[0:1, e:e + 1], min_val=0, max_val=E * region)
            sp.dma_start(by_tile(disp[bass.ds(row, TILE)]), padrows[:]).then_inc(padded, 16)
        sp.wait_ge(brow_in, 32)
        sp.wait_ge(w_in, 32)
        sp.wait_ge(tables_set, 1)
        sp.wait_ge(padded, 16 * (E + 1))
        sp.wait_ge(dispatched, 16 * TOPK * T * nb)

        def load_tile(n, k):
            row = sp.value_load(tab_row[0:1, bass.ds(n, 1)], min_val=0, max_val=E * region)
            at_least(sp, xgt_full, n - DEEP + 1, n - DEEP)
            at_least(sp, meta_set, n - DEEP + 1, n - DEEP)
            sp.dma_start(xg[k], by_tile(disp[bass.ds(row, TILE)])).then_inc(xg_in[k], 16)

        def load_w1(n, k):
            off = sp.value_load(tab_off[0:1, bass.ds(n, 1)], min_val=0, max_val=(E - 1) * DFF)
            at_least(sp, h_full, n - DEEP + 1, n - DEEP)
            sp.dma_start(w1t[k], w1[:, bass.ds(off, DFF)]).then_inc(w1_in[k], 16)
            sp.dma_start(b1t[k], b1rows[:, bass.ds(off, DFF)]).then_inc(w1_in[k], 16)

        for n in range(DEEP):
            load_tile(n, n)
            if n < 3:
                load_w1(n, n)

        def turn(m):
            for k in range(DEEP):
                n = DEEP * m + k
                left = table - n if isinstance(n, int) else 2 * DEEP
                if left > DEEP:
                    load_tile(n + DEEP, k)
                if left > 3 + table - ntiles:
                    load_w1(n + 3, (k + 3) % DEEP)

        tile_loop(turn, sp)
        sp.wait_ge(y_out, 32 * ntiles)
        for k in range(DEEP):
            sp.wait_ge(xg_in[k], 16 * turns)

    def experts_products(pe):
        pe.wait_ge(w_in, 32)
        pe.wait_ge(brow_in, 32)
        pe.wait_ge(bcol_set, 2)
        pe.wait_ge(tables_set, 1)

        def transpose_rows(n, k, m):
            pe.wait_ge(xg_in[k], 16 * (m + 1))
            at_least(pe, xgt_set, n - 1, n - 2)
            for j in range(TJ):
                mm = nc.tensor.transpose(xgtp[k % 2][:, P * j:P * j + P], xg[k][:, j, 0:D], ident[:])
            mm.then_inc(xgt_full, 1)

        def hidden(n, k, m):
            pe.wait_ge(w1_in[k], 32 * (m + 1))
            pe.wait_ge(xgt_set, n + 1)
            at_least(pe, silu_set, n - 1, n - 2)
            for f in range(FT):
                nc.tensor.matmul(hp[k % 2][:, f, :], w1t[k][:, P * f:P * f + P], xgt[k % 2], start=True, stop=False)
                mm = nc.tensor.matmul(hp[k % 2][:, f, :], b1t[k][:, P * f:P * f + P], ones3[:], start=False, stop=True)
            mm.then_inc(h_full, 1)

        def back(n, k):
            off = pe.value_load(tab_off[0:1, bass.ds(n, 1)], min_val=0, max_val=(E - 1) * DFF)
            pe.wait_ge(acts_set, n + 1)
            at_least(pe, y_set, n - 1, n - 2)
            for j in range(TJ):
                for f in range(FT):
                    nc.tensor.matmul(yp[k % 2][:, j, :], acts[k % 2][:, f, P * j:P * j + P], w2[:, bass.ds(off + P * f, D)],
                                     start=(f == 0), stop=False)
                mm = nc.tensor.matmul(yp[k % 2][:, j, :], ones3[:, 0:P], b2rows[:, bass.ds(off, D)], start=False, stop=True)
            mm.then_inc(y_full, 1)

        for n in range(2):
            transpose_rows(n, n, 0)
        hidden(0, 0, 0)
        transpose_rows(2, 2, 0)
        hidden(1, 1, 0)

        def turn(m):
            for k in range(DEEP):
                n = DEEP * m + k
                left = ntiles - n if isinstance(n, int) else 2 * DEEP
                if left <= 0:
                    break
                if left > 3:
                    transpose_rows(n + 3, (k + 3) % DEEP, m + (k + 3) // DEEP)
                if left > 2:
                    hidden(n + 2, (k + 2) % DEEP, m + (k + 2) // DEEP)
                back(n, k)

        tile_loop(turn, pe)

    def experts_functions(act):
        act.wait_ge(tables_set, 1)

        def copy_rows(n, k):
            act.wait_ge(xgt_full, n + 1)
            at_least(act, h_full, n - 1, n - 2)
            nc.scalar.copy(xgt[k % 2], xgtp[k % 2]).then_inc(xgt_set, 1)

        def functions(n, k):
            act.wait_ge(h_full, n + 1)
            at_least(act, acts_set, n - 1, n - 2)
            nc.scalar.activation(gelu[k % 2], hp[k % 2], ACT.Gelu, scale=tab_gelu[:, bass.ds(n, 1)])
            nc.scalar.activation(tanh[k % 2], hp[k % 2], ACT.Tanh, scale=tab_half[:, bass.ds(n, 1)]).then_inc(functions_set, 1)

        for n in range(2):
            copy_rows(n, n)
        functions(0, 0)
        copy_rows(2, 2)
        functions(1, 1)

        def turn(m):
            for k in range(DEEP):
                n = DEEP * m + k
                left = ntiles - n if isinstance(n, int) else 2 * DEEP
                if left <= 0:
                    break
                if left > 3:
                    copy_rows(n + 3, (k + 3) % DEEP)
                if left > 2:
                    functions(n + 2, (k + 2) % DEEP)

        tile_loop(turn, act)

    def chain_on(eng, sem_, before, alone=None):
        done = [0]

        def link(ins):
            done[0] += 1
            ins.then_inc(sem_, 1)
            wait = eng.wait_ge(sem_, before + done[0])
            return wait.then_inc(alone, 1) if alone else wait
        return link

    def inverse_root(eng, n, chain, seq):
        link = chain_on(eng, chain, LN_STEPS * seq.b + 2, apply_started)
        a, y, yy = ln_a[n], ln_y[n], ln_t[n]
        link(eng.tensor_scalar(a[:], mv[n][:, :, 1], EPS, None, ALU.add))
        link(eng.tensor_scalar(y[:].bitcast(I32), a[:].bitcast(I32), -0.5, RSQRT_SEED, ALU.mult, ALU.add))
        for _ in range(NEWTON):
            link(eng.tensor_tensor(yy[:], y[:], y[:], ALU.mult))
            link(eng.tensor_tensor(yy[:], yy[:], a[:], ALU.mult))
            link(eng.tensor_scalar(yy[:], yy[:], -0.5, 1.5, ALU.mult, ALU.add))
            link(eng.tensor_tensor(y[:], yy[:], y[:], ALU.mult))

    def ln1_apply(eng, seq):
        eng.wait_ge(ln_chain, LN_STEPS * seq.b + 2).then_inc(apply_started, 1)
        inverse_root(eng, 0, ln_chain, seq)
        if not (seq.known and seq.b == 0):
            before = seq.next(-1)
            count = 1 if before.known and before.b == 0 else (
                5 if before.known and before.b == 1 else misc_count(before.next(-2), "xt"))
            eng.wait_ge(misc_full, count).then_inc(apply_started, 1)
        for t in range(T):
            ins = eng.tensor_scalar(xn[:, t, :], xin[seq.p][:, t, :], mv[0][:, t, 0:1], ln_y[0][:, t:t + 1],
                                    ALU.subtract, ALU.mult)
        ins.then_inc(xn_set, 1)

    def ln2_apply(eng, seq):
        eng.wait_ge(ln2_chain, LN_STEPS * seq.b + 2).then_inc(apply_started, 1)
        inverse_root(eng, 1, ln2_chain, seq)
        if not (seq.known and seq.b == 0):
            eng.wait_ge(base_set, seq.b)
            eng.wait_ge(dispatched, 16 * TOPK * T * seq.b).then_inc(apply_started, 1)
        for t in range(T):
            eng.tensor_scalar(rows[:, t, 0, 0:D], x2[:, t, :], mv[1][:, t, 0:1], ln_y[1][:, t:t + 1],
                              ALU.subtract, ALU.mult)
        eng.tensor_scalar(rows[:, :, :, ID_COL], numbers[:, C_IDS:C_IDS + T].rearrange("p (t o) -> p t o", o=1).to_broadcast((P, T, TOPK)),
                          token_base[:], None, ALU.add).then_inc(rows_set, 1)
        eng.wait_ge(rows_set, seq.b + 1).then_inc(apply_started, 1)
        eng.tensor_scalar(token_base[:], token_base[:], float(S), None, ALU.add).then_inc(base_set, 1)

    def normalise(eng, seq):
        eng.wait_ge(norm_in, 32 * (seq.b + 1))
        eng.tensor_tensor(ctxt[:], ctxt[:], rdenb[:], ALU.mult).then_inc(ctxt_set, 1)

    def split(eng, seq, k, count, src, parts):
        eng.wait_ge(misc_free, count)
        if not (seq.known and seq.b == 0):
            eng.wait_ge(qk_out[k], 16 * STORES[k] * seq.b).then_inc(split_started, 1)
        base = 6 * seq.b + 3 * k
        eng.tensor_copy(parts[:, 0, :], src[:]).then_inc(parts_chain, 1)
        eng.wait_ge(parts_chain, base + 1)
        eng.tensor_tensor(rest[:], src[:], parts[:, 0, :], ALU.subtract).then_inc(parts_chain, 1)
        eng.wait_ge(parts_chain, base + 2).then_inc(split_started, 1)
        eng.tensor_copy(parts[:, 1, :], rest[:]).then_inc(parts_chain, 1)
        eng.wait_ge(parts_chain, base + 3)
        eng.tensor_tensor(parts[:, 2, :], rest[:], parts[:, 1, :], ALU.subtract).then_inc(qk_parts, 1)

    def experts_vectors(dve):
        link = chain_on(dve, table_chain, 0)

        link(nc.vector.tensor_copy(tab_pad, counts[:])).then_inc(pads_set, 1)
        link(nc.vector.tensor_tensor(cnt, counts[:], numbers[:, C_BASE:C_BASE + E], ALU.subtract))
        link(nc.vector.tensor_scalar(cnt, cnt, 1.0 / TILE, None, ALU.mult))
        wide = (P, E, per_expert)
        link(nc.vector.tensor_tensor(few, numbers[:, C_IOTA:C_IOTA + per_expert].rearrange("p (o n) -> p o n", o=1).to_broadcast(wide),
                                     cnt.rearrange("p (e o) -> p e o", o=1).to_broadcast(wide), ALU.is_lt))
        link(nc.vector.tensor_reduce(tcount, few, AXX, ALU.add))
        link(nc.vector.memset(one8, 1.0))
        link(nc.vector.tensor_tensor_scan(tsum, one8, tcount, 0.0, ALU.mult, ALU.add))
        wide = (P, table, E)
        iota = numbers[:, C_IOTA:C_IOTA + table]
        per_e = lambda ap: ap.rearrange("p (o e) -> p o e", o=1).to_broadcast(wide)
        link(nc.vector.tensor_tensor(before, per_e(tsum), iota.rearrange("p (n o) -> p n o", o=1).to_broadcast(wide), ALU.is_le))
        link(nc.vector.tensor_tensor(weighed, before, per_e(tcount), ALU.mult))
        link(nc.vector.tensor_reduce(tab_t, weighed[:, :, 0:E - 1], AXX, ALU.add))
        link(nc.vector.tensor_tensor(tab_t, iota, tab_t, ALU.subtract))
        link(nc.vector.tensor_scalar(tab_t, tab_t, float(TILE), None, ALU.mult))
        link(nc.vector.tensor_tensor(weighed, before, per_e(numbers[:, C_SIGN:C_SIGN + E]), ALU.mult))
        link(nc.vector.tensor_reduce(tab_e, before[:, :, 0:E - 1], AXX, ALU.add))
        link(nc.vector.tensor_scalar(tab_off, tab_e, float(DFF), None, ALU.mult))
        link(nc.vector.tensor_reduce(tab_silu, weighed[:, :, 0:E - 1], AXX, ALU.add))
        link(nc.vector.tensor_scalar(tab_gelu, tab_silu, -1.0, 1.0, ALU.mult, ALU.add))
        link(nc.vector.tensor_scalar(tab_half, tab_silu, 0.5, None, ALU.mult))
        link(nc.vector.scalar_tensor_tensor(tab_r, tab_e, float(region), tab_t, ALU.mult, ALU.add))
        link(nc.vector.tensor_scalar(tab_t, tab_r, -1.0, float(E * region), ALU.mult, ALU.add))
        link(nc.vector.tensor_tensor(tab_t, tab_t, before[:, :, E - 1], ALU.mult))
        nc.vector.tensor_tensor(tab_row, tab_r, tab_t, ALU.add).then_inc(tables_set, 1)

        def take_numbers(n, k, m):
            dve.wait_ge(xg_in[k], 16 * (m + 1))
            at_least(dve, y_out, 32 * (n - DEEP + 1), n - DEEP)
            nc.vector.tensor_copy(ids[k], xg[k][:, :, ID_COL])
            nc.vector.tensor_copy(wts[k], xg[k][:, :, W_COL]).then_inc(meta_set, 1)

        def activations(n, k):
            dve.wait_ge(functions_set, n + 1)
            nc.vector.scalar_tensor_tensor(tanh[k % 2], tanh[k % 2], tab_silu[:, bass.ds(n, 1)], hp[k % 2], ALU.add, ALU.mult).then_inc(silu_set, 1)
            dve.wait_ge(silu_set, n + 1)
            at_least(dve, y_full, n - 1, n - 2)
            nc.vector.scalar_tensor_tensor(acts[k % 2], tanh[k % 2], 0.5, gelu[k % 2], ALU.mult, ALU.add).then_inc(acts_set, 1)

        def weigh(n, k):
            dve.wait_ge(y_full, n + 1)
            at_least(dve, y_out, 32 * (n - 1), n - 2)
            for j in range(TJ):
                ins = nc.vector.tensor_scalar(yw[k % 2][:, j, :], yp[k % 2][:, j, :], wts[k][:, j:j + 1], None, ALU.mult)
            ins.then_inc(y_set, 1)

        dve.wait_ge(tables_set, 1)
        for n in range(2):
            take_numbers(n, n, 0)
        activations(0, 0)

        def turn(m):
            for k in range(DEEP):
                n = DEEP * m + k
                left = ntiles - n if isinstance(n, int) else 2 * DEEP
                if left <= 0:
                    break
                if left > 1:
                    activations(n + 1, (k + 1) % DEEP)
                weigh(n, k)
                if left > 2:
                    take_numbers(n + 2, (k + 2) % DEEP, m + (k + 2) // DEEP)

        tile_loop(turn, dve)

    def experts_scatters(pool):
        pool.wait_ge(x2_out, 16 * nb)
        pool.wait_ge(dummy_out, 16)

        def turn(m):
            for k in range(DEEP):
                n = DEEP * m + k
                if isinstance(n, int) and n >= ntiles:
                    break
                at_least(pool, y_out, 32 * n, n - 1)
                pool.wait_ge(y_set, n + 1).then_inc(add_started, 1)
                for j in range(TJ):
                    pool.indirect_dma_start(out, bass.IndirectOffsetOnAxis(ids[k][:, j:j + 1], 0), yw[k % 2][:, j, :], None, compute_op=ALU.add).then_inc(y_out, 16)

        tile_loop(turn, pool)

    block = ctx.enter_context(nc.Block())

    @block.sync
    def _(sp):
        for dst, src in ((rel[:], io["rel"]), (onehot, io["onehot"]), (stepmask, io["stepmask"])):
            sp.dma_start(dst, src).then_inc(bias_consts_in, 16)

        def load_x(seq):
            if not (seq.known and seq.b < 2):
                sp.wait_ge(xn_set, seq.b - 1)
            sp.dma_start(xin[seq.p][:], io["x"][bass.ds(seq.b, 1)].rearrange("o (t p) d -> p (o t) d", p=P)).then_inc(x_in[seq.p], 16)

        def store_parts(seq):
            sp.wait_ge(qk_parts, 2 * seq.b + 1)
            for i in range(NPARTS):
                sp.dma_start(q_scr[seq.p][i].rearrange("j p s -> p j s"), qparts[:, i:i + 1, :].to_broadcast((P, NPARTS, S))).then_inc(qk_out[0], 16)
            sp.wait_ge(qk_parts, 2 * seq.b + 2)
            sp.dma_start(k_scr[seq.p].rearrange("i p s -> p i s"), kparts[:]).then_inc(qk_out[1], 16)

        def load_stack(seq, half):
            buf = 2 * seq.p + half
            if not (seq.known and seq.b < 2):
                sp.wait_ge(s2_full, 2 * (H * (seq.b - 2) + UH * (half + 1)))
            for k in range(2):
                sp.wait_ge(qk_out[k], 16 * STORES[k] * (seq.b + 1)).then_inc(load_started, 1)
            heads = slice(UH * half, UH * half + UH)
            sp.dma_start(qst[buf][0:STACK], q_scr[seq.p].rearrange("i j (d h) s -> (i j d) h s", h=H)[:, heads, :]).then_inc(stack_in[buf], 16)
            for i in range(NPARTS):
                r = NPARTS * HD * i
                sp.dma_start(kst[buf][r:r + NPARTS * HD], k_scr[seq.p].rearrange("j (d h) s -> (j d) h s", h=H)[:, heads, :]).then_inc(stack_in[buf], 16)

        def store_ctx(seq, g):
            sp.wait_ge(ctx_copied, 4 * seq.b + g + 1)
            sp.dma_start(ctx_scr[seq.p][g], ctxu[g % 2][:]).then_inc(ctx_out[g % 2], 16)

        load_x(Seq(0, 0))
        load_x(Seq(0, 1))
        static_rows = io["kstatic"].rearrange("r (o s) -> r o s", o=1).to_broadcast((ROWS2 - STACK, UH, S))
        sp.wait_ge(dummy_set, 1)
        sp.dma_start(by_tile(out[tokens:]), padrows[:, :, 0:D]).then_inc(dummy_out, 16)
        for dst, src in ((ident[:], io["ident"]), (wq[:], io["wq"]), (wk[:], io["wk"]),
                         (bq[:], io["bq"].rearrange("(p o) -> p o", o=1)), (bk[:], io["bk"].rearrange("(p o) -> p o", o=1))):
            sp.dma_start(dst, src).then_inc(proj_in, 16)
        sp.wait_ge(bias_sb, 1)
        sp.dma_start(bias_scr, bias_rows).then_inc(bias_out, 16)
        for dst, src in ((wv[:], io["wv"]), (bv[:], io["bv"].rearrange("(p o) -> p o", o=1)),
                         (pick[:], io["pick"].rearrange("k p n -> p k n")), (numbers[:], io["numbers"])):
            sp.dma_start(dst, src).then_inc(consts_in, 16)
        sp.wait_ge(bias_out, 16)
        sp.dma_start(toep1, bass.AP(bias_scr.tensor, FWD, [[1, P], [S, H], [1, B1W]])).then_inc(toep_in, 16)
        for lo in (0, HALF):
            sp.dma_start(toep2[lo:lo + HALF], bass.AP(bias_scr.tensor, 0, [[1, HALF], [S, H], [1, BW]])).then_inc(toep_in, 16)
        for half in range(2):
            sp.wait_ge(steps_set, half + 1)
            for buf in (half, half + 2):
                sp.dma_start(qst[buf][STACK:ROWS1], steprows).then_inc(steps_out[half], 16)
            if half == 0:
                sp.dma_start(kst[0][STACK:ROWS2], static_rows).then_inc(static_in[0], 16)
                store_parts(Seq(0, 0))
                load_stack(Seq(0, 0), 0)
        for buf in range(1, 4):
            sp.dma_start(kst[buf][STACK:ROWS2], static_rows).then_inc(static_in[1], 16)
        load_stack(Seq(0, 0), 1)
        for dst, src in ((wg[:], io["wg"]), (order[:], io["order"]), (wo[:], io["wo"]),
                         (bg[:], io["bg"].rearrange("(o e) -> o e", o=1).to_broadcast((P, E))),
                         (bo[:], io["bo"].rearrange("(o d) -> o d", o=1).to_broadcast((P, D)))):
            sp.dma_start(dst, src).then_inc(late_consts_in, 16)
        sp.wait_ge(pads_set, 1)
        sp.dma_start(by_tile(disp[E * region:]), padrows[:]).then_inc(padded, 16)
        sp.dma_start(b1col[:], io["b1"].rearrange("e (a f) -> (e a) f", a=P // E)).then_inc(bcol_in, 16)
        sp.dma_start(b2col[:], io["b2"].rearrange("e (a d) -> (e a) d", a=P // E)).then_inc(bcol_in, 16)
        store_parts(Seq(0, 1))
        load_stack(Seq(0, 1), 0)
        sp.wait_ge(bcol_set, 2)
        nb1, nb2 = E * DFF // P, E * D // P
        sp.dma_start(b_scr[:, 0:E * DFF].rearrange("s (p f) -> p s f", p=P), bcols[:, :, 0:nb1]).then_inc(bcol_out, 16)
        sp.dma_start(b_scr[:, E * DFF:].rearrange("s (p f) -> p s f", p=P), bcols[:, :, nb1:]).then_inc(bcol_out, 16)

        def slot(seq):
            prev, nxt, inp = seq.next(-1), seq.next(1), seq.next(2)
            first = seq.known and seq.b == 0
            last = seq.known and seq.b == LAST
            inputs = not (seq.known and seq.b + 2 > LAST)
            if inputs:
                load_x(inp)
            if not first:
                if not (seq.known and seq.b == 1):
                    sp.wait_ge(misc_free, out_count(seq.next(-2)))
                sp.dma_start(xres[:], io["x"][bass.ds(prev.b, 1)].rearrange("o (t p) d -> p (o t) d", p=P)).then_inc(xres_in, 16)
                store_ctx(prev, 2)
            if not last:
                load_stack(nxt, 1)
            if not first:
                finish_ctx(prev)
            store_ctx(seq, 0)
            if not first:
                store_x2(prev)
            if inputs:
                store_parts(inp)
                load_stack(inp, 0)
            store_ctx(seq, 1)
            if last:
                load_expert_weights()

        def finish_ctx(seq):
            store_ctx(seq, 3)
            sp.wait_ge(ctx_out[0], 32 * (seq.b + 1))
            sp.wait_ge(ctx_out[1], 32 * (seq.b + 1))
            heads = ctx_scr[seq.p].rearrange("g (c r) s -> (g c) r s", r=32)
            sp.dma_start(den[:], heads[:, HD, :].rearrange("h (j n) -> h j n", j=HD)).then_inc(den_in, 16)
            sp.dma_start(ctxt[:], heads[:, 0:HD, :]).then_inc(norm_in, 16)
            sp.wait_ge(rden_set, seq.b + 1)
            sp.dma_start(rden_scr[seq.p], rden[:]).then_inc(rden_out, 16)
            sp.wait_ge(rden_out, 16 * (seq.b + 1))
            sp.dma_start(rdenb[:], rden_scr[seq.p].rearrange("(h o j) n -> h o (j n)", j=HD, o=1).to_broadcast((H, HD, S))).then_inc(norm_in, 16)

        def store_x2(seq):
            sp.wait_ge(misc_free, out_count(seq))
            sp.dma_start(out[0:tokens].rearrange("(b t p) d -> b p t d", p=P, t=T)[bass.ds(seq.b, 1)].rearrange("o p t d -> p (o t) d"),
                         x2[:]).then_inc(x2_out, 16)

        def load_expert_weights():
            sp.wait_ge(s2_full, 2 * H * LAST)
            sp.wait_ge(bcol_out, 32)
            sp.wait_ge(pv_done, 4 * T * LAST)
            sp.dma_start(b1rows, b_scr[:, 0:E * DFF]).then_inc(brow_in, 16)
            sp.dma_start(w1.rearrange("d (e f) -> d e f", e=E), io["w1"].rearrange("e d f -> d e f")).then_inc(w_in, 16)
            sp.dma_start(w2.rearrange("f (e d) -> f e d", d=D), io["w2"].rearrange("e (t f) d -> f (e t) d", f=P)).then_inc(w_in, 16)

        slots(slot, sp)
        end = Seq(LAST // 2, LAST % 2)
        sp.wait_ge(misc_free, out_count(Seq((LAST - 1) // 2, (LAST - 1) % 2)))
        sp.dma_start(xres[:], io["x"][LAST:LAST + 1].rearrange("o (t p) d -> p (o t) d", p=P)).then_inc(xres_in, 16)
        store_ctx(end, 2)
        finish_ctx(end)
        store_x2(end)
        sp.wait_ge(x2_out, 16 * nb)
        experts_loads(sp)

    @block.tensor
    def _(pe):
        filled = [0]

        def open_misc(count):
            if not (isinstance(count, int) and count == 1):
                pe.wait_ge(misc_free, count - 1)

        def job_xt(seq, count):
            open_misc(count)
            pe.wait_ge(xn_set, seq.b + 1)
            for t in range(T):
                mm = nc.tensor.transpose(misc[:, P * t:P * t + P], xn[:, t, :], ident[:])
            mm.then_inc(misc_full, 1)

        def job_project(seq, count, w, xt_count):
            open_misc(count)
            pe.wait_ge(misc_free, xt_count)
            nc.tensor.matmul(misc[:], w[:], xnt[seq.p][:], start=True, stop=True).then_inc(misc_full, 1)

        def job_v(seq, count):
            open_misc(count)
            for t in range(T):
                mm = nc.tensor.matmul(misc[:, D * t:D * t + D], xnt[seq.p][:, P * t:P * t + P], wv[:], start=True, stop=True)
            mm.then_inc(misc_full, 1)

        def job_m(seq, half, count):
            open_misc(count)
            pe.wait_ge(s1_free, 4 * (head_no(seq, UH * half) + UH))
            nc.tensor.transpose(misc[0:UH * T, 0:P], negm[half][:], ident[:]).then_inc(misc_full, 1)

        def job_out(seq, count):
            open_misc(count)
            pe.wait_ge(ctxt_set, seq.b + 1)
            for t in range(T):
                mm = nc.tensor.matmul(misc[:, D * t:D * t + D], ctxt[:, P * t:P * t + P], wo[:], start=True, stop=True)
            mm.then_inc(misc_full, 1)

        def job_rowst(seq, count):
            open_misc(count)
            pe.wait_ge(rows_set, seq.b + 1)
            for t in range(T):
                mm = nc.tensor.transpose(misc[:, P * t:P * t + P], rows[:, t, 0, 0:D], ident[:])
            mm.then_inc(misc_full, 1)

        def job_gate(seq, count):
            open_misc(count)
            for t in range(T):
                mm = nc.tensor.matmul(misc[:, E * t:E * t + E], rowst[:, P * t:P * t + P], wg[:], start=True, stop=True)
            mm.then_inc(misc_full, 1)

        def job_rank(seq, count):
            open_misc(count)
            pe.wait_ge(chosen_set, seq.b + 1)
            nc.tensor.matmul(misc[:, 0:(T + 1) * E], order[:, 0, :], chosenb[:].rearrange("p t e -> p (t e)"), start=True, stop=False)
            for d in range(1, T + 1):
                n = T + 1 - d
                mm = nc.tensor.matmul(misc[:, E * d:E * (T + 1)], order[:, 1, :], chosenb[:, 0:n, :], start=False, stop=(d == T))
            mm.then_inc(misc_full, 1)

        def max_scores(seq, h, tiles):
            buf, hh = unit_buf(seq, h), h % UH
            if h % UH == 0 and tiles[0] == 0:
                pe.wait_ge(stack_in[buf], (1 + NPARTS) * 16 * (seq.i + 1))
            for t in tiles:
                n = 4 * head_no(seq, h) + t
                banks = len(s1_banks(seq, h))
                if not (seq.known and n < banks):
                    pe.wait_ge(s1_free, n - banks + 1)
                lo = max(0, P * t - HALF)
                bank = s1_banks(seq, h)[t % banks]
                nc.tensor.matmul(bank, qst[buf][0:ROWS1, hh, P * t:P * t + P], kst[buf][0:ROWS1, hh, :],
                                 start=True, stop=False)
                nc.tensor.matmul(bank[:, lo:P * t + P], pick[:, 2, :], band1[:, h, lo - P * t + HALF:],
                                 start=False, stop=True).then_inc(s1_full, 1)

        def exp_scores(seq, h, pair):
            buf, hh = unit_buf(seq, h), h % UH
            n = 2 * head_no(seq, h) + pair
            if h % UH == 0 and pair == 0:
                pe.wait_ge(m_in[buf], 16 * (seq.i + 1))
            if not (seq.known and n < 2):
                pe.wait_ge(exp_done, n - 1)
            if seq.known and n == 1:
                pe.wait_ge(s1_free, 4 * LEAD)
            for j in range(2):
                t = 2 * pair + j
                out = s2p[pair][:, j, :]
                nc.tensor.matmul(out, kst[buf][:, hh, P * t:P * t + P], qst[buf][:, hh, :], start=True, stop=False)
                for g in range(2):
                    q0 = P * t + HALF * g
                    w = min(BW, S - q0)
                    mm = nc.tensor.matmul(out[:, q0:q0 + w], pick[:, g, :], band2[:, h, 0:w], start=False, stop=(g == 1))
            mm.then_inc(s2_full, 1)

        def weigh_values(seq, h):
            t, par = h % 4, (h // 4) % 2
            g = 4 * seq.b + h // 4
            if t == 0:
                pe.wait_ge(exp_done, 8 * (g + 1))
                if not (seq.known and g == 0):
                    pe.wait_ge(ctx_copied, g)
            for c in range(4):
                mm = nc.tensor.matmul(pvp[32 * c:32 * c + 32, :], vp[seq.p][:, t, 4 * (h // 4) + c, :],
                                      pt[par][:, c, t, :], start=(t == 0), stop=(t == T - 1))
            mm.then_inc(pv_done, 1)

        pe.wait_ge(bias_consts_in, 48)
        nc.tensor.matmul(s2p[0][0:H, 0, :], rel[:], onehot, start=True, stop=True).then_inc(bias_ps, 1)
        nc.tensor.matmul(s2p[1][0:STEPS, 0, 0:H], onehot[:, 0:1].to_broadcast((BUCKETS, STEPS)), rel[:], start=True, stop=True).then_inc(bias_ps, 1)
        pe.wait_ge(proj_in, 5 * 16)
        k = PROLOGUE.index("xt0") + 1
        job_xt(Seq(0, 0), k)
        job_project(Seq(0, 0), k + 1, wq, k)
        job_project(Seq(0, 0), k + 2, wk, k)
        pe.wait_ge(consts_in, 4 * 16)
        job_v(Seq(0, 0), k + 3)
        pe.wait_ge(static_in[0], 16)
        pe.wait_ge(steps_out[0], 32)
        pe.wait_ge(band1_set, 1)
        k = PROLOGUE.index("xt1") + 1
        for h in range(UH):
            max_scores(Seq(0, 0), h, range(T))
            if h == 0:
                job_xt(Seq(0, 1), k)
            if h == 1:
                job_project(Seq(0, 1), k + 1, wq, k)
            if h == 2:
                job_project(Seq(0, 1), k + 2, wk, k)
        job_m(Seq(0, 0), 0, PROLOGUE.index("m0") + 1)
        for h in range(UH, LEAD):
            if h == LEAD - 1:
                pe.wait_ge(late_consts_in, 5 * 16)
                open_misc(PROLOGUE.index("bias") + 1)
                nc.tensor.matmul(misc[:, 0:D], bv[:].to_broadcast((P, P)), wo[:], start=True, stop=True).then_inc(misc_full, 1)
            if h == UH:
                pe.wait_ge(static_in[1], 48)
                pe.wait_ge(steps_out[1], 32)
            max_scores(Seq(0, 0), h, range(T))
        pe.wait_ge(band_set, 1)

        def slot(seq):
            prev, nxt, inp = seq.next(-1), seq.next(1), seq.next(2)
            first = seq.known and seq.b == 0
            last = seq.known and seq.b == LAST
            inputs = not (seq.known and seq.b + 2 > LAST)
            for h in range(H):
                exp_scores(seq, h, 0)
                lead = ahead(seq, h)
                if lead:
                    max_scores(*lead, (0,))
                if h == 0 and not (seq.known and seq.b < 2):
                    job_gate(seq.next(-2), misc_count(seq, "gate"))
                if h == 2 and not (seq.known and seq.b < 2):
                    job_rank(seq.next(-2), misc_count(seq, "rank"))
                if h == 4:
                    job_m(seq, 1, misc_count(seq, "m_mid"))
                if h == 6 and not last:
                    job_v(nxt, misc_count(seq, "v"))
                if inputs:
                    if h == 8:
                        job_xt(inp, misc_count(seq, "xt"))
                    if h == 9:
                        job_project(inp, misc_count(seq, "q"), wq, misc_count(seq, "xt"))
                    if h == 10:
                        job_project(inp, misc_count(seq, "k"), wk, misc_count(seq, "xt"))
                if h == 12 and not last:
                    job_m(nxt, 0, misc_count(seq, "m_end"))
                if not first:
                    if h == 11:
                        job_out(prev, misc_count(seq, "out"))
                    if h == 15:
                        job_rowst(prev, misc_count(seq, "rowst"))
                behind = (seq, h - 4) if h >= 4 else (prev, h + 12)
                if lead:
                    max_scores(*lead, (1,))
                exp_scores(seq, h, 1)
                if lead:
                    max_scores(*lead, (2,))
                if h >= 4 or not first:
                    weigh_values(*behind)
                if lead:
                    max_scores(*lead, (3,))

        slots(slot, pe)
        end = Seq(LAST // 2, LAST % 2)
        for h in range(4):
            weigh_values(end, h + 12)
        job_gate(end.next(-1), misc_count(end.next(1), "gate_a"))
        job_rank(end.next(-1), misc_count(end.next(1), "rank_a"))
        job_out(end, out_count(end))
        job_rowst(end, misc_count(end.next(1), "rowst"))
        job_gate(end, misc_count(end.next(1), "gate_b"))
        job_rank(end, misc_count(end.next(1), "rank_b"))
        experts_products(pe)

    @block.scalar
    def _(act):
        def copy_xt(seq, count):
            act.wait_ge(misc_full, count)
            nc.scalar.copy(xnt[seq.p][:], misc[:]).then_inc(misc_free, 1)

        def copy_q(seq, count):
            act.wait_ge(misc_full, count)
            if not (seq.known and seq.b == 0):
                act.wait_ge(qk_parts, 2 * seq.b - 1)
            nc.scalar.activation(q32[:], misc[:], ACT.Identity, bias=bqs[:], scale=HD ** -0.5).then_inc(misc_free, 1)

        def copy_k(seq, count):
            act.wait_ge(misc_full, count)
            if not (seq.known and seq.b == 0):
                act.wait_ge(qk_parts, 2 * seq.b)
            nc.scalar.activation(k32[:], misc[:], ACT.Identity, bias=bk[:], scale=1.0).then_inc(misc_free, 1)

        def copy_v(seq, count):
            act.wait_ge(misc_full, count)
            if seq.known and seq.b == 0:
                act.wait_ge(ones_set, 1)
            if not (seq.known and seq.b < 2):
                act.wait_ge(pv_done, 16 * (seq.b - 1))
            nc.scalar.copy(vp[seq.p][:, :, :, 0:HD], misc[:].rearrange("p (t h d) -> p t h d", t=T, h=H)).then_inc(misc_free, 1)

        def copy_rowst(seq, count):
            act.wait_ge(misc_full, count)
            nc.scalar.copy(rowst[:], misc[:]).then_inc(misc_free, 1)

        def gate_exponent(seq):
            act.wait_ge(gate_diff, seq.b + 1)
            nc.scalar.activation(gate_e[:], gate_d[:], ACT.Exp).then_inc(gate_exp, 1)

        def store_maxima(seq, half):
            act.wait_ge(m_parts, 2 * seq.b + half + 1)
            act.dma_start(m_scr[half].rearrange("s g n -> g s n"), mparts[half][:]).then_inc(m_out[half], 16)

        def load_maxima(seq, half):
            buf = 2 * seq.p + half
            act.wait_ge(m_out[half], 16 * (seq.b + 1))
            if not (seq.known and seq.b < 2):
                act.wait_ge(s2_full, 2 * (H * (seq.b - 2) + UH * (half + 1)))
            act.dma_start(qst[buf][ROWS1:ROWS2].rearrange("s h n -> s (h n)"),
                          m_scr[half].rearrange("s g n -> s (g n)")).then_inc(m_in[buf], 16)

        def copy_ctx(seq, g):
            n = 4 * seq.b + g
            act.wait_ge(pv_done, 4 * (n + 1))
            if not (seq.known and n < 2):
                act.wait_ge(ctx_out[g % 2], 16 * (2 * seq.b + g // 2))
            nc.scalar.copy(ctxu[g % 2][:], pvp[:]).then_inc(ctx_copied, 1)

        act.wait_ge(bias_ps, 1)
        nc.scalar.copy(bias_rows, s2p[0][0:H, 0, :]).then_inc(bias_sb, 1)
        act.wait_ge(proj_in, 5 * 16)
        nc.scalar.mul(bqs[:], bq[:], HD ** -0.5).then_inc(bqs_set, 1)
        act.wait_ge(bqs_set, 1)
        for n in range(2):
            k = PROLOGUE.index(f"xt{n}") + 1
            copy_xt(Seq(0, n), k)
            copy_q(Seq(0, n), k + 1)
            copy_k(Seq(0, n), k + 2)
            if n == 0:
                copy_v(Seq(0, 0), k + 3)
        act.wait_ge(band1_set, 1)
        act.wait_ge(band_set, 1)
        act.wait_ge(steps_out[0], 32)
        act.wait_ge(steps_out[1], 32)
        act.wait_ge(bias_out, 16)
        store_maxima(Seq(0, 0), 0)
        load_maxima(Seq(0, 0), 0)

        def slot(seq):
            prev, nxt, inp = seq.next(-1), seq.next(1), seq.next(2)
            first = seq.known and seq.b == 0
            last = seq.known and seq.b == LAST
            inputs = not (seq.known and seq.b + 2 > LAST)
            for h in range(H):
                g = 4 * seq.b + h // 4
                if h % 4 == 0 and not (seq.known and g < 2):
                    act.wait_ge(pv_done, 4 * (g - 1))
                for pair in range(2):
                    act.wait_ge(s2_full, 2 * head_no(seq, h) + pair + 1)
                    nc.scalar.activation(pt[(h // 4) % 2][:, h % 4, 2 * pair:2 * pair + 2, :], s2p[pair][:],
                                         ACT.Exp).then_inc(exp_done, 1)
                    if pair == 1:
                        if not last and h == 6:
                            copy_v(nxt, misc_count(seq, "v"))
                        if inputs and h == 8:
                            copy_xt(inp, misc_count(seq, "xt"))
                        if inputs and h == 9:
                            copy_q(inp, misc_count(seq, "q"))
                        if inputs and h == 10:
                            copy_k(inp, misc_count(seq, "k"))
                        if h == 1 and not (seq.known and seq.b < 2):
                            gate_exponent(seq.next(-2))
                        if h == 5:
                            store_maxima(seq, 1)
                        if h == 6:
                            load_maxima(seq, 1)
                        if h == 13 and not last:
                            store_maxima(nxt, 0)
                        if h == 14 and not last:
                            load_maxima(nxt, 0)
                    if pair == 0 and h == 15 and not first:
                        copy_rowst(prev, misc_count(seq, "rowst"))
                    if pair == 0 and h % 4 == 0:
                        if h >= 8:
                            copy_ctx(seq, h // 4 - 2)
                        elif not first:
                            copy_ctx(prev, h // 4 + 2)

        slots(slot, act)
        end = Seq(LAST // 2, LAST % 2)
        copy_ctx(end, 2)
        copy_ctx(end, 3)
        gate_exponent(end.next(-1))
        copy_rowst(end, misc_count(end.next(1), "rowst"))
        gate_exponent(end)
        experts_functions(act)

    @block.vector
    def _(dve):
        def chain_of(sem_, before):
            return chain_on(dve, sem_, before)

        def measure(n, src, link):
            for t in range(T):
                ins = nc.vector.bn_stats(stats[n][:, t, :], src[:, t, :])
            link(ins).then_inc(stats_seen, 1)

        def collect(n, link):
            for t in range(T):
                ins = nc.vector.bn_aggr(mv[n][:, t, :], stats[n][:, t, :])
            link(ins)

        def ln1_measure(seq):
            dve.wait_ge(x_in[seq.p], 16 * (seq.i + 1))
            if not (seq.known and seq.b == 0):
                dve.wait_ge(xn_set, seq.b)
            link = chain_of(ln_chain, LN_STEPS * seq.b)
            measure(0, xin[seq.p], link)
            collect(0, link)

        def layernorm_rows(seq):
            ln1_measure(seq)
            ln1_apply(dve, seq)

        def ln2_measure(seq, count):
            dve.wait_ge(misc_free, count)
            if not (seq.known and seq.b == 0):
                dve.wait_ge(rows_set, seq.b)
            measure(1, x2, chain_of(ln2_chain, LN_STEPS * seq.b))

        def ln2_collect(seq):
            collect(1, chain_of(ln2_chain, LN_STEPS * seq.b + 1))

        GATE_STEPS = 10

        def take_top(seq, count):
            link = chain_of(gate_chain, GATE_STEPS * seq.b)
            dve.wait_ge(misc_full, count)
            nc.vector.tensor_tensor(logits[:], misc[:, 0:T * E].rearrange("p (t e) -> p t e", t=T),
                                    bg[:].rearrange("p (o e) -> p o e", o=1).to_broadcast((P, T, E)), ALU.add).then_inc(misc_free, 1)
            dve.wait_ge(misc_free, count).then_inc(logits_seen, 1)
            for t in range(T):
                ins = nc.vector.max(top[:, t, :], logits[:, t, :])
            link(ins)
            nc.vector.tensor_tensor(gate_d[:], top[:, :, 1], top[:, :, 0], ALU.subtract).then_inc(gate_diff, 1)

        def choose(seq):
            link = chain_of(gate_chain, GATE_STEPS * seq.b + 1)
            for t in range(T):
                ins = nc.vector.max_index(topi[:, t, :], top[:, t, :], logits[:, t, :])
            link(ins)
            link(nc.vector.tensor_copy(choice[:], topi[:, :, 0:TOPK]))
            link(nc.vector.tensor_tensor(
                chosen[:], choice[:].rearrange("p t (c o) -> p (t c) o", o=1).to_broadcast((P, T * TOPK, E)),
                numbers[:, C_IOTA8:C_IOTA8 + E].rearrange("p (o e) -> p o e", o=1).to_broadcast((P, T * TOPK, E)),
                ALU.is_equal))
            both = chosen[:].rearrange("p (t c) e -> p t c e", c=TOPK)
            nc.vector.tensor_tensor(chosenb[:, 0:T, :], both[:, :, 0, :], both[:, :, 1, :], ALU.add).then_inc(chosen_set, 1)

        def weigh_choices(seq):
            dve.wait_ge(gate_exp, seq.b + 1)
            n = GATE_STEPS * seq.b + 4

            def step(k, ins):
                ins.then_inc(gate_chain, 1)
                dve.wait_ge(gate_chain, n + k)

            step(1, nc.vector.tensor_scalar(gate_s[:], gate_e[:], 1.0, None, ALU.add))
            step(2, nc.vector.reciprocal(rows[:, :, 0, W_COL], gate_s[:]))
            step(3, nc.vector.tensor_tensor(rows[:, :, 1, W_COL], rows[:, :, 0, W_COL], gate_e[:], ALU.mult))

        def place_rows(seq, count):
            n = GATE_STEPS * seq.b + 7

            def step(k, ins):
                ins.then_inc(gate_chain, 1)
                dve.wait_ge(gate_chain, n + k)

            dve.wait_ge(misc_full, count)
            step(1, nc.vector.tensor_tensor(place[:], misc[:, 0:T * E].rearrange("p (t e) -> p t e", t=T),
                                            counts[:].rearrange("p (o e) -> p o e", o=1).to_broadcast((P, T, E)), ALU.add))
            nc.vector.tensor_tensor(counts[:], counts[:], misc[:, T * E:(T + 1) * E], ALU.add).then_inc(misc_free, 1)

        def find_places(seq):
            n = GATE_STEPS * seq.b + 7

            def step(k, ins):
                ins.then_inc(gate_chain, 1)
                dve.wait_ge(gate_chain, n + k)

            step(2, nc.vector.tensor_tensor(picked[:].rearrange("p (t c) e -> p t c e", c=TOPK), chosen[:].rearrange("p (t c) e -> p t c e", c=TOPK),
                                            place[:].rearrange("p t (o e) -> p t o e", o=1).to_broadcast((P, T, TOPK, E)), ALU.mult))
            step(3, nc.vector.tensor_reduce(slot_f[:], picked[:], AXX, ALU.add))
            if not (seq.known and seq.b == 0):
                dve.wait_ge(dispatched, 16 * TOPK * T * seq.b)
            nc.vector.tensor_copy(slot_i[:], slot_f[:]).then_inc(slots_set, 1)

        def split_m(seq, half, count):
            u = 2 * seq.b + half
            parts, src = mparts[half], misc[0:UH * T, 0:P]
            dve.wait_ge(misc_full, count)
            if not (seq.known and seq.b == 0):
                dve.wait_ge(m_out[half], 16 * seq.b)
            nc.vector.tensor_copy(parts[:, 0, :], src).then_inc(m_chain, 1)
            dve.wait_ge(m_chain, 2 * u + 1)
            nc.vector.tensor_tensor(mrest[:], src, parts[:, 0, :], ALU.subtract).then_inc(misc_free, 1)
            dve.wait_ge(misc_free, count)

        def split_rest_of_m(seq, half):
            u = 2 * seq.b + half
            parts = mparts[half]
            nc.vector.tensor_copy(parts[:, 1, :], mrest[:]).then_inc(m_chain, 1)
            dve.wait_ge(m_chain, 2 * u + 2)
            nc.vector.tensor_tensor(parts[:, 2, :], mrest[:], parts[:, 1, :], ALU.subtract).then_inc(m_parts, 1)

        def take_maxima(seq, h, tiles=range(T)):
            half = h // UH
            for t in tiles:
                dve.wait_ge(s1_full, 4 * head_no(seq, h) + t + 1)
                nc.vector.tensor_reduce(negm[half][:, (h % UH) * T + t:(h % UH) * T + t + 1], s1_banks(seq, h)[t % len(s1_banks(seq, h))], AXX,
                                        ALU.max, negate=True).then_inc(s1_free, 1)

        def invert_sums(seq):
            dve.wait_ge(den_in, 16 * (seq.b + 1))
            if not (seq.known and seq.b == 0):
                dve.wait_ge(rden_out, 16 * seq.b)
            nc.vector.reciprocal(rden[:], den[:]).then_inc(rden_set, 1)

        def add_residual(seq, count):
            dve.wait_ge(misc_full, count)
            dve.wait_ge(xres_set, seq.b + 1)
            if not (seq.known and seq.b == 0):
                dve.wait_ge(x2_out, 16 * seq.b)
                dve.wait_ge(rows_set, seq.b)
            nc.vector.tensor_tensor(x2[:].rearrange("p t d -> p (t d)"), misc[:], xres[:].rearrange("p t d -> p (t d)"),
                                    ALU.add).then_inc(misc_free, 1)

        chain = [0]

        def link(ins):
            chain[0] += 1
            ins.then_inc(bias_chain, 1)
            dve.wait_ge(bias_chain, chain[0])

        nc.vector.memset(token_base[:], 0.0)
        nc.vector.memset(chosenb[:], 0.0)
        nc.vector.memset(rows[:], 0.0)
        nc.vector.memset(padrows[:], 0.0).then_inc(dummy_set, 1)
        layernorm_rows(Seq(0, 0))
        dve.wait_ge(bias_ps, 2)
        dve.wait_ge(bias_consts_in, 48)
        link(nc.vector.tensor_copy(delta[:], s2p[1][0:STEPS, 0, 0:H]))
        link(nc.vector.tensor_copy(dparts[:, 0, :], delta[:]))
        link(nc.vector.tensor_tensor(drest[:], delta[:], dparts[:, 0, :], ALU.subtract))
        link(nc.vector.tensor_copy(dparts[:, 1, :], drest[:]))
        link(nc.vector.tensor_tensor(dparts[:, 2, :], drest[:], dparts[:, 1, :], ALU.subtract))
        link(nc.vector.tensor_scalar(dsel[:], dparts[:, 0, :], stepmask[:, S:S + 1], None, ALU.mult))
        for s in (1, 2):
            link(nc.vector.scalar_tensor_tensor(dsel[:], dparts[:, s, :], stepmask[:, S + s:S + s + 1], dsel[:], ALU.mult, ALU.add))
        for half in range(2):
            if half:
                k = PROLOGUE.index("q0") + 1
                split(dve, Seq(0, 0), 0, k, q32, qparts)
                split(dve, Seq(0, 0), 1, k + 1, k32, kparts)
                dve.wait_ge(steps_out[0], 32)
            for hh in range(UH):
                h = UH * half + hh
                ins = nc.vector.tensor_scalar(steprows[:, hh, :], stepmask[:, 0:S], dsel[:, h:h + 1], None, ALU.mult)
            ins.then_inc(steps_set, 1)
        dve.wait_ge(toep_in, 48)
        link(nc.vector.tensor_scalar(band1[:], toep1, 1.0 / BIAS_SCALE, None, ALU.mult))
        nc.vector.memset(band1[HALF:P, :, P:B1W], 0.0).then_inc(band1_set, 1)
        dve.wait_ge(consts_in, 4 * 16)
        nc.vector.tensor_copy(counts[:], numbers[:, C_BASE:C_BASE + E])
        dve.wait_ge(dummy_out, 16)
        nc.vector.tensor_copy(padrows[:, :, ID_COL], numbers[:, C_PADID:C_PADID + TJ]).then_inc(pads_set, 1)
        layernorm_rows(Seq(0, 1))
        for h in range(UH):
            take_maxima(Seq(0, 0), h)
        split_m(Seq(0, 0), 0, PROLOGUE.index("m0") + 1)
        split_rest_of_m(Seq(0, 0), 0)
        for h in range(UH, LEAD):
            take_maxima(Seq(0, 0), h)
        dve.wait_ge(late_consts_in, 5 * 16)
        dve.wait_ge(misc_full, PROLOGUE.index("bias") + 1)
        nc.vector.tensor_tensor(bo[:], bo[:], misc[:, 0:D], ALU.add).then_inc(bo_set, 1)
        dve.wait_ge(bo_set, 1).then_inc(misc_free, 1)

        def slot(seq):
            prev, nxt, inp = seq.next(-1), seq.next(1), seq.next(2)
            first = seq.known and seq.b == 0
            last = seq.known and seq.b == LAST
            routed = not (seq.known and seq.b < 2)
            inputs = not (seq.known and seq.b + 2 > LAST)
            for h in range(H):
                lead = ahead(seq, h)
                if lead:
                    take_maxima(*lead, (0, 1))
                if h == 5:
                    split_rest_of_m(seq, 1)
                if h == 12 and not first:
                    ln2_collect(prev)
                if h == 13 and not last:
                    split_rest_of_m(nxt, 0)
                if routed:
                    if h == 1:
                        choose(seq.next(-2))
                    if h == 2:
                        weigh_choices(seq.next(-2))
                if inputs:
                    if h == 5:
                        ln1_measure(inp)
                if not first:
                    if h == 7:
                        invert_sums(prev)
                if lead:
                    take_maxima(*lead, (2,))
                if routed:
                    if h == 0:
                        take_top(seq.next(-2), misc_count(seq, "gate"))
                    if h == 2:
                        place_rows(seq.next(-2), misc_count(seq, "rank"))
                if h == 4:
                    split_m(seq, 1, misc_count(seq, "m_mid"))
                if not last:
                    if h == 12:
                        split_m(nxt, 0, misc_count(seq, "m_end"))
                if not first:
                    if h == 11:
                        add_residual(prev, misc_count(seq, "out"))
                if lead:
                    take_maxima(*lead, (3,))
                if h == 2 and routed:
                    find_places(seq.next(-2))
                if h == 11 and not first:
                    ln2_measure(prev, misc_count(seq, "out"))

        slots(slot, dve)
        end = Seq(LAST // 2, LAST % 2)
        take_top(end.next(-1), misc_count(end.next(1), "gate_a"))
        choose(end.next(-1))
        weigh_choices(end.next(-1))
        place_rows(end.next(-1), misc_count(end.next(1), "rank_a"))
        find_places(end.next(-1))
        invert_sums(end)
        normalise(dve, end)
        add_residual(end, out_count(end))
        ln2_measure(end, out_count(end))
        ln2_collect(end)
        ln2_apply(dve, end)
        take_top(end, misc_count(end.next(1), "gate_b"))
        choose(end)
        weigh_choices(end)
        place_rows(end, misc_count(end.next(1), "rank_b"))
        find_places(end)
        experts_vectors(dve)

    @block.gpsimd
    def _(pool):
        for n in range(2):
            ins = pool.memset(vp[n][:, :, :, HD:32], 1.0)
        ins.then_inc(ones_set, 1)

        def add_out_bias(seq):
            if seq.known and seq.b == 0:
                pool.wait_ge(bo_set, 1)
            pool.wait_ge(xres_in, 16 * (seq.b + 1))
            pool.tensor_tensor(xres[:], xres[:], bo[:].rearrange("p (o d) -> p o d", o=1).to_broadcast((P, T, D)),
                               ALU.add).then_inc(xres_set, 1)

        def double_rows(seq):
            pool.wait_ge(rows_set, seq.b + 1).then_inc(double_started, 1)
            pool.tensor_copy(rows[:, :, 1, 0:D], rows[:, :, 0, 0:D]).then_inc(rows_doubled, 1)

        def dispatch(seq):
            pool.wait_ge(rows_doubled, seq.b + 1)
            pool.wait_ge(slots_set, seq.b + 1).then_inc(dispatch_started, 1)
            for t in range(T):
                for c in range(TOPK):
                    k = TOPK * t + c
                    pool.indirect_dma_start(disp, bass.IndirectOffsetOnAxis(slot_i[:, k:k + 1], 0), rows[:, t, c, :], None).then_inc(dispatched, 16)

        def split_biases():
            nb1 = E * DFF // P
            pool.wait_ge(bcol_in, 32)
            steps = 0
            for src, lo, hi in ((b1col, 0, nb1), (b2col, nb1, (E * DFF + E * D) // P)):
                r = brest[:, 0:hi - lo]
                for n, (o, i0, i1) in enumerate(((bcols[:, 0, lo:hi], src[:], None), (r, src[:], bcols[:, 0, lo:hi]),
                                                 (bcols[:, 1, lo:hi], r, None), (bcols[:, 2, lo:hi], r, bcols[:, 1, lo:hi]))):
                    ins = pool.tensor_copy(o, i0) if i1 is None else pool.tensor_tensor(o, i0, i1, ALU.subtract)
                    ins.then_inc(bcol_chain, 1)
                    steps += 1
                    pool.wait_ge(bcol_chain, steps)
            pool.memset(ones3[:], 1.0).then_inc(bcol_set, 2)

        pool.wait_ge(toep_in, 48)
        for step, (dst, args) in enumerate((
                (band2[:], (toep2, 1.0 / BIAS_SCALE, None, ALU.mult)),
                (toep2[HALF:P], (toep2[HALF:P], 1.0 / BIAS_SCALE, None, ALU.mult)))):
            pool.tensor_scalar(dst, *args).then_inc(band2_chain, 1)
            pool.wait_ge(band2_chain, step + 1)
        pool.tensor_tensor(toep2[HALF:P], toep2[HALF:P], band2[HALF:P], ALU.subtract).then_inc(band2_chain, 1)
        pool.wait_ge(band2_chain, 3)
        pool.tensor_scalar(band2[HALF:P], toep2[HALF:P], LOW_SCALE, None, ALU.mult).then_inc(band_set, 1)
        pool.wait_ge(band_set, 1)
        k = PROLOGUE.index("q1") + 1
        split(pool, Seq(0, 1), 0, k, q32, qparts)
        split(pool, Seq(0, 1), 1, k + 1, k32, kparts)
        split_biases()
        pool.wait_ge(late_consts_in, 5 * 16)

        def slot(seq):
            prev, nxt, inp = seq.next(-1), seq.next(1), seq.next(2)
            first = seq.known and seq.b == 0
            last = seq.known and seq.b == LAST
            inputs = not (seq.known and seq.b + 2 > LAST)
            if not (seq.known and seq.b < 2):
                dispatch(seq.next(-2))
            if not first:
                add_out_bias(prev)
            if inputs:
                ln1_apply(pool, inp)
            if not first:
                normalise(pool, prev)
            if inputs:
                split(pool, inp, 0, misc_count(seq, "q"), q32, qparts)
                split(pool, inp, 1, misc_count(seq, "k"), k32, kparts)
            if not first:
                ln2_apply(pool, prev)
                double_rows(prev)

        slots(slot, pool)
        end = Seq(LAST // 2, LAST % 2)
        add_out_bias(end)
        dispatch(end.next(-1))
        double_rows(end)
        dispatch(end)
        experts_scatters(pool)


def buckets():
    d = np.arange(S)
    f = np.maximum(d, 1).astype(np.float32) / np.float32(16)
    large = 16 + (np.log(f) / np.float32(np.log(4.0)) * np.float32(16)).astype(np.int32)
    return np.where(d < 16, d, np.minimum(large, BUCKETS - 1))


def constants(nb):
    bf16 = mybir.dt.np(BF16)
    tokens = nb * S
    region = tokens + TILE
    ntiles = TOPK * tokens // TILE + E - 1
    ntiles += -ntiles % DEEP
    numbers = np.zeros((P, C_IOTA + ntiles), np.float32)
    lane = np.arange(P)
    numbers[:, C_IDS:C_IOTA8] = lane[:, None] + P * np.arange(T)
    numbers[:, C_IOTA8:C_SIGN] = np.arange(E)
    numbers[:, C_SIGN:C_BASE] = 1 - 2 * (np.arange(E) % 2)
    numbers[:, C_BASE:C_PADID] = region * np.arange(E)
    numbers[:, C_PADID:C_IOTA] = tokens + lane[:, None] + P * np.arange(TJ)
    numbers[:, C_IOTA:] = np.arange(ntiles)
    order = np.ones((P, 2, P), np.float32)
    order[:, 0, :] = lane[:, None] < lane[None, :]
    bucket = buckets()
    assert bucket[FAR] == BUCKETS - 1 and bucket[FAR - 1] < BUCKETS - 1
    onehot = np.zeros((BUCKETS, S), np.float32)
    for e in range(S):
        d = e - (HALF - 1) if e < FWD else FWD - 1 - (e - FWD)
        onehot[bucket[max(d, 0)], e] += 8.0
        onehot[BUCKETS - 1, e] -= 8.0
    stepmask = np.zeros((STEPS, S + NPARTS), np.float32)
    kstatic = np.zeros((ROWS2 - STACK, S), np.float32)
    for u in range(1, S // HALF):
        for s in range(NPARTS):
            r = NPARTS * (u - 1) + s
            stepmask[r, 0:HALF * u] = 1.0
            stepmask[r, S + s] = 1.0
            kstatic[r, HALF * u:HALF * u + HALF] = 1.0
    kstatic[STEPS:] = 1.0
    pick = np.zeros((3, P, P), np.float16)
    for g in range(2):
        for r in range(HALF):
            pick[g, HALF - 1 - r, HALF * g + r] = BIAS_SCALE
            pick[g, P - 1 - r, HALF * g + r] = BIAS_SCALE / LOW_SCALE
    pick[2] = np.eye(P)[::-1] * BIAS_SCALE
    return {"onehot": onehot, "stepmask": stepmask, "kstatic": kstatic.astype(bf16), "pick": pick,
            "ident": np.eye(P, dtype=np.float32), "numbers": numbers, "order": order.astype(bf16)}


NAMES = {"x": "L0_attn_hidden_states", "wq": "L0_attn_Wq", "bq": "L0_attn_bq", "wk": "L0_attn_Wk", "bk": "L0_attn_bk",
         "wv": "L0_attn_Wv", "bv": "L0_attn_bv", "wo": "L0_attn_Wo", "bo": "L0_attn_bo", "rel": "L0_attn_rel_bias",
         "w1": "L0_ffn_W1", "b1": "L0_ffn_b1", "w2": "L0_ffn_W2", "b2": "L0_ffn_b2", "wg": "L0_ffn_Wg", "bg": "L0_ffn_bg"}


def by_dim(a):
    return np.ascontiguousarray(a.reshape(a.shape[:-1] + (H, HD)).swapaxes(-1, -2).reshape(a.shape))


def build(nc, nb, io, out):
    with ExitStack() as ctx:
        layer(nc, ctx, nb, io, out)


def kernel(**inputs):
    import concourse.bacc as bacc
    from concourse.bass_utils import run_bass_kernel_spmd

    nc = bacc.Bacc("TRN2", target_bir_lowering=False, num_devices=1)
    arrays = {name: np.ascontiguousarray(inputs[full]) for name, full in NAMES.items()}
    for name in ("wq", "bq", "wk", "bk"):
        arrays[name] = by_dim(arrays[name])
    nb = arrays["x"].shape[0]
    arrays.update(constants(nb))
    io = {name: nc.dram_tensor(f"in_{name}", a.shape, mybir.dt.from_np(a.dtype), kind="ExternalInput").ap()
          for name, a in arrays.items()}
    out = nc.dram_tensor("out_rows", (nb * S + TILE, D), F32, kind="ExternalOutput").ap()
    build(nc, nb, io, out)
    r = run_bass_kernel_spmd(nc, [{f"in_{name}": a for name, a in arrays.items()}], core_ids=[0])
    return r.results[0]["out_rows"][0:nb * S].reshape(nb, S, D)
```
